# Optimizing a Trainium2 kernel written in Bass

```python
import numpy as np
import jax
import jax.numpy as jnp

def _softmax(x, axis=-1):
    return jax.nn.softmax(x, axis=axis)

def _gelu(x):
    return jax.nn.gelu(x, approximate=True)

def _silu(x):
    return jax.nn.silu(x)

def _sigmoid(x):
    return jax.nn.sigmoid(x)

def _layernorm(x, axis=-1, eps=1e-05):
    m = jnp.mean(x, axis=axis, keepdims=True)
    v = jnp.var(x, axis=axis, keepdims=True)
    return (x - m) / jnp.sqrt(v + eps)

def _scatter_add(tgt, idx, src, axis=0):
    return tgt.at[idx].add(src)

def _segment_sum(src, seg, n):
    return jax.ops.segment_sum(src, seg, n)
kernel_name = 'mk_gnn_preln_d4_gnn_r32_650ca6'

def setup_inputs(seed: int=0):
    np.random.seed(seed)
    _w = jnp.asarray

    def _rec_inputs():
        import jax
        import jax.numpy as jnp
        _gk = jax.random.key(seed)
        x = -0.0003713 + 1 * jax.random.normal(jax.random.fold_in(_gk, 1), (3125, 128), jnp.float32)
        src = jax.random.randint(jax.random.fold_in(_gk, 2), (100000,), 0, 3125, jnp.int32)
        dst = jnp.minimum((3125 * jax.random.uniform(jax.random.fold_in(_gk, 3), (100000,)) ** 2.0).astype(jnp.int32), 99999)
        _o = jnp.argsort(dst, stable=True)
        src = src[_o]
        dst = dst[_o]
        return (x, src, dst)
    x, src, dst = _rec_inputs()

    def _L0_gnn_setup():
        import jax, jax.numpy as jnp
        import numpy as np
        N_NODES = 3125
        IN_CH, HID_CH, OUT_CH = (128, 256, 128)
        N_EDGES = 50000
        key = jax.random.key(seed)
        k_x, k_e, k_w1, k_b1, k_w2, k_b2 = jax.random.split(key, 6)
        x = jax.random.normal(k_x, (N_NODES, IN_CH), dtype=jnp.float32)
        edge_index = jax.random.randint(k_e, (2, N_EDGES), 0, N_NODES, dtype=jnp.int64)
        lim1 = 1.0 / np.sqrt(IN_CH)
        lim2 = 1.0 / np.sqrt(HID_CH)
        W1 = jax.random.uniform(k_w1, (IN_CH, HID_CH), jnp.float32, -lim1, lim1)
        b1 = jax.random.uniform(k_b1, (HID_CH,), jnp.float32, -lim1, lim1)
        W2 = jax.random.uniform(k_w2, (HID_CH, OUT_CH), jnp.float32, -lim2, lim2)
        b2 = jax.random.uniform(k_b2, (OUT_CH,), jnp.float32, -lim2, lim2)
        eps = jnp.zeros((), jnp.float32)
        return {'x': x, 'edge_index': edge_index, 'W1': W1, 'b1': b1, 'W2': W2, 'b2': b2, 'eps': eps}
    _L0_gnn_all = _L0_gnn_setup()
    _L0_gnn_in = {k: v for k, v in _L0_gnn_all.items() if k in ('W1', 'b1', 'W2', 'b2', 'eps')}
    del _L0_gnn_all

    def _L1_gnn_setup():
        import jax, jax.numpy as jnp
        import numpy as np
        N_NODES = 3125

        def gcn_conv(x, W, b, src, dst, n):
            x = x @ W
            ar = jnp.arange(n, dtype=src.dtype)
            src = jnp.concatenate([src, ar])
            dst = jnp.concatenate([dst, ar])
            deg = jax.ops.segment_sum(jnp.ones_like(dst, dtype=x.dtype), dst, num_segments=n)
            dinv = jax.lax.rsqrt(deg)
            coef = dinv[src] * dinv[dst]
            msg = x[src] * coef[:, None]
            out = jax.ops.segment_sum(msg, dst, num_segments=n)
            return out + b
        key = jax.random.key(seed)
        k1, k2, k3, k4 = jax.random.split(key, 4)
        n, e, d_in, d_h, d_out = (N_NODES, 50000, 128, 128, 128)
        x = jax.random.normal(k1, (n, d_in), dtype=jnp.float32)
        edge_index = jax.random.randint(k2, (2, e), 0, n, dtype=jnp.int64)
        s1 = 1.0 / np.sqrt(d_in)
        s2 = 1.0 / np.sqrt(d_h)
        W1 = jax.random.uniform(k3, (d_in, d_h), jnp.float32, -s1, s1)
        W2 = jax.random.uniform(k4, (d_h, d_out), jnp.float32, -s2, s2)
        b1 = jnp.zeros((d_h,), jnp.float32)
        b2 = jnp.zeros((d_out,), jnp.float32)
        return {'x': x, 'edge_index': edge_index, 'W1': W1, 'b1': b1, 'W2': W2, 'b2': b2}
    _L1_gnn_all = _L1_gnn_setup()
    _L1_gnn_in = {k: v for k, v in _L1_gnn_all.items() if k in ('W1', 'b1', 'W2', 'b2')}
    del _L1_gnn_all

    def _L2_gnn_setup():
        import jax, jax.numpy as jnp
        import numpy as np
        N_NODES = 3125
        N_EDGES = 50000
        F_IN = 128
        HID = 128
        N_LAYERS = 4
        BN_EPS = 1e-05
        key = jax.random.key(seed)
        ks = jax.random.split(key, 8)
        x = jax.random.normal(ks[0], (N_NODES, F_IN), dtype=jnp.float32)
        edge_index = jax.random.randint(ks[1], (2, N_EDGES), 0, N_NODES, dtype=jnp.int32)
        s = 0.05
        W1 = jax.random.normal(ks[2], (N_LAYERS, F_IN, HID), dtype=jnp.float32) * s
        b1 = jnp.zeros((N_LAYERS, HID), dtype=jnp.float32)
        W2 = jax.random.normal(ks[3], (N_LAYERS, HID, HID), dtype=jnp.float32) * s
        b2 = jnp.zeros((N_LAYERS, HID), dtype=jnp.float32)
        gamma = jnp.ones((N_LAYERS, HID), dtype=jnp.float32)
        beta = jnp.zeros((N_LAYERS, HID), dtype=jnp.float32)
        return {'x': x, 'edge_index': edge_index, 'W1': W1, 'b1': b1, 'W2': W2, 'b2': b2, 'gamma': gamma, 'beta': beta}
    _L2_gnn_all = _L2_gnn_setup()
    _L2_gnn_in = {k: v for k, v in _L2_gnn_all.items() if k in ('W1', 'b1', 'W2', 'b2', 'gamma', 'beta')}
    del _L2_gnn_all

    def _L3_gnn_setup():
        import jax, jax.numpy as jnp
        import numpy as np
        N, E, IN_C, HID, OUT_C, HOPS = (50000, 50000, 128, 128, 128, 2)
        BN_EPS = 1e-05

        def _gcn_norm(edge_index, n, dtype):
            loop = jnp.arange(n, dtype=edge_index.dtype)
            row = jnp.concatenate([edge_index[0], loop])
            col = jnp.concatenate([edge_index[1], loop])
            w = jnp.ones(row.shape[0], dtype=dtype)
            deg = jax.ops.segment_sum(w, col, num_segments=n)
            dinv = jnp.where(deg > 0, deg ** (-0.5), 0.0).astype(dtype)
            val = dinv[row] * w * dinv[col]
            return (row, col, val)

        def _spmm(row, col, val, h, n):
            return jax.ops.segment_sum(val[:, None] * h[col], row, num_segments=n)

        def _mixhop(h, Ws, bs, row, col, val, n):
            xs = []
            for j in range(Ws.shape[0]):
                xj = h @ Ws[j] + bs[j]
                for _ in range(j):
                    xj = _spmm(row, col, val, xj, n)
                xs.append(xj)
            return jnp.concatenate(xs, axis=1)
        key = jax.random.key(seed)
        ks = jax.random.split(key, 8)
        x = jax.random.normal(ks[0], (N, IN_C), dtype=jnp.float32)
        edge_index = jax.random.randint(ks[1], (2, E), 0, N, dtype=jnp.int64)
        l1_w = jax.random.normal(ks[2], (HOPS + 1, IN_C, HID), dtype=jnp.float32) / np.sqrt(IN_C)
        l1_b = jnp.zeros((HOPS + 1, HID), dtype=jnp.float32)
        l2_in = HID * (HOPS + 1)
        l2_w = jax.random.normal(ks[3], (HOPS + 1, l2_in, OUT_C), dtype=jnp.float32) / np.sqrt(l2_in)
        l2_b = jnp.zeros((HOPS + 1, OUT_C), dtype=jnp.float32)
        fp_in = OUT_C * (HOPS + 1)
        fp_w = jax.random.normal(ks[4], (fp_in, OUT_C), dtype=jnp.float32) / np.sqrt(fp_in)
        fp_b = jnp.zeros((OUT_C,), dtype=jnp.float32)
        bn_gamma = jnp.ones((HID * (HOPS + 1),), dtype=jnp.float32)
        bn_beta = jnp.zeros((HID * (HOPS + 1),), dtype=jnp.float32)
        return {'x': x, 'edge_index': edge_index, 'l1_w': l1_w, 'l1_b': l1_b, 'bn_gamma': bn_gamma, 'bn_beta': bn_beta, 'l2_w': l2_w, 'l2_b': l2_b, 'fp_w': fp_w, 'fp_b': fp_b}
    _L3_gnn_all = _L3_gnn_setup()
    _L3_gnn_in = {k: v for k, v in _L3_gnn_all.items() if k in ('l1_w', 'l1_b', 'bn_gamma', 'bn_beta', 'l2_w', 'l2_b', 'fp_w', 'fp_b')}
    del _L3_gnn_all
    return {'x': x, 'src': src, 'dst': dst, 'L0_gnn_W1': _L0_gnn_in['W1'], 'L0_gnn_b1': _L0_gnn_in['b1'], 'L0_gnn_W2': _L0_gnn_in['W2'], 'L0_gnn_b2': _L0_gnn_in['b2'], 'L0_gnn_eps': _L0_gnn_in['eps'], 'L1_gnn_W1': _L1_gnn_in['W1'], 'L1_gnn_b1': _L1_gnn_in['b1'], 'L1_gnn_W2': _L1_gnn_in['W2'], 'L1_gnn_b2': _L1_gnn_in['b2'], 'L2_gnn_W1': _L2_gnn_in['W1'], 'L2_gnn_b1': _L2_gnn_in['b1'], 'L2_gnn_W2': _L2_gnn_in['W2'], 'L2_gnn_b2': _L2_gnn_in['b2'], 'L2_gnn_gamma': _L2_gnn_in['gamma'], 'L2_gnn_beta': _L2_gnn_in['beta'], 'L3_gnn_l1_w': _L3_gnn_in['l1_w'], 'L3_gnn_l1_b': _L3_gnn_in['l1_b'], 'L3_gnn_bn_gamma': _L3_gnn_in['bn_gamma'], 'L3_gnn_bn_beta': _L3_gnn_in['bn_beta'], 'L3_gnn_l2_w': _L3_gnn_in['l2_w'], 'L3_gnn_l2_b': _L3_gnn_in['l2_b'], 'L3_gnn_fp_w': _L3_gnn_in['fp_w'], 'L3_gnn_fp_b': _L3_gnn_in['fp_b']}

def reference(x, src, dst, L0_gnn_W1, L0_gnn_b1, L0_gnn_W2, L0_gnn_b2, L0_gnn_eps, L1_gnn_W1, L1_gnn_b1, L1_gnn_W2, L1_gnn_b2, L2_gnn_W1, L2_gnn_b1, L2_gnn_W2, L2_gnn_b2, L2_gnn_gamma, L2_gnn_beta, L3_gnn_l1_w, L3_gnn_l1_b, L3_gnn_bn_gamma, L3_gnn_bn_beta, L3_gnn_l2_w, L3_gnn_l2_b, L3_gnn_fp_w, L3_gnn_fp_b):
    import jax
    import jax.numpy as jnp

    def _L0_gnn_ref(x, edge_index, W1, b1, W2, b2, eps):
        import jax, jax.numpy as jnp
        import numpy as np
        N_NODES = 3125
        IN_CH, HID_CH, OUT_CH = (128, 256, 128)
        N_EDGES = 50000
        src, dst = (edge_index[0], edge_index[1])
        aggr = jax.ops.segment_sum(x[src], dst, num_segments=N_NODES)
        h = (1.0 + eps) * x + aggr
        h = jax.nn.relu(h @ W1 + b1)
        h = h @ W2 + b2
        h = jax.nn.relu(h)
        return jax.nn.log_softmax(h, axis=-1)

    def _L1_gnn_ref(x, edge_index, W1, b1, W2, b2):
        import jax, jax.numpy as jnp
        import numpy as np
        N_NODES = 3125

        def gcn_conv(x, W, b, src, dst, n):
            x = x @ W
            ar = jnp.arange(n, dtype=src.dtype)
            src = jnp.concatenate([src, ar])
            dst = jnp.concatenate([dst, ar])
            deg = jax.ops.segment_sum(jnp.ones_like(dst, dtype=x.dtype), dst, num_segments=n)
            dinv = jax.lax.rsqrt(deg)
            coef = dinv[src] * dinv[dst]
            msg = x[src] * coef[:, None]
            out = jax.ops.segment_sum(msg, dst, num_segments=n)
            return out + b
        n = x.shape[0]
        src, dst = (edge_index[0], edge_index[1])
        h = gcn_conv(x, W1, b1, src, dst, n)
        h = jax.nn.relu(h)
        out = gcn_conv(h, W2, b2, src, dst, n)
        return out

    def _L2_gnn_ref(x, edge_index, W1, b1, W2, b2, gamma, beta):
        import jax, jax.numpy as jnp
        import numpy as np
        N_NODES = 3125
        N_EDGES = 50000
        F_IN = 128
        HID = 128
        N_LAYERS = 4
        BN_EPS = 1e-05
        src, dst = (edge_index[0], edge_index[1])
        n = x.shape[0]
        h = x
        for i in range(N_LAYERS):
            agg = jax.ops.segment_sum(h[src], dst, num_segments=n)
            z = agg + h
            z = jax.nn.relu(z @ W1[i] + b1[i]) @ W2[i] + b2[i]
            mean = jnp.mean(z, axis=0)
            var = jnp.var(z, axis=0)
            z = (z - mean) * jax.lax.rsqrt(var + BN_EPS) * gamma[i] + beta[i]
            h = jax.nn.relu(z)
        return h

    def _L3_gnn_ref(x, edge_index, l1_w, l1_b, bn_gamma, bn_beta, l2_w, l2_b, fp_w, fp_b):
        import jax, jax.numpy as jnp
        import numpy as np
        N, E, IN_C, HID, OUT_C, HOPS = (50000, 50000, 128, 128, 128, 2)
        BN_EPS = 1e-05

        def _gcn_norm(edge_index, n, dtype):
            loop = jnp.arange(n, dtype=edge_index.dtype)
            row = jnp.concatenate([edge_index[0], loop])
            col = jnp.concatenate([edge_index[1], loop])
            w = jnp.ones(row.shape[0], dtype=dtype)
            deg = jax.ops.segment_sum(w, col, num_segments=n)
            dinv = jnp.where(deg > 0, deg ** (-0.5), 0.0).astype(dtype)
            val = dinv[row] * w * dinv[col]
            return (row, col, val)

        def _spmm(row, col, val, h, n):
            return jax.ops.segment_sum(val[:, None] * h[col], row, num_segments=n)

        def _mixhop(h, Ws, bs, row, col, val, n):
            xs = []
            for j in range(Ws.shape[0]):
                xj = h @ Ws[j] + bs[j]
                for _ in range(j):
                    xj = _spmm(row, col, val, xj, n)
                xs.append(xj)
            return jnp.concatenate(xs, axis=1)
        n = x.shape[0]
        row, col, val = _gcn_norm(edge_index, n, x.dtype)
        h = _mixhop(x, l1_w, l1_b, row, col, val, n)
        mean = jnp.mean(h, axis=0)
        var = jnp.var(h, axis=0)
        h = (h - mean) * jax.lax.rsqrt(var + BN_EPS) * bn_gamma + bn_beta
        h = jax.nn.relu(h)
        h = _mixhop(h, l2_w, l2_b, row, col, val, n)
        return h @ fp_w + fp_b
    edge_index = jnp.stack([src, dst])
    h = jnp.maximum(_layernorm(x, axis=-1), 0.0)
    x = x + _L0_gnn_ref(h, edge_index, L0_gnn_W1, L0_gnn_b1, L0_gnn_W2, L0_gnn_b2, L0_gnn_eps)
    h = jnp.maximum(_layernorm(x, axis=-1), 0.0)
    x = x + _L1_gnn_ref(h, edge_index, L1_gnn_W1, L1_gnn_b1, L1_gnn_W2, L1_gnn_b2)
    h = jnp.maximum(_layernorm(x, axis=-1), 0.0)
    x = x + _L2_gnn_ref(h, edge_index, L2_gnn_W1, L2_gnn_b1, L2_gnn_W2, L2_gnn_b2, L2_gnn_gamma, L2_gnn_beta)
    h = jnp.maximum(_layernorm(x, axis=-1), 0.0)
    x = x + _L3_gnn_ref(h, edge_index, L3_gnn_l1_w, L3_gnn_l1_b, L3_gnn_bn_gamma, L3_gnn_bn_beta, L3_gnn_l2_w, L3_gnn_l2_b, L3_gnn_fp_w, L3_gnn_fp_b)
    return x

_drawn_inputs = setup_inputs


def setup_inputs(seed=0):
    import zlib

    import numpy as np

    out = dict(_drawn_inputs(seed))
    spreads = {'L1_gnn_b1': (0.0, 0.8),
     'L1_gnn_b2': (0.0, 0.751),
     'L2_gnn_b1': (0.0, 2.0),
     'L2_gnn_b2': (0.0, 2.0),
     'L2_gnn_gamma': (1.0, 0.6),
     'L2_gnn_beta': (0.0, 0.346),
     'L3_gnn_l1_b': (0.0, 2.0),
     'L3_gnn_bn_gamma': (1.0, 0.6),
     'L3_gnn_bn_beta': (0.0, 0.8),
     'L3_gnn_l2_b': (0.0, 0.8),
     'L3_gnn_fp_b': (0.0, 0.8)}
    factors = {'L0_gnn_b1': 30.05, 'L0_gnn_b2': 8.0, 'L1_gnn_W1': 4.721, 'L1_gnn_W2': 3.309}
    for name, (base, spread) in spreads.items():
        noise = np.random.default_rng([zlib.crc32(name.encode()), seed]).standard_normal(out[name].shape)
        drawn = base * np.exp(spread * noise) if base else spread * noise
        out[name] = jnp.asarray(drawn.astype(out[name].dtype))
    for name, factor in factors.items():
        out[name] = (out[name] * factor).astype(out[name].dtype)
    return out
```

```python
from contextlib import ExitStack

import concourse.bass as bass
from concourse import mybir

F32 = mybir.dt.float32
BF16 = mybir.dt.bfloat16
F16 = mybir.dt.float16
I32 = mybir.dt.int32
U32 = mybir.dt.uint32
ALU = mybir.AluOpType
ACT = mybir.ActivationFunctionType
AX = mybir.AxisListType

P = 128
CH = 128
GC = 2
GE = GC * CH
WIN = 25
HG = 7
RING = 7
GW = 20
LN_EPS = 1e-5
BN_EPS = 1e-5
PAD_SRC = -10000000


class Line:

    def __init__(self, eng, sem):
        self.eng, self.sem, self.n, self.off = eng, sem, 0, 0

    def __call__(self, ins):
        ins.then_inc(self.sem, 1)
        self.n += 1

    def sync(self):
        self.eng.wait_ge(self.sem, self.off + self.n)

    def loop(self, times, per):
        start, off = self.n, self.off
        with self.eng.Fori(0, times) as i:
            self.off = off + i * per
            yield i
            assert self.n - start == per, (self.n - start, per)
        self.off, self.n = off, start + times * per


def divisor(n, most):
    return max(d for d in range(1, most + 1) if n % d == 0)


def build(nc, a, out):
    N, D = a["x"].shape
    E = a["src"].shape[0]
    assert D == P
    PN = divisor(N, P)
    NT = N // PN
    assert NT % 2 == 1 and NT % 5 == 0
    NB = NT // 5
    BT = 5
    HT = (NT - 1) // 2
    G = -(-E // GE)
    G = -(-G // (2 * HG)) * 2 * HG
    assert G > E // GE
    QG = divisor(G, P)
    KR = G // QG
    NCH = G * GC
    STEPS = G // (2 * HG)
    KW = WIN * NT
    KWP = KW + KW % 2
    HALF = (WIN - 1) // 2
    AW = N + WIN
    AW += AW % 2
    GWN = -(-N // GW)
    assert GWN * GW <= AW and NT * GW <= 512
    FULL = E // GE
    assert (2 * HG * GC) % RING == 0
    LAYERS = a["L2_gnn_W1"].shape[0]
    HW = 388
    X0 = 3 * P

    ctx = ExitStack()
    with ctx:
        def sb(name, shape, dt):
            return ctx.enter_context(nc.sbuf_tensor(name, shape, dt))

        def sem(name):
            return ctx.enter_context(nc.semaphore(name))

        def dram(name, shape, dt):
            return nc.dram_tensor(name, shape, dt).ap()

        RW = KR * GE
        OHW = -(-KWP // 64) * 64
        IOW = max(KWP, P)
        FTW = (STEPS + 1) * 16
        ADJ = sb("ADJ", [P, NT, AW], BF16)
        HPb = sb("HPb", [P, max(NT * HW, RING * (OHW + P) + NT * GW, 8 * RW, 48 * P)], BF16)[:, :]
        XRf = sb("XRf", [P, max(NT * P, 2 * RW + KWP // 2 + 4 + P // 2 + FTW)], F32)[:, :]
        Zf = sb("Zf", [P, max(NT * P, 3 * NCH, 21 * P)], F32)[:, :]
        HP = HPb[:, 0:NT * HW].rearrange("p (t f) -> p t f", t=NT)
        XR = XRf[:, 0:NT * P].rearrange("p (t f) -> p t f", t=NT)
        Zn = Zf[:, 0:NT * P].rearrange("p (t f) -> p t f", t=NT)
        WB = sb("WB", [P, max(4 * P + 6 * NT, 3 * P + 18 * NT)], F32)
        STATS = WB[:, 3 * P:3 * P + 18 * NT].rearrange("p (q t c) -> p q t c", q=3, c=6)
        LNS = WB[:, 4 * P:4 * P + 6 * NT].rearrange("p (t c) -> p t c", c=6)
        BB = sb("BB", [P, P], F32)
        IDF = sb("IDF", [P, P], F32)
        IDB = sb("IDB", [P, P], BF16)
        ST = sb("ST", [P, 2, P], F32)
        SF = sb("SF", [P, 2, P], F32)
        SG = sb("SG", [P, 2, P], F32)
        SMW = 11 * NT + 16
        SM = sb("SM", [P, SMW], F32)
        FL = sb("FL", [P, 4], I32)
        B_L0 = sb("B_L0", [P, 2], F32)
        B_L1 = sb("B_L1", [P, 1], F32)
        B_L2 = sb("B_L2", [P, 4, LAYERS], F32)
        B_L3 = sb("B_L3", [P, 4, 3], F32)
        Q_B1, Q_B2, Q_GA, Q_BE = range(4)
        R_B1, R_GA, R_BE, R_B2 = range(4)
        LOT = sb("LOT", [P, P], BF16)
        LOX = sb("LOX", [P, P], BF16)
        ROW = sb("ROW", [1, P], F32)
        PS = ctx.enter_context(nc.psum_tensor("PS", [P, 8, 512], F32))

        at = [0]

        def small(n):
            at[0] += n
            assert at[0] <= SMW
            return SM[:, at[0] - n:at[0]]

        DI = small(NT)
        DEG = small(NT)
        RD = small(NT)
        MV = small(2 * NT).rearrange("p (t c) -> p t c", c=2)
        SDV = small(NT)
        RS = small(NT)
        NBI = small(NT)
        MX = small(NT)
        SE = small(NT)
        TMP = small(NT)
        RC = small(1)
        EPSC = small(1)
        EPS0 = small(1)
        BNM = small(2)
        BNS = small(1)
        BNR = small(1)
        BNT = small(1)
        BNA = small(3)
        BNB = small(3)
        ONEC = small(1)
        WBASE = small(1)

        HPf = HPb.bitcast(F32)
        dst_i = XRf[:, 0:RW].bitcast(I32)
        src_i = XRf[:, RW:2 * RW].bitcast(I32)
        c0 = 2 * RW
        IOK = XRf[:, c0:c0 + KWP // 2].bitcast(F16)
        c0 += -(-(KWP // 2) // 4) * 4
        IOP = XRf[:, c0:c0 + P // 2].bitcast(F16)
        c0 += P // 2
        FT = XRf[:, c0:c0 + FTW].bitcast(I32)
        dst_f, src_f, til_f, key_f = (HPf[:, k * RW:(k + 1) * RW] for k in range(4))
        iota_i = HPf[:, 0:IOW].bitcast(I32)
        OHK = [HPb[:, k * OHW:k * OHW + KWP] for k in range(RING)]
        OHP = [HPb[:, RING * OHW + k * P:RING * OHW + (k + 1) * P] for k in range(RING)]
        LOB = HPb[:, RING * (OHW + P):RING * (OHW + P) + NT * GW].rearrange("p (t d) -> p t d", t=NT)
        KT, PT, KGT = (Zf[:, k * NCH:(k + 1) * NCH] for k in range(3))

        base_d = dram("base_d", [G + 1], I32)
        lo_d = dram("lo_d", [P, NT, AW], BF16)
        y_d = dram("y_d", [3, P, N], F32)
        q1_d = dram("q1_d", [NT, PN, P], F32)

        AG = [PS[:, 0, :], PS[:, 1, :]]
        TP, P1, P2, P3 = (PS[:, b, :] for b in (2, 3, 4, 5))
        RB = [PS[:, 4:6, :].rearrange("p b c -> p (b c)"), PS[:, 6:8, :].rearrange("p b c -> p (b c)")]
        WPS = [PS[:, 0:2, :], PS[:, 2:4, :]]
        CPS = [PS[:, 4, :], PS[:, 5, :]]

        s_in, s_w, s_x, s_base, s_const, s_pad, s_rows = (sem("s_" + n) for n in
                                                          ("in", "w", "x", "base", "const", "pad", "rows"))
        s_dve0, s_dve1, s_act1, s_pool0 = (sem(n) for n in ("s_dve0", "s_dve1", "s_act1", "s_pool0"))
        s_rowt, s_rowc = sem("s_rowt"), sem("s_rowc")
        s_frow, s_fsum, s_frow2, s_fsum2 = (sem("s_f%d" % k) for k in range(4))
        s_flag, s_flag2 = sem("s_flag"), sem("s_flag2")
        s_oh = sem("s_oh")
        s_ohx = sem("s_ohx")
        s_mv = sem("s_mv")
        s_add = sem("s_add")
        s_bline = sem("s_bline")
        s_goh, s_gox, s_gline, s_glo = (sem("s_g" + n) for n in ("oh", "ox", "line", "lo"))
        s_lol, s_lox, s_lom, s_lod, s_loc = (sem("s_lo" + n) for n in "lxmdc")
        s_adj = sem("s_adj")
        PHASES = {"L0": "tr cf d1 rg d2 z", "L1a": "tr cf d1 rg d2 z r0", "L1b": "", "L2": "tr cf d1 rg d2",
                  "L3a": "tr cf d1 z r0", "L3b": "tr cf d1 z", "L3c": "z", "L3d": "z"}
        ev = {p: {n: sem(f"{p}_{n}") for n in ("agg red hi r1 mid hp " + more).split()}
              for p, more in PHASES.items()}
        s_ln = [[sem(f"ln{k}_{m}") for m in range(4)] for k in range(4)]
        s_soft = [sem(f"soft_{m}") for m in range(2)]
        s_bn = {n: sem("bn_" + n) for n in ("var", "sd", "ab", "rel", "tr", "w")}
        s_wt, s_ones = sem("s_wt"), sem("s_ones")
        s_at = {n: sem("at_" + n) for n in ("tr", "act", "dve")}
        s_y, s_yl0, s_vw, s_vt, s_vc, s_vm, s_vv, s_vr, s_vq, s_vd = (sem("s_v%d" % k) for k in range(10))
        s_yl = [s_yl0, sem("s_yl1")]
        s_null = sem("s_null")
        s_q1, s_q1l, s_out = sem("s_q1"), sem("s_q1l"), sem("s_out")
        s_rt = sem("s_rt")
        credited = [s for p in PHASES for s in ev[p].values()] + [s_y, s_q1, s_q1l, s_at["act"], s_at["dve"],
                                                                  s_vr, s_vq, s_vd, s_out, s_lom, s_bn["w"]]

        def col(v):
            return v.rearrange("(p o) -> p o", o=1)

        def bcast(v, n=P):
            return v.rearrange("(o n) -> o n", o=1).broadcast_to([n, v.shape[0]])

        def program(role, e):
            pe, act, dve, pool, sp = (role == r for r in ("pe", "act", "dve", "pool", "sp"))

            n_in = 2 * (sum(1 for k in range(KR) if FULL - k * QG > 0) + (1 if E % GE else 0))
            if sp:
                e.wait_ge(s_pad, 2)
                for dram_t, tile in ((a["dst"], dst_i), (a["src"], src_i)):
                    t3 = tile.rearrange("p (k e) -> p k e", k=KR)
                    for k in range(KR):
                        n = min(QG, FULL - k * QG)
                        if n > 0:
                            e.dma_start(t3[0:n, k, :], dram_t[k * QG * GE:(k * QG + n) * GE]
                                        .rearrange("(q e) -> q e", e=GE)).then_inc(s_in, 16)
                    r = E - FULL * GE
                    if r:
                        q, k = FULL % QG, FULL // QG
                        e.dma_start(t3[q:q + 1, k, 0:r], dram_t[FULL * GE:E].rearrange("(o e) -> o e", o=1))\
                         .then_inc(s_in, 16)
            if act:
                e.dma_start(WB[:, 0:2 * P], a["L0_gnn_W1"]).then_inc(s_w, 16)
                e.dma_start(WB[:, 2 * P:4 * P].rearrange("p (k n) -> p k n", k=2),
                            a["L0_gnn_W2"].rearrange("(k p) n -> p k n", p=P)).then_inc(s_w, 16)
                e.dma_start(BB[:, :], bcast(a["L0_gnn_b2"])).then_inc(s_w, 16)
                e.dma_start(EPS0, bcast(a["L0_gnn_eps"])).then_inc(s_w, 16)
                e.dma_start(B_L0[:, :], a["L0_gnn_b1"].rearrange("(k p) -> p k", p=P),
                            allow_slow_non_contiguous=True).then_inc(s_w, 16)
                e.dma_start(B_L1[:, :], col(a["L1_gnn_b1"])).then_inc(s_w, 16)
                for q, n in enumerate(("b1", "b2", "gamma", "beta")):
                    e.dma_start(B_L2[:, q, :], a["L2_gnn_" + n].rearrange("l p -> p l"),
                                allow_slow_non_contiguous=True).then_inc(s_w, 16)
                for q, n in enumerate(("l1_b", "bn_gamma", "bn_beta", "l2_b")):
                    v = a["L3_gnn_" + n]
                    v = v.rearrange("q p -> p q") if len(v.shape) == 2 else v.rearrange("(q p) -> p q", p=P)
                    e.dma_start(B_L3[:, q, :], v, allow_slow_non_contiguous=True).then_inc(s_w, 16)
            if pool:
                for s in credited:
                    e.sem_inc(s, 1)
                line = Line(e, s_pool0)
                line(e.memset(IDF[:, :], 0.0))
                line(e.iota(iota_i, [[1, IOW]], base=0, channel_multiplier=0))
                line(e.memset(ADJ[:, :, 0:1], 0.0))
                line(e.memset(ADJ[:, :, AW - WIN - 8:AW], 0.0))
                line.sync()
                line(e.affine_select(out=IDF[:, :], in_=IDF[:, :], compare_op=ALU.not_equal, fill=1.0,
                                     base=0, pattern=[[-1, P]], channel_multiplier=1))
                line(e.tensor_copy(IOK, iota_i[:, 0:KWP]))
                line(e.tensor_copy(IOP, iota_i[:, 0:P]))
                line.sync()
                line(e.tensor_copy(IDB[:, :], IDF[:, :]))
                line.sync()
                e.sem_inc(s_const, 1)
            if dve:
                line = Line(e, s_dve0)
                e.memset(dst_i, N).then_inc(s_pad, 1)
                e.memset(src_i, PAD_SRC).then_inc(s_pad, 1)
                e.memset(FL[:, 3:4], N).then_inc(s_pad, 1)
                line(e.memset(ONEC, 1.0))
                line(e.memset(EPSC, LN_EPS))
                e.wait_ge(s_const, 1)
                e.wait_ge(s_in, 16 * n_in)
                line(e.tensor_copy(src_f, src_i))
                line(e.tensor_copy(dst_f, dst_i))
                line.sync()
                line(e.tensor_scalar(key_f.bitcast(I32), src_f, -(PN - 1) / 2.0, 1.0 / PN, ALU.add, ALU.mult))
                line.sync()
                line(e.tensor_copy(til_f, key_f.bitcast(I32)))
                line.sync()
                line(e.scalar_tensor_tensor(out=src_f, in0=til_f, scalar=-float(PN), in1=src_f,
                                            op0=ALU.mult, op1=ALU.add))
                line.sync()
                for cmp, edge, way in ((ALU.is_lt, 0.0, -1.0), (ALU.is_ge, float(PN), 1.0)):
                    line(e.tensor_scalar(key_f, src_f, edge, way, cmp, ALU.mult))
                    line.sync()
                    line(e.tensor_tensor(til_f, til_f, key_f, ALU.add))
                    line(e.scalar_tensor_tensor(out=src_f, in0=key_f, scalar=-float(PN), in1=src_f,
                                                op0=ALU.mult, op1=ALU.add))
                    line.sync()
                line(e.scalar_tensor_tensor(out=key_f, in0=dst_f, scalar=float(NT), in1=til_f,
                                            op0=ALU.mult, op1=ALU.add))
                d3 = dst_f.rearrange("p (k e) -> p k e", k=KR)
                t3 = til_f.rearrange("p (k e) -> p k e", k=KR)
                m3 = key_f.rearrange("p (k e) -> p k e", k=KR)
                line(e.tensor_scalar(ST[:, 0, 0:KR], d3[:, :, 0], -float(NT), None, ALU.mult))
                line.sync()
                for k in range(KR):
                    line(e.tensor_scalar(t3[:, k, :], m3[:, k, :], ST[:, 0, k:k + 1], None, ALU.add))
                line.sync()
                e.sem_inc(s_rows, 1)
            if sp:
                e.wait_ge(s_in, 16 * n_in)
                e.wait_ge(s_pad, 3)
                e.dma_start(base_d[0:G].rearrange("(k q) -> q k", k=KR),
                            dst_i[0:QG, :].rearrange("p (k e) -> p k e", k=KR)[:, :, 0],
                            allow_slow_non_contiguous=True).then_inc(s_base, 16)
                e.dma_start(base_d[G:G + 1].rearrange("(o n) -> o n", o=1), FL[0:1, 3:4]).then_inc(s_base, 16)
                e.wait_ge(s_base, 32)
                e.dma_start(ST[0:QG, 1, 0:KR].bitcast(I32), base_d[1:G + 1].rearrange("(k q) -> q k", k=KR),
                            allow_slow_non_contiguous=True).then_inc(s_base, 16)
                e.dma_start(FT[0:1, 8:8 + 16 * STEPS].rearrange("o (s g) -> o s g", g=8)[:, :, 0:HG],
                            base_d[0:G].rearrange("(o s g) -> o s g", o=1, g=HG)).then_inc(s_base, 16)
            if dve:
                dense = float(min(256, N // 2))
                d = d3[0:QG]
                flags = SG[0:QG, 0, 0:6 * KR].rearrange("p (k c) -> p k c", c=6)
                nxt = SF[0:QG, 0, 0:KR]
                e.wait_ge(s_base, 64)
                line(e.tensor_copy(nxt, ST[0:QG, 1, 0:KR].bitcast(I32)))
                line(e.memset(FT[0:1, :].rearrange("o (s g) -> o s g", g=8)[:, :, HG:8], 0))
                line(e.memset(FT[0:1, 0:HG], 0))
                line(e.memset(FT[0:1, 8 + 16 * STEPS:8 + 16 * STEPS + HG], 0))
                line(e.memset(SG[0:QG, 0, :], 0.0))
                line(e.memset(SG[0:QG, 1, :], 0.0))
                cmp3 = src_i[0:QG, :].bitcast(F32).rearrange("p (k e) -> p k e", k=KR)
                line(e.tensor_tensor(cmp3[:, :, 0:GE - 1], d[:, :, 0:GE - 1], d[:, :, 1:GE], ALU.is_gt))
                line.sync()
                first, mid = d[:, :, 0], d[:, :, CH]
                for k in range(KR):
                    line(e.tensor_reduce(flags[:, k, 0:1], cmp3[:, k, 0:GE - 1], AX.X, ALU.add))
                line(e.tensor_tensor(flags[:, :, 1], d[:, :, GE - 1], nxt, ALU.is_gt))
                w = [SG[0:QG, 1, c * KR:(c + 1) * KR] for c in range(3)]
                line(e.tensor_tensor(w[0], nxt, first, ALU.subtract))
                line(e.tensor_tensor(w[1], first, mid, ALU.is_equal))
                line(e.tensor_tensor(w[2], mid, nxt, ALU.is_equal))
                line.sync()
                line(e.tensor_scalar(flags[:, :, 2], w[0], float(WIN - 1), None, ALU.is_gt))
                for c, v in ((1, first), (2, mid)):
                    line(e.scalar_tensor_tensor(out=w[c], in0=v, scalar=dense, in1=w[c],
                                                op0=ALU.is_ge, op1=ALU.mult))
                    line.sync()
                    line(e.scalar_tensor_tensor(out=flags[:, :, 2 + c], in0=v, scalar=float(N), in1=w[c],
                                                op0=ALU.is_lt, op1=ALU.mult))
                line(e.tensor_scalar(flags[0:1, 0, 5:6], first[0:1, 0:1], 0.0, None, ALU.is_gt))
                line.sync()
                line(e.tensor_reduce(SF[0:QG, 1, 0:1], SG[0:QG, 0, 0:6 * KR], AX.X, ALU.add))
                line.sync()
                e.sem_inc(s_frow, 1)
                e.wait_ge(s_fsum, 1)
                line(e.tensor_scalar(FL[0:1, 0:1], P3[0:1, 0:1], 0.0, None, ALU.is_gt))
                line.sync()
                e.sem_inc(s_flag, 1)

            tables = ((KT, til_f, 2), (PT, src_f, 3), (KGT, key_f, 4))
            if pe:
                e.wait_ge(s_const, 1)
                e.wait_ge(s_rows, 1)
                for n, (_, src, bank) in enumerate(tables):
                    s3 = src.rearrange("p (k h e) -> p k h e", k=KR, h=GC)
                    for h in range(GC):
                        if h:
                            e.wait_ge(s_rowc, 2 * n + 1)
                        for k in range(KR):
                            mm = e.transpose(PS[:, bank, k * QG:(k + 1) * QG], s3[0:QG, k, h, :], IDF[0:QG, 0:QG])
                        mm.then_inc(s_rowt, 1)
                e.wait_ge(s_frow, 1)
                e.matmul(P3[0:1, 0:1], SF[0:QG, 1, 0:1], ONEC[0:QG, :], start=True, stop=True)\
                 .then_inc(s_fsum, 1)
            if act:
                for n, (tab, _, bank) in enumerate(tables):
                    for h in range(GC):
                        e.wait_ge(s_rowt, 2 * n + h + 1)
                        e.copy(tab.rearrange("p (g h) -> p g h", h=GC)[:, :, h], PS[:, bank, 0:G])\
                         .then_inc(s_rowc, 1)

            e.wait_ge(s_flag, 1)
            bad = e.value_load(FL[0:1, 0:1], min_val=0, max_val=1)
            with e.If(bad == 0):
                quick_build(role, e)
            with e.Else():
                if dve:
                    e.memset(FL[0:1, 1:2], 1).then_inc(s_flag2, 1)
            e.wait_ge(s_flag2, 1)
            bad2 = e.value_load(FL[0:1, 1:2], min_val=0, max_val=1)
            with e.If(bad2 == 0):
                layers(role, e, False)
            with e.Else():
                general_build(role, e)
                layers(role, e, True)

        def quick_build(role, e):
            PER = 2 * HG * GC
            if role == "dve":
                line = Line(e, s_bline)
                regs = [e.alloc_register(f"vb{k}") for k in range(16)]

                def one_hots(i, h):
                    for m in range(h * HG * GC, (h + 1) * HG * GC):
                        n, k = i * PER + m, m % RING
                        e.wait_ge(s_ohx, n + 1)
                        e.tensor_scalar(OHK[k], IOK, KT[:, bass.ds(n, 1)], None, ALU.is_equal)\
                         .then_inc(s_oh, 1)
                        e.tensor_scalar(OHP[k], IOP, PT[:, bass.ds(n, 1)], None, ALU.is_equal)\
                         .then_inc(s_oh, 1)

                def first_columns(vals, n0, h):
                    e.wait_ge(s_ohx, (n0 + HG) * GC + RING)
                    for g in range(HG):
                        n = n0 + g
                        e.wait_ge(s_mv, n + 2)
                        e.wait_ge(s_add, n + 2 * HG)
                        to = ADJ[0:PN, :, bass.ds(vals[g], 1)].rearrange("p t o -> p (t o)")
                        e.tensor_tensor(to, to, CPS[h][0:PN, g * NT:(g + 1) * NT], ALU.add).then_inc(s_add, 1)

                def load_bases(i):
                    e.load(regs, FT[0:1, bass.ds(i * 16, 16)])
                    vals = [e.snap(r, min_val=0, max_val=N) for r in regs]
                    return vals[0:HG], vals[8:8 + HG]

                e.wait_ge(s_rowc, 6)
                e.sem_inc(s_ohx, RING)
                e.sem_inc(s_add, 2 * HG)
                one_hots(0, 0)
                one_hots(0, 1)
                first_columns(load_bases(0)[1], 0, 0)
                with e.Fori(1, STEPS) as i:
                    before, now = load_bases(i)
                    one_hots(i, 0)
                    first_columns(before, i * 2 * HG - HG, 1)
                    one_hots(i, 1)
                    first_columns(now, i * 2 * HG, 0)
                first_columns(load_bases(STEPS)[0], G - HG, 1)
                e.wait_ge(s_add, G + 2 * HG)
                e.wait_ge(s_mv, G + 2)
                line(e.tensor_reduce(TMP[0:PN, 0:1], ADJ[0:PN, :, 0:min(256, N)], AX.XY, ALU.max))
                line.sync()
                line(e.tensor_scalar(TMP[0:PN, 1:2], TMP[0:PN, 0:1], 256.0, None, ALU.is_ge))
                line.sync()
                e.sem_inc(s_frow2, 1)
                e.wait_ge(s_fsum2, 1)
                line(e.tensor_scalar(FL[0:1, 1:2], P3[0:1, 0:1], 0.0, None, ALU.is_gt))
                line.sync()
                e.sem_inc(s_flag2, 1)
            if role == "pe":
                with e.Fori(0, STEPS) as i:
                    for h in range(2):
                        e.wait_ge(s_add, (i * 2 + h + 1) * HG)
                        for m in range(h * HG, (h + 1) * HG):
                            e.wait_ge(s_mv, i * 2 * HG + m + 1)
                            for c in range(GC):
                                k = (m * GC + c) % RING
                                e.wait_ge(s_oh, (i * PER + m * GC + c + 1) * 2)
                                first, last = c == 0, c == GC - 1
                                g = m - h * HG
                                e.matmul(CPS[h][:, g * NT:(g + 1) * NT], OHP[k], OHK[k][:, 0:NT],
                                         start=first, stop=last)
                                for b in range(2):
                                    lo = NT + b * HALF * NT
                                    mm = e.matmul(WPS[m % 2][:, b, 0:HALF * NT], OHP[k], OHK[k][:, lo:lo + HALF * NT],
                                                  start=first, stop=last)
                                mm.then_inc(s_ohx, 1)
                e.wait_ge(s_frow2, 1)
                e.matmul(P3[0:1, 0:1], TMP[0:PN, 1:2], ONEC[0:PN, :], start=True, stop=True)\
                 .then_inc(s_fsum2, 1)
            if role == "act":
                regs = [e.alloc_register(f"ab{k}") for k in range(16)]
                e.wait_ge(s_base, 64)
                e.wait_ge(s_const, 1)
                e.sem_inc(s_mv, 2)
                with e.Fori(0, STEPS) as i:
                    e.load(regs, FT[0:1, bass.ds(i * 16 + 8, 16)])
                    vals = [e.snap(r, min_val=0, max_val=N) for r in regs]
                    for m in range(2 * HG):
                        n = i * 2 * HG + m
                        e.wait_ge(s_ohx, (n + 1) * GC + RING)
                        e.wait_ge(s_mv, n + 2)
                        to = ADJ[0:PN, :, bass.ds(vals[m // HG * 8 + m % HG] + 1, 2 * HALF)]
                        e.copy(to.rearrange("p t (b d) -> p b d t", b=2),
                               WPS[m % 2][0:PN, :, 0:HALF * NT].rearrange("p b (d t) -> p b d t", t=NT))\
                         .then_inc(s_mv, 1)

        def general_build(role, e):
            KV = GW * NT
            ACC = PS[:, 0, 0:KV]
            if role == "dve":
                e.wait_ge(s_rowc, 6)
                line = Line(e, s_gline)
                line(e.memset(WBASE, -float(KV)))
                line(e.memset(ADJ[:, :, :], 0.0))
                e.sem_inc(s_gox, 2)
                e.sem_inc(s_goh, 2)

                def one_hots(w, c, k):
                    e.wait_ge(s_gox, w * NCH + c + 1)
                    e.tensor_scalar(OHK[k][:, 0:KV], IOK[:, 0:KV], WBASE, KGT[:, bass.ds(c, 1)],
                                    ALU.add, ALU.is_equal).then_inc(s_goh, 1)
                    e.tensor_scalar(OHP[k], IOP, PT[:, bass.ds(c, 1)], None, ALU.is_equal).then_inc(s_goh, 1)

                for w in line.loop(GWN, 3):
                    line.sync()
                    e.wait_ge(s_goh, w * 2 * NCH + 2)
                    line(e.tensor_scalar(WBASE, WBASE, float(KV), None, ALU.add))
                    line.sync()
                    e.sem_inc(s_null, 1)
                    with e.Fori(0, NCH // 2) as c:
                        for k in range(2):
                            one_hots(w, c * 2 + k, k)
                    e.wait_ge(s_gox, w * NCH + NCH + 2)
                    e.wait_ge(s_glo, w * 16 + 16)
                    acc = ACC[0:PN].rearrange("p (d t) -> p t d", t=NT)
                    hi = ADJ[0:PN, :, bass.ds(w * GW, GW)]
                    line(e.tensor_copy(hi, acc))
                    line.sync()
                    line(e.tensor_tensor(LOB[0:PN], acc, hi, ALU.subtract))
                line.sync()
            if role == "pe":
                def product(w, c, k, first, last):
                    e.wait_ge(s_goh, (w * NCH + c + 1) * 2 + 2)
                    e.matmul(ACC, OHP[k], OHK[k][:, 0:KV], start=first, stop=last,
                             skip_group_check=True).then_inc(s_gox, 1)

                with e.Fori(0, GWN) as w:
                    e.wait_ge(s_gline, w * 3 + 2)
                    product(w, 0, 0, True, False)
                    with e.Fori(0, NCH // 2 - 1) as c:
                        for k in range(2):
                            product(w, c * 2 + 1 + k, 1 - k, False, False)
                    product(w, NCH - 1, 1, False, True)
            if role == "sp":
                e.sem_inc(s_glo, 16)
                with e.Fori(0, GWN) as w:
                    e.wait_ge(s_gline, w * 3 + 5)
                    e.dma_start(lo_d[0:PN, :, bass.ds(w * GW, GW)], LOB[0:PN]).then_inc(s_glo, 16)
                e.wait_ge(s_glo, 16 * (GWN + 1))

        def remainders(e):
            def bring(tiles0, count, turned):
                with e.Fori(0, count) as l:
                    with e.Fori(0, NT) as j:
                        with e.Fori(0, NT) as t:
                            e.wait_ge(s_lom, (tiles0 + l * NT + j) * NT + t + 1)
                            src = lo_d[0:PN, bass.ds(j, 1), bass.ds(t * PN, P)] if turned else \
                                lo_d[0:PN, bass.ds(t, 1), bass.ds(j * PN, P)]
                            e.dma_start(LOT[0:PN, :], src.rearrange("p o d -> p (o d)")).then_inc(s_lol, 16)

            bring(0, 3 + LAYERS, False)
            e.wait_ge(s_lom, (3 + LAYERS) * NT * NT + 1)
            with e.Fori(0, NT) as t:
                with e.Fori(0, NT) as b:
                    m = t * NT + b
                    blk = lo_d[0:PN, bass.ds(t, 1), bass.ds(b * PN, PN)].rearrange("p o d -> p (o d)")
                    e.dma_start(LOX[0:PN, 0:PN], blk).then_inc(s_lod, 16)
                    e.wait_ge(s_loc, m + 1)
                    e.sem_inc(s_null, 1)
                    e.dma_start(blk, LOT[0:PN, 0:PN]).then_inc(s_lod, 16)
                    e.wait_ge(s_lod, (m + 1) * 32)
            bring((3 + LAYERS) * NT, 4, True)

        def layers(role, e, general):
            pe, act, dve, pool, sp = (role == r for r in ("pe", "act", "dve", "pool", "sp"))
            if pool:
                if general:
                    remainders(e)
                return
            line = Line(e, s_dve1 if dve else s_act1)
            done = lambda s, n: e.wait_ge(s, n + 1)
            settle = lambda: e.sem_inc(s_null, 1)
            lo_at = [0]

            if dve:
                e.wait_ge(s_const, 1)
                with e.Fori(0, NT) as t:
                    blk = ADJ[0:PN, bass.ds(t, 1), bass.ds(t * PN, PN)].rearrange("p o d -> p (o d)")
                    e.tensor_tensor(blk, blk, IDB[0:PN, 0:PN], ALU.add).then_inc(s_adj, 1)
            if sp:
                e.dma_start(XR[0:PN], a["x"].rearrange("(t p) f -> p t f", p=PN)).then_inc(s_x, 16)

            def layer_norm(k, first_wait):
                stats, sd, rs, z = s_ln[k]
                if dve:
                    first_wait()
                    for j in line.loop(NT, 1):
                        line(e.bn_stats(LNS[0:PN, bass.ds(j, 1), :].rearrange("p o c -> p (o c)"), tile_of(XR, j)))
                    line.sync()
                    me, ve, mo, vo = (LNS[0:PN, :, c] for c in (1, 2, 4, 5))
                    mean, var = MV[0:PN, :, 0], MV[0:PN, :, 1]
                    line(e.tensor_tensor(mean, me, mo, ALU.add))
                    line(e.tensor_tensor(TMP[0:PN], me, mo, ALU.subtract))
                    line(e.tensor_tensor(var, ve, vo, ALU.add))
                    line.sync()
                    line(e.tensor_scalar(mean, mean, 0.5, None, ALU.mult))
                    line(e.tensor_tensor(TMP[0:PN], TMP[0:PN], TMP[0:PN], ALU.mult))
                    line(e.tensor_scalar(var, var, 1.0 / P, None, ALU.mult))
                    line.sync()
                    line(e.scalar_tensor_tensor(out=var, in0=TMP[0:PN], scalar=0.25, in1=var, op0=ALU.mult,
                                                op1=ALU.add))
                    line.sync()
                    e.sem_inc(stats, 1)
                    e.wait_ge(sd, 1)
                    line(e.reciprocal(RS[0:PN], SDV[0:PN]))
                    line.sync()
                    line(e.scalar_tensor_tensor(out=NBI[0:PN], in0=MV[0:PN, :, 0], scalar=-1.0, in1=RS[0:PN],
                                                op0=ALU.mult, op1=ALU.mult))
                    line.sync()
                    e.sem_inc(rs, 1)
                if act:
                    e.wait_ge(stats, 1)
                    e.activation(SDV[0:PN], MV[0:PN, :, 1], ACT.Sqrt, bias=EPSC[0:PN]).then_inc(sd, 1)
                    e.wait_ge(rs, 1)
                    with e.Fori(0, NT) as j:
                        e.activation(Zf[0:PN, bass.ds(j * P, P)],
                                     XR[0:PN, bass.ds(j, 1), :].rearrange("p o f -> p (o f)"), ACT.Relu,
                                     bias=NBI[0:PN, bass.ds(j, 1)], scale=RS[0:PN, bass.ds(j, 1)]).then_inc(z, 1)

            def blocks(b):
                return (Zn[0:PN, b * BT:(b + 1) * BT, :], HP[0:PN, b * BT:(b + 1) * BT, 0:P],
                        HP[0:PN, b * BT:(b + 1) * BT, P:2 * P], HP[0:PN, b * BT:(b + 1) * BT, 2 * P:3 * P],
                        RB[b % 2][0:PN, 0:BT * P].rearrange("p (t f) -> p t f", f=P))

            def act_parts(E_, base, ready, before=lambda b: None):
                def hi(b):
                    ready(b)
                    z, h, m, lo, rb = blocks(b)
                    e.copy(h, rb if E_ is not None and ready.from_psum else z).then_inc(E_["hi"], 1)

                def mid(b):
                    done(E_["r1"], base + b + 1)
                    z, h, m, lo, rb = blocks(b)
                    e.copy(m, rb).then_inc(E_["mid"], 1)

                before(0)
                hi(0)
                for b in range(1, NB):
                    before(b)
                    hi(b)
                    mid(b - 1)
                mid(NB - 1)

            def dve_parts(E_, base, from_psum):
                def r1(b):
                    done(E_["hi"], base + b + 1)
                    if b >= 2 and not from_psum:
                        done(E_["hp"], base + b - 1)
                    z, h, m, lo, rb = blocks(b)
                    e.tensor_tensor(rb, rb if from_psum else z, h, ALU.subtract).then_inc(E_["r1"], 1)

                def low(b):
                    done(E_["mid"], base + b + 1)
                    z, h, m, lo, rb = blocks(b)
                    e.tensor_tensor(lo, rb, m, ALU.subtract).then_inc(E_["hp"], 1)
                return r1, low

            def split(ph, scaled, wait_z):
                E_ = ev[ph]
                if act:
                    if not scaled:
                        wait_z()

                    def ready(b):
                        if scaled:
                            done(E_["r0"], b + 1)
                    ready.from_psum = scaled
                    act_parts(E_, 0, ready)
                if dve:
                    wait_z()
                    r1, low = dve_parts(E_, 0, scaled)

                    def r0(b):
                        z, h, m, lo, rb = blocks(b)
                        if scaled:
                            if b >= 2:
                                done(E_["hp"], b - 1)
                            e.tensor_tensor(rb, z, DI[0:PN, b * BT:(b + 1) * BT].rearrange("p (t o) -> p t o", o=1)
                                            .broadcast_to([PN, BT, P]), ALU.mult).then_inc(E_["r0"], 1)
                    r0(0)
                    r1(0)
                    for b in range(1, NB):
                        r0(b)
                        r1(b)
                        low(b - 1)
                    low(NB - 1)
                    done(E_["hp"], NB)

            def extra_columns(v):
                w = TMP[0:PN]
                src = v
                for q in range(3):
                    hc = HP[0:PN, :, X0 + q]
                    line(e.tensor_copy(hc, src))
                    line.sync()
                    if q < 2:
                        line(e.tensor_tensor(w, src, hc, ALU.subtract))
                        line.sync()
                        src = w

            def tiles(ph, base, post, per=None):
                if per:
                    loop = line.loop(HT, 2 * per)
                    for i in loop:
                        for k in range(2):
                            post(i * 2 + k, k, base + i * 2 + k + 1)
                else:
                    with e.Fori(0, HT) as i:
                        for k in range(2):
                            post(i * 2 + k, k, base + i * 2 + k + 1)
                post(NT - 1, 0, base + NT)

            def aggregate(ph, base, width, turned, hp_base, stages, first_wait):
                E_ = ev[ph]
                spots = {NT * (q + 1) // 4: q for q in range(3)}
                lo0 = lo_at[0]

                def one(j, k, n, late, first=False):
                    done(E_["red"], n - 2 if not first else base)
                    for t in range(NT):
                        if first and t % BT == 0:
                            done(E_["hp"], hp_base + t // BT + 1)
                        if late is not None and t in spots:
                            stages(*late, spots[t])
                        if turned:
                            lhs = ADJ[0:PN, bass.ds(j, 1), t * PN:t * PN + P].rearrange("p o d -> p (o d)")
                        else:
                            lhs = ADJ[0:PN, t, bass.ds(j * PN, P)]
                        mm = e.matmul(AG[k][:, 0:width], lhs, HP[0:PN, t, 0:width], start=(t == 0),
                                      stop=(t == NT - 1), skip_group_check=general)
                    if general:
                        with e.Fori(0, NT) as t:
                            m = (lo0 + base + j) * NT + t
                            e.wait_ge(s_lol, (m + 1) * 16)
                            mm = e.matmul(AG[k][:, 0:width], LOT[0:PN, :],
                                          HP[0:PN, bass.ds(t, 1), 0:width].rearrange("p o f -> p (o f)"),
                                          start=False, stop=True, skip_group_check=True)
                            mm.then_inc(s_lom, 1)
                        e.wait_ge(s_lom, (lo0 + base + j + 1) * NT + 1)
                        e.sem_inc(E_["agg"], 1)
                    else:
                        mm.then_inc(E_["agg"], 1)

                first_wait()
                one(0, 0, base + 1, None, True)
                with e.Fori(0, HT) as i:
                    for k in range(2):
                        one(i * 2 + k + 1, 1 - k, base + i * 2 + k + 2, (i * 2 + k, k, base + i * 2 + k + 1))
                for q in range(3):
                    stages(NT - 1, 0, base + NT, q)

            def tile_of(X, j):
                return X[0:PN, bass.ds(j, 1), :].rearrange("p o f -> p (o f)")

            def parts_sum(E_, k, n, to):
                done(E_["agg"], n)
                return e.tensor_reduce(to, AG[k][0:PN, 0:3 * P].rearrange("p (c f) -> p f c", c=3), AX.X, ALU.add)

            def di(j):
                return DI[0:PN, bass.ds(j, 1)]

            def z_of(j):
                return Zf[0:PN, bass.ds(j * P, P)]

            s0, s1 = ST[0:PN, 0, :], ST[0:PN, 1, :]

            E0 = ev["L0"]
            layer_norm(0, lambda: e.wait_ge(s_x, 16))

            def z_ready(k):
                return lambda: e.wait_ge(s_ln[k][3], NT)
            split("L0", False, z_ready(0))
            if dve:
                line(e.memset(HP[0:PN, :, X0:X0 + 1], 1.0))
                line.sync()
                e.sem_inc(s_ones, 1)
                e.wait_ge(s_w, 16 * N_CONST)

                def post(j, k, n):
                    line(parts_sum(E0, k, n, s1))
                    line(e.tensor_copy(DEG[0:PN, bass.ds(j, 1)], AG[k][0:PN, X0:X0 + 1]))
                    line.sync()
                    done(E0["tr"], n - 1)
                    e.scalar_tensor_tensor(out=s0, in0=z_of(j), scalar=EPS0[0:PN], in1=s1, op0=ALU.mult,
                                           op1=ALU.add).then_inc(E0["red"], 1)
                    done(E0["d2"], n)
                    done(E0["red"], n)
                    line(e.tensor_tensor(s1, P2[0:PN, 0:P], BB[0:PN, :], ALU.add))
                    line.sync()
                    line(e.tensor_scalar(z_of(j), s1, 0.0, None, ALU.max))
                    line.sync()
                    e.tensor_reduce(MX[0:PN, bass.ds(j, 1)], z_of(j), AX.X, ALU.max, negate=True)\
                     .then_inc(E0["z"], 1)
                tiles("L0", 0, post, 4)
            if act:
                e.wait_ge(s_w, 16 * N_CONST)

                def post(j, k, n):
                    done(E0["tr"], n)
                    e.copy(SF[:, 0, 0:PN], TP[:, 0:PN]).then_inc(E0["cf"], 1)
                    done(E0["d1"], n)
                    done(E0["d2"], n - 1)
                    for m in range(2):
                        e.activation(SG[:, m, 0:PN], P1[:, m * P:m * P + PN], ACT.Relu, bias=B_L0[:, m:m + 1])\
                         .then_inc(E0["rg"], 1)
                    done(E0["z"], n)
                    e.wait_ge(E0["mid"], NB + n)
                    settle()
                    e.activation(SF[0:PN, 1, :], z_of(j), ACT.Exp, bias=MX[0:PN, bass.ds(j, 1)],
                                 accum_out=SE[0:PN, bass.ds(j, 1)]).then_inc(E0["mid"], 1)
                tiles("L0", 0, post)
            if pe:
                def stages(j, k, n, q):
                    if q == 0:
                        done(E0["red"], n)
                        e.transpose(TP[:, 0:PN], s0, IDF[0:PN, 0:PN]).then_inc(E0["tr"], 1)
                    if q == 1:
                        done(E0["cf"], n)
                        for m in range(2):
                            mm = e.matmul(P1[:, m * P:m * P + PN], WB[:, m * P:(m + 1) * P], SF[:, 0, 0:PN],
                                          start=True, stop=True)
                        mm.then_inc(E0["d1"], 1)
                    if q == 2:
                        done(E0["rg"], n * 2)
                        for m in range(2):
                            mm = e.matmul(P2[0:PN, 0:P], SG[:, m, 0:PN], WB[:, (2 + m) * P:(3 + m) * P],
                                          start=(m == 0), stop=(m == 1))
                        mm.then_inc(E0["d2"], 1)

                def first():
                    e.wait_ge(s_adj, NT)
                    e.wait_ge(s_ones, 1)
                    e.wait_ge(s_w, 16 * N_CONST)
                aggregate("L0", 0, X0 + 1, False, 0, stages, first)
            lo_at[0] += NT

            if act:
                e.wait_ge(E0["mid"], NB + NT + 1)
                e.activation(TMP[0:PN], SE[0:PN], ACT.Ln).then_inc(s_soft[0], 1)
                done(E0["z"], NT)
                e.activation(SDV[0:PN], DEG[0:PN], ACT.Sqrt).then_inc(s_soft[0], 1)
            if dve:
                e.wait_ge(s_soft[0], 2)
                line(e.reciprocal(DI[0:PN], SDV[0:PN]))
                line(e.tensor_tensor(TMP[0:PN], MX[0:PN], TMP[0:PN], ALU.subtract))
                line(e.tensor_tensor(XR[0:PN], XR[0:PN], Zn[0:PN], ALU.add))
                line.sync()
                line(e.tensor_tensor(XR[0:PN], XR[0:PN], TMP[0:PN].rearrange("p (t o) -> p t o", o=1)
                                     .broadcast_to([PN, NT, P]), ALU.add))
                line.sync()
            if sp:
                done(E0["d2"], NT)
                e.dma_start(WB[:, 0:P], a["L1_gnn_W1"]).then_inc(s_w, 16)
                e.dma_start(WB[:, P:2 * P], a["L1_gnn_W2"]).then_inc(s_w, 16)
                e.wait_ge(s_soft[0], 2)
                done(E0["z"], NT)
                e.dma_start(BB[:, :], bcast(a["L1_gnn_b2"])).then_inc(s_w, 16)
            n_w1 = N_CONST + 3

            layer_norm(1, lambda: None)
            split("L1a", True, z_ready(1))
            E1 = ev["L1a"]
            if dve:
                def post(j, k, n):
                    line(parts_sum(E1, k, n, s1))
                    line.sync()
                    done(E1["tr"], n - 1)
                    e.tensor_scalar(s0, s1, di(j), None, ALU.mult).then_inc(E1["red"], 1)
                    done(E1["d2"], n)
                    e.tensor_scalar(z_of(j), P2[0:PN, 0:P], di(j), None, ALU.mult).then_inc(E1["z"], 1)
                tiles("L1a", 0, post, 1)
            if act:
                def post(j, k, n):
                    done(E1["tr"], n)
                    e.copy(SF[:, 0, 0:PN], TP[:, 0:PN]).then_inc(E1["cf"], 1)
                    done(E1["d1"], n)
                    done(E1["d2"], n - 1)
                    e.activation(SG[:, 0, 0:PN], P1[:, 0:PN], ACT.Relu, bias=B_L1[:, :]).then_inc(E1["rg"], 1)
                tiles("L1a", 0, post)
            if pe:
                def stages(j, k, n, q):
                    if q == 0:
                        done(E1["red"], n)
                        e.transpose(TP[:, 0:PN], s0, IDF[0:PN, 0:PN]).then_inc(E1["tr"], 1)
                    if q == 1:
                        done(E1["cf"], n)
                        e.matmul(P1[:, 0:PN], WB[:, 0:P], SF[:, 0, 0:PN], start=True, stop=True)\
                         .then_inc(E1["d1"], 1)
                    if q == 2:
                        done(E1["rg"], n)
                        done(E1["z"], n - 1)
                        e.matmul(P2[0:PN, 0:P], SG[:, 0, 0:PN], WB[:, P:2 * P], start=True, stop=True)\
                         .then_inc(E1["d2"], 1)
                aggregate("L1a", 0, X0, False, 0, stages, lambda: e.wait_ge(s_w, 16 * n_w1))
            lo_at[0] += NT

            E1b = ev["L1b"]
            split("L1b", False, lambda: done(E1["z"], NT))
            if dve:
                def post(j, k, n):
                    parts_sum(E1b, k, n, s1).then_inc(E1b["red"], 1)
                    done(E1b["red"], n)
                    xj = tile_of(XR, j)
                    line(e.scalar_tensor_tensor(out=xj, in0=s1, scalar=di(j), in1=xj, op0=ALU.mult, op1=ALU.add))
                    line.sync()
                    line(e.tensor_tensor(xj, xj, BB[0:PN, :], ALU.add))
                    line.sync()
                e.wait_ge(s_w, 16 * n_w1)
                tiles("L1b", 0, post, 2)
            if pe:
                aggregate("L1b", 0, X0, False, 0, lambda *_: None, lambda: None)
            lo_at[0] += NT

            E2 = ev["L2"]
            layer_norm(2, lambda: None)
            split("L2", False, z_ready(2))
            if sp:
                done(E1["d2"], NT)
                with e.Fori(0, LAYERS) as l:
                    done(s_bn["w"], l)
                    e.dma_start(WB[:, 0:P], a["L2_gnn_W1"][bass.ds(l, 1)].rearrange("o p n -> (o p) n"))\
                     .then_inc(s_wt, 16)
                    e.dma_start(WB[:, P:2 * P], a["L2_gnn_W2"][bass.ds(l, 1)].rearrange("o p n -> (o p) n"))\
                     .then_inc(s_wt, 16)

            def bias2(q, l):
                return B_L2[:, q, bass.ds(l, 1)]

            def zc_of(j):
                return Zf[:, bass.ds(j * PN, PN)]

            if dve:
                for l in line.loop(LAYERS, 2 * NT + 5):
                    base = l * NT
                    done(E2["hp"], (l + 1) * NB)
                    settle()

                    def post(j, k, n):
                        done(E2["tr"], n - 1)
                        parts_sum(E2, k, n, s0).then_inc(E2["red"], 1)
                        done(E2["d2"], n)
                        line(e.tensor_scalar(zc_of(j), P2[:, 0:PN], bias2(Q_B2, l), None, ALU.add))
                        line.sync()
                        line(e.bn_stats(STATS[:, 0, bass.ds(j, 1), :].rearrange("p o c -> p (o c)"), zc_of(j)))
                        line.sync()
                    tiles("L2", base, post, 2)
                    settle()
                    line(e.bn_aggr(BNM, STATS[:, 0, :, :].rearrange("p t c -> p (t c)")))
                    line.sync()
                    e.sem_inc(s_bn["var"], 1)
                    e.wait_ge(s_bn["sd"], l + 1)
                    line(e.reciprocal(BNR, BNS))
                    line.sync()
                    line(e.tensor_tensor(BNA[:, 0:1], BNR, bias2(Q_GA, l), ALU.mult))
                    line.sync()
                    line(e.tensor_tensor(BNT, BNM[:, 0:1], BNA[:, 0:1], ALU.mult))
                    line.sync()
                    line(e.tensor_tensor(BNB[:, 0:1], bias2(Q_BE, l), BNT, ALU.subtract))
                    line.sync()
                    e.sem_inc(s_bn["ab"], 1)
                    r1, low = dve_parts(E2, (l + 1) * NB, True)
                    r1(0)
                    for b in range(1, NB):
                        r1(b)
                        low(b - 1)
                    low(NB - 1)
                done(E2["hp"], (LAYERS + 1) * NB)
                for q in range(3):
                    line(e.tensor_tensor(XR[0:PN], XR[0:PN], HP[0:PN, :, q * P:(q + 1) * P], ALU.add))
                    line.sync()
            if act:
                with e.Fori(0, LAYERS) as l:
                    def post(j, k, n):
                        done(E2["tr"], n)
                        e.copy(SF[:, 0, 0:PN], TP[:, 0:PN]).then_inc(E2["cf"], 1)
                        done(E2["d1"], n)
                        done(E2["d2"], n - 1)
                        settle()
                        e.activation(SG[:, 0, 0:PN], P1[:, 0:PN], ACT.Relu, bias=bias2(Q_B1, l))\
                         .then_inc(E2["rg"], 1)
                    tiles("L2", l * NT, post)
                    e.wait_ge(s_bn["var"], l + 1)
                    e.activation(BNS, BNM[:, 1:2], ACT.Sqrt, bias=EPSC).then_inc(s_bn["sd"], 1)
                    e.wait_ge(s_bn["ab"], l + 1)

                    def relu(b):
                        zb = Zf[:, b * BT * PN:(b + 1) * BT * PN]
                        e.activation(zb, zb, ACT.Relu, bias=BNB[:, 0:1], scale=BNA[:, 0:1]).then_inc(s_bn["rel"], 1)

                    def before(b):
                        if b == 0:
                            relu(0)
                        if b + 1 < NB:
                            relu(b + 1)

                    def ready(b):
                        e.wait_ge(s_bn["tr"], l * NB + b + 1)
                    ready.from_psum = True
                    act_parts(E2, (l + 1) * NB, ready, before)
            if pe:
                with e.Fori(0, LAYERS) as l:
                    def stages(j, k, n, q):
                        if q == 0:
                            done(E2["red"], n)
                            e.transpose(TP[:, 0:PN], s0, IDF[0:PN, 0:PN]).then_inc(E2["tr"], 1)
                        if q == 1:
                            done(E2["cf"], n)
                            e.matmul(P1[:, 0:PN], WB[:, 0:P], SF[:, 0, 0:PN], start=True, stop=True)\
                             .then_inc(E2["d1"], 1)
                        if q == 2:
                            done(E2["rg"], n)
                            e.matmul(P2[:, 0:PN], WB[:, P:2 * P], SG[:, 0, 0:PN], start=True, stop=True)\
                             .then_inc(E2["d2"], 1)
                    aggregate("L2", l * NT, X0, False, l * NB, stages,
                              lambda: e.wait_ge(s_wt, (l + 1) * 32))
                    e.wait_ge(E2["d2"], (l + 1) * NT + 1)
                    e.sem_inc(s_bn["w"], 1)
                    for b in range(NB):
                        e.wait_ge(s_bn["rel"], l * NB + b + 1)
                        if b >= 2:
                            done(E2["hp"], (l + 1) * NB + b - 1)
                        for m in range(BT):
                            c = (b * BT + m) * PN
                            mm = e.transpose(RB[b % 2][0:PN, m * P:(m + 1) * P], Zf[:, c:c + PN], IDF[:, :])
                        mm.then_inc(s_bn["tr"], 1)
            lo_at[0] += NT * LAYERS

            TB = [(q * NT // 4, (q + 1) * NT // 4) for q in range(4)]
            banks = [PS[:, q, :].bitcast(BF16) for q in range(4)]
            PB = P
            if general and pe:
                with e.Fori(0, NT * NT) as m:
                    e.wait_ge(s_lod, m * 32 + 16)
                    e.transpose(banks[0][0:PN, 0:PN], LOX[0:PN, 0:PN], IDB[0:PN, 0:PN]).then_inc(s_lox, 1)
            if general and dve:
                with e.Fori(0, NT * NT) as m:
                    e.wait_ge(s_lox, m + 1)
                    e.tensor_copy(LOT[0:PN, 0:PN], banks[0][0:PN, 0:PN]).then_inc(s_loc, 1)
            if general and pe:
                e.wait_ge(s_loc, NT * NT)
            if pe:
                with e.Fori(0, NT) as t:
                    for q, (b0, b1) in enumerate(TB):
                        done(s_at["dve" if q % 2 else "act"], t * 2)
                        for b in range(b0, b1):
                            mm = e.transpose(banks[q][0:PN, (b - b0) * PB:(b - b0) * PB + PN],
                                             ADJ[0:PN, bass.ds(t, 1), b * PN:(b + 1) * PN]
                                             .rearrange("p o d -> p (o d)"), IDB[0:PN, 0:PN])
                        mm.then_inc(s_at["tr"], 1)
            if act or dve:
                layer_norm(3, lambda: None)
                with e.Fori(0, NT) as t:
                    for q, (b0, b1) in enumerate(TB):
                        if (q % 2 == 1) != dve:
                            continue
                        e.wait_ge(s_at["tr"], t * 4 + q + 1)
                        to = ADJ[0:PN, bass.ds(t, 1), b0 * PN:b1 * PN].rearrange("p o (b d) -> p (o b) d", d=PN)
                        fr = banks[q][0:PN, 0:(b1 - b0) * PB].rearrange("p (b d) -> p b d", d=PB)[:, :, 0:PN]
                        (e.tensor_copy if dve else e.copy)(to, fr).then_inc(s_at["dve" if dve else "act"], 1)

            Y = lambda q: y_d[q]
            E3, E3b = ev["L3a"], ev["L3b"]
            split("L3a", True, z_ready(3))
            if sp:
                done(E2["d2"], NT * LAYERS)
                e.dma_start(WB[:, 0:3 * P].rearrange("p (q n) -> p q n", q=3),
                            a["L3_gnn_l1_w"].rearrange("q p n -> p q n")).then_inc(s_wt, 16)
                e.wait_ge(s_ln[3][2], 1)
                e.dma_start(BB[0:1, :], a["L3_gnn_l1_b"][1:2]).then_inc(s_wt, 16)

                def post(j, k, n):
                    e.wait_ge(E3["z"], n * 2 + 1)
                    e.dma_start(y_d[1][:, bass.ds(j * PN, PN)], SG[:, 0, 0:PN]).then_inc(s_y, 16)
                    e.dma_start(y_d[0][:, bass.ds(j * PN, PN)], SG[:, 1, 0:PN]).then_inc(s_y, 16)
                tiles("L3a", 0, post)
                e.wait_ge(E3["d1"], NT + 1)
                e.dma_start(BB[0:1, :], a["L3_gnn_l1_b"][2:3]).then_inc(s_wt, 16)

                def post(j, k, n):
                    e.wait_ge(E3b["z"], n + 1)
                    e.dma_start(y_d[2][:, bass.ds(j * PN, PN)], SG[:, 0, 0:PN]).then_inc(s_y, 16)
                tiles("L3b", 0, post)
            wt0 = 32 * LAYERS

            def mix_dve(E_, first):
                yb = 0 if first else 32 * NT

                def post(j, k, n):
                    done(E_["tr"], n - 1)
                    if first:
                        line(e.tensor_copy(s1, z_of(j)))
                    line(parts_sum(E_, k, n, s0))
                    line(e.tensor_reduce(RC[0:PN], AG[k][0:PN, X0:X0 + 3], AX.X, ALU.add))
                    line.sync()
                    line(e.tensor_scalar(s0, s0, di(j), None, ALU.mult))
                    line(e.tensor_scalar(RC[0:PN], RC[0:PN], di(j), None, ALU.mult))
                    line.sync()
                    if first:
                        line(e.tensor_scalar(z_of(j), s0, di(j), None, ALU.mult))
                        line(e.tensor_scalar(RD[0:PN, bass.ds(j, 1)], RC[0:PN], di(j), None, ALU.mult))
                        line.sync()
                    e.sem_inc(E_["red"], 1)
                    done(E_["d1"], n)
                    done(s_y, yb + (n - 1) * (32 if first else 16))
                    outs = ((0, P1[:, 0:PN], None, 1), (1, P1[:, P:P + PN], B_L3[:, R_B1, 0:1], 0)) if first else \
                           ((0, P1[:, 0:PN], None, 2),)
                    for r, src, bias, q in outs:
                        if bias is None:
                            line(e.tensor_copy(SG[:, r, 0:PN], src))
                        else:
                            line(e.tensor_scalar(SG[:, r, 0:PN], src, bias, None, ALU.add))
                    line.sync()
                    for r, src, bias, q in outs:
                        e.bn_stats(STATS[:, q, bass.ds(j, 1), :].rearrange("p o c -> p (o c)"), SG[:, r, 0:PN])\
                         .then_inc(E_["z"], 1)
                return post

            def mix_act(E_, first):
                def post(j, k, n):
                    done(E_["tr"], n)
                    done(E_["d1"], n - 1)
                    e.copy(SF[:, 0, 0:PN], TP[:, 0:PN]).then_inc(E_["cf"], 1)
                    if first:
                        e.copy(SF[:, 1, 0:PN], TP[:, P:P + PN]).then_inc(E_["cf"], 1)
                    e.copy(ROW[0:1, 0:PN], TP[0:1, 2 * P:2 * P + PN]).then_inc(E_["cf"], 1)
                return post

            def mix_pe(E_, first, wq):
                per = 3 if first else 2

                def stages(j, k, n, q):
                    if q == 0:
                        done(E_["red"], n)
                        e.transpose(TP[:, 0:PN], s0, IDF[0:PN, 0:PN])
                        if first:
                            e.transpose(TP[:, P:P + PN], s1, IDF[0:PN, 0:PN])
                        e.matmul(TP[0:1, 2 * P:2 * P + PN], RC[0:PN], IDF[0:PN, 0:PN], start=True, stop=True)\
                         .then_inc(E_["tr"], 1)
                    if q == 2:
                        done(E_["cf"], n * per)
                        done(E_["z"], (n - 1) * (per - 1))
                        e.matmul(P1[:, 0:PN], WB[:, wq * P:(wq + 1) * P], SF[:, 0, 0:PN], start=True, stop=False)
                        mm = e.matmul(P1[:, 0:PN], BB[0:1, :], ROW[0:1, 0:PN], start=False, stop=True)
                        if first:
                            mm = e.matmul(P1[:, P:P + PN], WB[:, 0:P], SF[:, 1, 0:PN], start=True, stop=True)
                        mm.then_inc(E_["d1"], 1)
                return stages

            if dve:
                done(E3["hp"], NB)
                extra_columns(DI[0:PN])
                e.sem_inc(s_rt, 1)
                tiles("L3a", 0, mix_dve(E3, True), 9)
            if act:
                tiles("L3a", 0, mix_act(E3, True))
            if pe:
                def first():
                    e.wait_ge(s_at["act"], 2 * NT + 1)
                    e.wait_ge(s_at["dve"], 2 * NT + 1)
                    e.wait_ge(s_rt, 1)
                    e.wait_ge(s_wt, wt0 + 32)
                aggregate("L3a", 0, X0 + 3, True, 0, mix_pe(E3, True, 1), first)
            lo_at[0] += NT
            if dve:
                done(E3["z"], 2 * NT)
            split("L3b", False, lambda: done(E3["z"], 2 * NT))
            if dve:
                extra_columns(RD[0:PN])
                e.sem_inc(s_rt, 1)
                tiles("L3b", 0, mix_dve(E3b, False), 5)
            if act:
                tiles("L3b", 0, mix_act(E3b, False))
            if pe:
                def first():
                    e.wait_ge(s_rt, 2)
                    e.wait_ge(s_wt, wt0 + 48)
                aggregate("L3b", 0, X0 + 3, True, 0, mix_pe(E3b, False, 2), first)
            lo_at[0] += NT

            VW = HPf[:, 0:9 * P]
            FP = HPf[:, 9 * P:12 * P]
            CB = HPf[:, 12 * P:15 * P]
            YT = [HPf[:, (15 + 3 * k) * P:(18 + 3 * k) * P].rearrange("p (q n) -> p q n", q=3) for k in range(2)]
            Q1T = [HPf[:, (21 + k) * P:(22 + k) * P] for k in range(2)]
            FB = HPf[:, 23 * P:24 * P]
            L2R = Zf[:, 0:9 * P].rearrange("p (j g n) -> p j g n", j=3, g=3)
            L2T = Zf[:, 9 * P:18 * P].rearrange("p (j g n) -> p j g n", j=3, g=3)
            BBR = Zf[:, 18 * P:21 * P]
            if sp:
                done(E3b["agg"], NT)
                e.dma_start(FP.rearrange("p (j n) -> p j n", j=3),
                            a["L3_gnn_fp_w"].rearrange("(j p) n -> p j n", p=P)).then_inc(s_vw, 16)
                e.dma_start(FB, bcast(a["L3_gnn_fp_b"])).then_inc(s_vw, 16)
                for j in range(3):
                    e.dma_start(L2R[:, j], a["L3_gnn_l2_w"][j].rearrange("(g p) n -> p g n", p=P))\
                     .then_inc(s_vw, 16)
            if pe:
                e.wait_ge(s_vw, 80)
                done(E3b["z"], NT)
                for j in range(3):
                    for g in range(3):
                        mm = e.transpose(PS[:, j, g * P:(g + 1) * P], L2R[:, j, g, :], IDF[:, :])
                    mm.then_inc(s_vt, 1)
                for j in range(3):
                    e.wait_ge(s_vc, j + 1)
                    for g in range(3):
                        e.matmul(PS[:, 3 + j, g * P:(g + 1) * P], L2T[:, j, g, :], FP[:, j * P:(j + 1) * P],
                                 start=True, stop=True)
                    e.matmul(PS[:, 3 + j, 3 * P:4 * P], BBR[:, j * P:(j + 1) * P], FP[:, j * P:(j + 1) * P],
                             start=True, stop=True).then_inc(s_vm, 1)
            if act:
                for j in range(3):
                    e.wait_ge(s_vt, j + 1)
                    line(e.copy(L2T[:, j].rearrange("p g n -> p (g n)"), PS[:, j, 0:3 * P]))
                    line(e.activation(BBR[:, j * P:(j + 1) * P], IDF[:, :], ACT.Identity,
                                      bias=B_L3[:, R_B2, j:j + 1], scale=0.0))
                    line.sync()
                    e.sem_inc(s_vc, 1)
                for j in range(3):
                    e.wait_ge(s_vm, j + 1)
                    e.copy(VW.rearrange("p (g j n) -> p g j n", g=3, j=3)[:, :, j, :],
                           PS[:, 3 + j, 0:3 * P].rearrange("p (g n) -> p g n", g=3)).then_inc(s_vv, 1)
                    e.copy(CB[:, j * P:(j + 1) * P], PS[:, 3 + j, 3 * P:4 * P]).then_inc(s_vv, 1)
            if dve:
                for q in range(3):
                    done(E3b["z"], NT)
                    done(E3["z"], 2 * NT)
                    line(e.bn_aggr(BNM, STATS[:, q, :, :].rearrange("p t c -> p (t c)")))
                    line.sync()
                    e.sem_inc(s_bn["var"], 1)
                    e.wait_ge(s_bn["sd"], LAYERS + q + 1)
                    line(e.reciprocal(BNR, BNS))
                    line.sync()
                    line(e.tensor_tensor(BNA[:, q:q + 1], BNR, B_L3[:, R_GA, q:q + 1], ALU.mult))
                    line.sync()
                    line(e.tensor_tensor(BNT, BNM[:, 0:1], BNA[:, q:q + 1], ALU.mult))
                    line.sync()
                    line(e.tensor_tensor(BNB[:, q:q + 1], B_L3[:, R_BE, q:q + 1], BNT, ALU.subtract))
                    line.sync()
                e.sem_inc(s_bn["ab"], 1)
                e.wait_ge(s_vv, 6)
                line(e.tensor_tensor(CB[:, 0:P], CB[:, 0:P], FB, ALU.add))
                line.sync()
            if act:
                for q in range(3):
                    e.wait_ge(s_bn["var"], LAYERS + q + 1)
                    e.activation(BNS, BNM[:, 1:2], ACT.Sqrt, bias=EPSC).then_inc(s_bn["sd"], 1)
                e.wait_ge(s_bn["ab"], LAYERS + 1)
            if sp:
                e.wait_ge(s_y, 1 + 48 * NT)
                e.wait_ge(s_vv, 6)
                for j in range(2):
                    e.dma_start(YT[j][:, :, 0:PN], y_d[:, :, j * PN:(j + 1) * PN].rearrange("q p n -> p q n"))\
                     .then_inc(s_yl[j], 16)

                def store(j, k, n, more=True):
                    if more:
                        done(s_vq, n)
                        e.dma_start(YT[k][:, :, 0:PN],
                                    y_d[:, :, bass.ds((j + 2) * PN, PN)].rearrange("q p n -> p q n"))\
                         .then_inc(s_yl[k], 16)
                    done(s_vd, n)
                    e.dma_start(q1_d[bass.ds(j, 1)].rearrange("o p f -> (o p) f"), Q1T[k][0:PN]).then_inc(s_q1, 16)
                with e.Fori(0, HT - 1) as i:
                    for k in range(2):
                        store(i * 2 + k, k, i * 2 + k + 1)
                store(NT - 3, 0, NT - 2)
                store(NT - 2, 1, NT - 1, False)
                store(NT - 1, 0, NT, False)
            if act:
                def post(j, k, n):
                    e.wait_ge(s_yl[k], (j - k) * 8 + 16)
                    for q in range(3):
                        yt = YT[k][:, q, 0:PN]
                        ins = e.activation(yt, yt, ACT.Relu, bias=BNB[:, q:q + 1], scale=BNA[:, q:q + 1])
                        ins.then_inc(s_vr, 1)
                tiles("V", 0, post)
            if pe:
                e.wait_ge(s_vv, 6)

                def post(j, k, n):
                    e.wait_ge(s_vr, n * 3 + 1)
                    done(s_vd, n - 1)
                    for q in range(3):
                        mm = e.matmul((P1, P2)[k][0:PN, 0:3 * P], YT[k][:, q, 0:PN], VW[:, q * 3 * P:(q + 1) * 3 * P],
                                      start=(q == 0), stop=(q == 2))
                    mm.then_inc(s_vq, 1)
                tiles("V", 0, post)
            if dve:
                def post(j, k, n):
                    done(s_vq, n)
                    pv = (P1, P2)[k][0:PN]
                    xj = tile_of(XR, j)
                    done(s_q1, (n - 1) * 16)
                    line(e.tensor_tensor(xj, pv[:, 0:P], xj, ALU.add))
                    line(e.tensor_tensor(Q1T[k][0:PN], pv[:, P:2 * P], CB[0:PN, P:2 * P], ALU.add))
                    line(e.tensor_tensor(s0, pv[:, 2 * P:3 * P], CB[0:PN, 2 * P:3 * P], ALU.add))
                    line.sync()
                    line(e.tensor_tensor(xj, xj, CB[0:PN, 0:P], ALU.add))
                    line(e.tensor_scalar(z_of(j), s0, di(j), None, ALU.mult))
                    line.sync()
                    e.sem_inc(s_vd, 1)
                tiles("V", 0, post, 5)

            Ec, Ed = ev["L3c"], ev["L3d"]
            split("L3c", False, lambda: (done(s_vd, NT), done(s_q1, 16 * NT)))
            if sp:
                e.wait_ge(s_q1, 1 + 16 * NT)

                def post(j, k, n):
                    done(Ec["z"], n - 1)
                    e.dma_start(SG[0:PN, 0, :], q1_d[bass.ds(j, 1)].rearrange("o p f -> (o p) f"))\
                     .then_inc(s_q1l, 16)
                tiles("L3c", 0, post)

                def post(j, k, n):
                    done(Ed["z"], n)
                    e.dma_start(out[bass.ds(j * PN, PN)], ST[0:PN, 1, :]).then_inc(s_out, 16)
                tiles("L3d", 0, post)
                e.wait_ge(s_out, 1 + 16 * NT)
            if dve:
                def post(j, k, n):
                    line(parts_sum(Ec, k, n, s1))
                    line.sync()
                    e.sem_inc(Ec["red"], 1)
                    e.wait_ge(s_q1l, n * 16 + 1)
                    line(e.scalar_tensor_tensor(out=s0, in0=s1, scalar=di(j), in1=SG[0:PN, 0, :], op0=ALU.mult,
                                                op1=ALU.add))
                    line.sync()
                    line(e.tensor_scalar(z_of(j), s0, di(j), None, ALU.mult))
                    line.sync()
                    e.sem_inc(Ec["z"], 1)
                tiles("L3c", 0, post, 3)
            if pe:
                aggregate("L3c", 0, X0, True, 0, lambda *_: None, lambda: None)
            lo_at[0] += NT
            split("L3d", False, lambda: done(Ec["z"], NT))
            if dve:
                def post(j, k, n):
                    line(parts_sum(Ed, k, n, s0))
                    line.sync()
                    e.sem_inc(Ed["red"], 1)
                    e.wait_ge(s_out, (n - 1) * 16 + 1)
                    line(e.scalar_tensor_tensor(out=s1, in0=s0, scalar=di(j), in1=tile_of(XR, j), op0=ALU.mult,
                                                op1=ALU.add))
                    line.sync()
                    e.sem_inc(Ed["z"], 1)
                tiles("L3d", 0, post, 2)
            if pe:
                aggregate("L3d", 0, X0, True, 0, lambda *_: None, lambda: None)
            lo_at[0] += NT

        N_CONST = 14
        block = ctx.enter_context(nc.Block())

        @block.sync
        def _(e):
            program("sp", e)

        @block.gpsimd
        def _(e):
            program("pool", e)

        @block.scalar
        def _(e):
            program("act", e)

        @block.tensor
        def _(e):
            program("pe", e)

        @block.vector
        def _(e):
            program("dve", e)


INPUTS = ("x", "src", "dst", "L0_gnn_W1", "L0_gnn_b1", "L0_gnn_W2", "L0_gnn_b2", "L0_gnn_eps", "L1_gnn_W1",
          "L1_gnn_b1", "L1_gnn_W2", "L1_gnn_b2", "L2_gnn_W1", "L2_gnn_b1", "L2_gnn_W2", "L2_gnn_b2",
          "L2_gnn_gamma", "L2_gnn_beta", "L3_gnn_l1_w", "L3_gnn_l1_b", "L3_gnn_bn_gamma", "L3_gnn_bn_beta",
          "L3_gnn_l2_w", "L3_gnn_l2_b", "L3_gnn_fp_w", "L3_gnn_fp_b")


def kernel(**inputs):
    import numpy as np
    import concourse.bacc as bacc
    from concourse.bass_utils import run_bass_kernel_spmd

    nc = bacc.Bacc("TRN2", target_bir_lowering=False, num_devices=1)
    arrays, aps = {}, {}
    for name in INPUTS:
        v = np.ascontiguousarray(inputs[name])
        if name == "L0_gnn_eps":
            v = v.reshape(1)
        arrays["in_" + name] = v
        aps[name] = nc.dram_tensor("in_" + name, v.shape, mybir.dt.from_np(v.dtype), kind="ExternalInput").ap()
    out = nc.dram_tensor("out_x", arrays["in_x"].shape, F32, kind="ExternalOutput").ap()
    build(nc, aps, out)
    r = run_bass_kernel_spmd(nc, [arrays], core_ids=[0])
    return r.results[0]["out_x"]
```

```python
from contextlib import ExitStack

import concourse.bass as bass
from concourse import mybir

F32 = mybir.dt.float32
BF16 = mybir.dt.bfloat16
F16 = mybir.dt.float16
I32 = mybir.dt.int32
U32 = mybir.dt.uint32
ALU = mybir.AluOpType
ACT = mybir.ActivationFunctionType
AX = mybir.AxisListType

P = 128
CH = 128
GC = 2
GE = GC * CH
WIN = 25
HG = 7
RING = 7
GW = 20
LN_EPS = 1e-5
BN_EPS = 1e-5
PAD_SRC = -10000000


class Line:

    def __init__(self, eng, sem):
        self.eng, self.sem, self.n, self.off = eng, sem, 0, 0

    def __call__(self, ins):
        ins.then_inc(self.sem, 1)
        self.n += 1

    def sync(self):
        self.eng.wait_ge(self.sem, self.off + self.n)

    def loop(self, times, per):
        start, off = self.n, self.off
        with self.eng.Fori(0, times) as i:
            self.off = off + i * per
            yield i
            assert self.n - start == per, (self.n - start, per)
        self.off, self.n = off, start + times * per


def divisor(n, most):
    return max(d for d in range(1, most + 1) if n % d == 0)


def build(nc, a, out):
    N, D = a["x"].shape
    E = a["src"].shape[0]
    assert D == P
    PN = divisor(N, P)
    NT = N // PN
    assert NT % 2 == 1 and NT % 5 == 0
    NB = NT // 5
    BT = 5
    HT = (NT - 1) // 2
    G = -(-E // GE)
    G = -(-G // (2 * HG)) * 2 * HG
    assert G > E // GE
    QG = divisor(G, P)
    KR = G // QG
    NCH = G * GC
    STEPS = G // (2 * HG)
    KW = WIN * NT
    KWP = KW + KW % 2
    HALF = (WIN - 1) // 2
    AW = N + WIN
    AW += AW % 2
    GWN = -(-N // GW)
    assert GWN * GW <= AW and NT * GW <= 512
    FULL = E // GE
    HC = HG * GC
    assert (2 * HC) % RING == 0 and HC >= RING + HG and HC % 2 == 0 and NCH % 2 == 0
    LAYERS = a["L2_gnn_W1"].shape[0]
    FW = P + 2
    X0 = P
    LOW = 2048.0
    TOP = 16384.0
    SPREAD = 32.0
    assert (E + N) * P ** 0.5 / SPREAD < 60000

    ctx = ExitStack()
    with ctx:
        def sb(name, shape, dt):
            return ctx.enter_context(nc.sbuf_tensor(name, shape, dt))

        def sem(name):
            return ctx.enter_context(nc.semaphore(name))

        def dram(name, shape, dt):
            return nc.dram_tensor(name, shape, dt).ap()

        RW = KR * GE
        OHW = -(-KWP // 64) * 64
        IOW = max(KWP, P)
        SRW = max(RW, HC * P // 2)
        FTW = (STEPS + 1) * 16
        ADJ = sb("ADJ", [P, NT, AW], BF16)
        HPb = sb("HPb", [P, max(NT * 2 * FW, RING * OHW + 2 * HC * P + NT * GW, 8 * RW, 48 * P)], BF16)[:, :]
        XRf = sb("XRf", [P, max(NT * P, RW + SRW + KWP // 2 + 4 + P // 2 + FTW)], F32)[:, :]
        Zf = sb("Zf", [P, max(NT * P, 3 * NCH + (NCH + HC) // 2, 21 * P)], F32)[:, :]
        HP = HPb[:, 0:NT * 2 * FW].bitcast(F16).rearrange("p (t q f) -> p t q f", t=NT, q=2)
        XR = XRf[:, 0:NT * P].rearrange("p (t f) -> p t f", t=NT)
        Zn = Zf[:, 0:NT * P].rearrange("p (t f) -> p t f", t=NT)
        WB = sb("WB", [P, max(4 * P + 6 * NT, 3 * P + 18 * NT)], F32)
        STATS = WB[:, 3 * P:3 * P + 18 * NT].rearrange("p (q t c) -> p q t c", q=3, c=6)
        LNS = WB[:, 4 * P:4 * P + 6 * NT].rearrange("p (t c) -> p t c", c=6)
        BB = sb("BB", [P, P], F32)
        IDF = sb("IDF", [P, P], F32)
        IDB = sb("IDB", [P, P], BF16)
        INV = sb("INV", [P, P], F32)
        ST = sb("ST", [P, 2, FW], F32)
        SF = sb("SF", [P, 2, P], F32)
        SG = sb("SG", [P, 2, P], F32)
        SMW = 11 * NT + 24
        SM = sb("SM", [P, SMW], F32)
        FL = sb("FL", [P, 4], I32)
        B_L0 = sb("B_L0", [P, 2], F32)
        B_L1 = sb("B_L1", [P, 1], F32)
        B_L2 = sb("B_L2", [P, 4, LAYERS], F32)
        B_L3 = sb("B_L3", [P, 4, 3], F32)
        Q_B1, Q_B2, Q_GA, Q_BE = range(4)
        R_B1, R_GA, R_BE, R_B2 = range(4)
        LOT = sb("LOT", [P, P], BF16)
        LOX = sb("LOX", [P, P], BF16)
        ROW = sb("ROW", [1, P], F32)
        PS = ctx.enter_context(nc.psum_tensor("PS", [P, 8, 512], F32))

        at = [0]

        def small(n):
            at[0] += n
            assert at[0] <= SMW
            return SM[:, at[0] - n:at[0]]

        DI = small(NT)
        DEG = small(NT)
        DIL = small(NT)
        MV = small(2 * NT).rearrange("p (t c) -> p t c", c=2)
        SDV = small(NT)
        RS = small(NT)
        NBI = small(NT)
        MX = small(NT)
        SE = small(NT)
        TMP = small(NT)
        RC = small(1)
        EPSC = small(1)
        EPS0 = small(1)
        EPSL = small(1)
        CF = small(1)
        BND = small(3)
        BNM = small(2)
        BNS = small(1)
        BNR = small(1)
        BNT = small(1)
        BNA = small(3)
        BNB = small(3)
        BND2 = small(3)
        ONEC = small(1)
        WBASE = small(1)

        HPf = HPb.bitcast(F32)
        dst_i = XRf[:, 0:RW].bitcast(I32)
        src_i = XRf[:, RW:2 * RW].bitcast(I32)
        c0 = RW + SRW
        IOK = XRf[:, c0:c0 + KWP // 2].bitcast(F16)
        c0 += -(-(KWP // 2) // 4) * 4
        IOP = XRf[:, c0:c0 + P // 2].bitcast(F16)
        c0 += P // 2
        FT = XRf[:, c0:c0 + FTW].bitcast(I32)
        dst_f, src_f, til_f, key_f = (HPf[:, k * RW:(k + 1) * RW] for k in range(4))
        iota_i = HPf[:, 0:IOW].bitcast(I32)
        OHK = [HPb[:, k * OHW:k * OHW + KWP] for k in range(RING)]
        c0 = RING * OHW
        OHP = [HPb[:, c0 + k * HC * P:c0 + (k + 1) * HC * P].rearrange("p (n c) -> p n c", c=HC) for k in range(2)]
        OHG = [HPb[:, c0 + k * P:c0 + (k + 1) * P] for k in range(2)]
        c0 += 2 * HC * P
        LOB = HPb[:, c0:c0 + NT * GW].rearrange("p (t d) -> p t d", t=NT)
        KT, PT, KGT = (Zf[:, k * NCH:(k + 1) * NCH] for k in range(3))
        PTH = Zf[:, 3 * NCH:3 * NCH + (NCH + HC) // 2].bitcast(F16)
        IOC = XRf[:, RW:RW + HC * P // 2].bitcast(F16).rearrange("p (n c) -> p n c", c=HC)

        base_d = dram("base_d", [G + 1], I32)
        lo_d = dram("lo_d", [P, NT, AW], BF16)
        y_d = dram("y_d", [3, P, N], F32)
        q1_d = dram("q1_d", [NT, PN, P], F32)

        AG = [PS[:, 0, :], PS[:, 1, :]]
        TP, P1, P2, P3 = (PS[:, b, :] for b in (2, 3, 4, 5))
        RB = [PS[:, 4:6, :].rearrange("p b c -> p (b c)"), PS[:, 6:8, :].rearrange("p b c -> p (b c)")]
        WPS = [PS[:, 0:2, :], PS[:, 2:4, :]]
        CPS = [PS[:, 4, :], PS[:, 5, :]]

        s_in, s_w, s_x, s_base, s_const, s_pad, s_rows = (sem("s_" + n) for n in
                                                          ("in", "w", "x", "base", "const", "pad", "rows"))
        s_dve0, s_dve1, s_act1, s_pool0 = (sem(n) for n in ("s_dve0", "s_dve1", "s_act1", "s_pool0"))
        s_rowt, s_rowc = sem("s_rowt"), sem("s_rowc")
        s_frow, s_fsum, s_frow2, s_fsum2 = (sem("s_f%d" % k) for k in range(4))
        s_flag, s_flag2 = sem("s_flag"), sem("s_flag2")
        s_oh = sem("s_oh")
        s_ohx = sem("s_ohx")
        s_mv = sem("s_mv")
        s_add = sem("s_add")
        s_bline = sem("s_bline")
        s_goh, s_gox, s_gline, s_glo = (sem("s_g" + n) for n in ("oh", "ox", "line", "lo"))
        s_lol, s_lox, s_lom, s_lod, s_loc = (sem("s_lo" + n) for n in "lxmdc")
        s_adj = sem("s_adj")
        PHASES = {"L0": "tr cf d1 rg d2 z ex", "L1a": "tr cf d1 rg d2 z", "L1b": "", "L2": "tr cf d1 rg d2 z",
                  "L3a": "tr cf d1 z", "L3b": "tr cf d1 z", "L3c": "z", "L3d": "z"}
        ev = {p: {n: sem(f"{p}_{n}") for n in ("agg red hi hp " + more).split()}
              for p, more in PHASES.items()}
        s_ln = [[sem(f"ln{k}_{m}") for m in range(3)] for k in range(4)]
        s_soft, s_xr, s_sc = sem("s_soft"), sem("s_xr"), [sem(f"s_sc{m}") for m in range(6)]
        s_bn = {n: sem("bn_" + n) for n in ("var", "sd", "ab", "rel", "tr", "w")}
        s_wt, s_ones = sem("s_wt"), sem("s_ones")
        s_at = {n: sem("at_" + n) for n in ("tr", "act", "dve")}
        s_y, s_yl0, s_vw, s_vt, s_vc, s_vm, s_vv, s_vr, s_vq, s_vd = (sem("s_v%d" % k) for k in range(10))
        s_yl = [s_yl0, sem("s_yl1")]
        s_null = sem("s_null")
        s_q1, s_q1l, s_out = sem("s_q1"), sem("s_q1l"), sem("s_out")
        s_rt = sem("s_rt")
        credited = [s for p in PHASES for s in ev[p].values()] + [s_y, s_q1, s_q1l, s_at["act"], s_at["dve"],
                                                                  s_vr, s_vq, s_vd, s_out, s_lom, s_bn["w"]]

        def col(v):
            return v.rearrange("(p o) -> p o", o=1)

        def bcast(v, n=P):
            return v.rearrange("(o n) -> o n", o=1).broadcast_to([n, v.shape[0]])

        def program(role, e):
            pe, act, dve, pool, sp = (role == r for r in ("pe", "act", "dve", "pool", "sp"))

            n_in = 2 * (sum(1 for k in range(KR) if FULL - k * QG > 0) + (1 if E % GE else 0))
            if sp:
                e.wait_ge(s_pad, 2)
                for dram_t, tile in ((a["dst"], dst_i), (a["src"], src_i)):
                    t3 = tile.rearrange("p (k e) -> p k e", k=KR)
                    for k in range(KR):
                        n = min(QG, FULL - k * QG)
                        if n > 0:
                            e.dma_start(t3[0:n, k, :], dram_t[k * QG * GE:(k * QG + n) * GE]
                                        .rearrange("(q e) -> q e", e=GE)).then_inc(s_in, 16)
                    r = E - FULL * GE
                    if r:
                        q, k = FULL % QG, FULL // QG
                        e.dma_start(t3[q:q + 1, k, 0:r], dram_t[FULL * GE:E].rearrange("(o e) -> o e", o=1))\
                         .then_inc(s_in, 16)
            if act:
                e.dma_start(WB[:, 0:2 * P], a["L0_gnn_W1"]).then_inc(s_w, 16)
                e.dma_start(WB[:, 2 * P:4 * P].rearrange("p (k n) -> p k n", k=2),
                            a["L0_gnn_W2"].rearrange("(k p) n -> p k n", p=P)).then_inc(s_w, 16)
                e.dma_start(BB[:, :], bcast(a["L0_gnn_b2"])).then_inc(s_w, 16)
                e.dma_start(EPS0, bcast(a["L0_gnn_eps"])).then_inc(s_w, 16)
                e.dma_start(B_L0[:, :], a["L0_gnn_b1"].rearrange("(k p) -> p k", p=P),
                            allow_slow_non_contiguous=True).then_inc(s_w, 16)
                e.dma_start(B_L1[:, :], col(a["L1_gnn_b1"])).then_inc(s_w, 16)
                for q, n in enumerate(("b1", "b2", "gamma", "beta")):
                    e.dma_start(B_L2[:, q, :], a["L2_gnn_" + n].rearrange("l p -> p l"),
                                allow_slow_non_contiguous=True).then_inc(s_w, 16)
                for q, n in enumerate(("l1_b", "bn_gamma", "bn_beta", "l2_b")):
                    v = a["L3_gnn_" + n]
                    v = v.rearrange("q p -> p q") if len(v.shape) == 2 else v.rearrange("(q p) -> p q", p=P)
                    e.dma_start(B_L3[:, q, :], v, allow_slow_non_contiguous=True).then_inc(s_w, 16)
            if pool:
                for s in credited:
                    e.sem_inc(s, 1)
                line = Line(e, s_pool0)
                line(e.memset(IDF[:, :], 0.0))
                line(e.iota(iota_i, [[1, IOW]], base=0, channel_multiplier=0))
                line(e.memset(ADJ[:, :, 0:1], 0.0))
                line(e.memset(ADJ[:, :, AW - WIN - 8:AW], 0.0))
                line.sync()
                line(e.affine_select(out=IDF[:, :], in_=IDF[:, :], compare_op=ALU.not_equal, fill=1.0,
                                     base=0, pattern=[[-1, P]], channel_multiplier=1))
                line(e.tensor_copy(IOK, iota_i[:, 0:KWP]))
                line(e.tensor_copy(IOP, iota_i[:, 0:P]))
                line.sync()
                line(e.tensor_copy(IDB[:, :], IDF[:, :]))
                line.sync()
                e.sem_inc(s_const, 1)
            if dve:
                line = Line(e, s_dve0)
                e.memset(dst_i, N).then_inc(s_pad, 1)
                e.memset(src_i, PAD_SRC).then_inc(s_pad, 1)
                e.memset(FL[:, 3:4], N).then_inc(s_pad, 1)
                line(e.memset(ONEC, 1.0))
                line(e.memset(EPSC, LN_EPS))
                e.wait_ge(s_const, 1)
                e.wait_ge(s_in, 16 * n_in)
                line(e.tensor_copy(src_f, src_i))
                line(e.tensor_copy(dst_f, dst_i))
                line.sync()
                line(e.tensor_scalar(key_f.bitcast(I32), src_f, -(PN - 1) / 2.0, 1.0 / PN, ALU.add, ALU.mult))
                line.sync()
                line(e.tensor_copy(til_f, key_f.bitcast(I32)))
                line.sync()
                line(e.scalar_tensor_tensor(out=src_f, in0=til_f, scalar=-float(PN), in1=src_f,
                                            op0=ALU.mult, op1=ALU.add))
                line.sync()
                for cmp, edge, way in ((ALU.is_lt, 0.0, -1.0), (ALU.is_ge, float(PN), 1.0)):
                    line(e.tensor_scalar(key_f, src_f, edge, way, cmp, ALU.mult))
                    line.sync()
                    line(e.tensor_tensor(til_f, til_f, key_f, ALU.add))
                    line(e.scalar_tensor_tensor(out=src_f, in0=key_f, scalar=-float(PN), in1=src_f,
                                                op0=ALU.mult, op1=ALU.add))
                    line.sync()
                line(e.scalar_tensor_tensor(out=key_f, in0=dst_f, scalar=float(NT), in1=til_f,
                                            op0=ALU.mult, op1=ALU.add))
                d3 = dst_f.rearrange("p (k e) -> p k e", k=KR)
                t3 = til_f.rearrange("p (k e) -> p k e", k=KR)
                m3 = key_f.rearrange("p (k e) -> p k e", k=KR)
                line(e.tensor_scalar(ST[:, 0, 0:KR], d3[:, :, 0], -float(NT), None, ALU.mult))
                line.sync()
                for k in range(KR):
                    line(e.tensor_scalar(t3[:, k, :], m3[:, k, :], ST[:, 0, k:k + 1], None, ALU.add))
                line.sync()
                e.sem_inc(s_rows, 1)
            if sp:
                e.wait_ge(s_in, 16 * n_in)
                e.wait_ge(s_pad, 3)
                e.dma_start(base_d[0:G].rearrange("(k q) -> q k", k=KR),
                            dst_i[0:QG, :].rearrange("p (k e) -> p k e", k=KR)[:, :, 0],
                            allow_slow_non_contiguous=True).then_inc(s_base, 16)
                e.dma_start(base_d[G:G + 1].rearrange("(o n) -> o n", o=1), FL[0:1, 3:4]).then_inc(s_base, 16)
                e.wait_ge(s_base, 32)
                e.dma_start(ST[0:QG, 1, 0:KR].bitcast(I32), base_d[1:G + 1].rearrange("(k q) -> q k", k=KR),
                            allow_slow_non_contiguous=True).then_inc(s_base, 16)
                e.dma_start(FT[0:1, 8:8 + 16 * STEPS].rearrange("o (s g) -> o s g", g=8)[:, :, 0:HG],
                            base_d[0:G].rearrange("(o s g) -> o s g", o=1, g=HG)).then_inc(s_base, 16)
            if dve:
                dense = float(min(256, N // 2))
                d = d3[0:QG]
                flags = SG[0:QG, 0, 0:6 * KR].rearrange("p (k c) -> p k c", c=6)
                nxt = SF[0:QG, 0, 0:KR]
                e.wait_ge(s_base, 64)
                line(e.tensor_copy(nxt, ST[0:QG, 1, 0:KR].bitcast(I32)))
                line(e.memset(FT[0:1, :].rearrange("o (s g) -> o s g", g=8)[:, :, HG:8], 0))
                line(e.memset(FT[0:1, 0:HG], 0))
                line(e.memset(FT[0:1, 8 + 16 * STEPS:8 + 16 * STEPS + HG], 0))
                line(e.memset(SG[0:QG, 0, :], 0.0))
                line(e.memset(SG[0:QG, 1, :], 0.0))
                cmp3 = src_i[0:QG, :].bitcast(F32).rearrange("p (k e) -> p k e", k=KR)
                line(e.tensor_tensor(cmp3[:, :, 0:GE - 1], d[:, :, 0:GE - 1], d[:, :, 1:GE], ALU.is_gt))
                line.sync()
                first, mid = d[:, :, 0], d[:, :, CH]
                for k in range(KR):
                    line(e.tensor_reduce(flags[:, k, 0:1], cmp3[:, k, 0:GE - 1], AX.X, ALU.add))
                line(e.tensor_tensor(flags[:, :, 1], d[:, :, GE - 1], nxt, ALU.is_gt))
                w = [SG[0:QG, 1, c * KR:(c + 1) * KR] for c in range(3)]
                line(e.tensor_tensor(w[0], nxt, first, ALU.subtract))
                line(e.tensor_tensor(w[1], first, mid, ALU.is_equal))
                line(e.tensor_tensor(w[2], mid, nxt, ALU.is_equal))
                line.sync()
                line(e.tensor_scalar(flags[:, :, 2], w[0], float(WIN - 1), None, ALU.is_gt))
                for c, v in ((1, first), (2, mid)):
                    line(e.scalar_tensor_tensor(out=w[c], in0=v, scalar=dense, in1=w[c],
                                                op0=ALU.is_ge, op1=ALU.mult))
                    line.sync()
                    line(e.scalar_tensor_tensor(out=flags[:, :, 2 + c], in0=v, scalar=float(N), in1=w[c],
                                                op0=ALU.is_lt, op1=ALU.mult))
                line(e.tensor_scalar(flags[0:1, 0, 5:6], first[0:1, 0:1], 0.0, None, ALU.is_gt))
                line.sync()
                line(e.tensor_reduce(SF[0:QG, 1, 0:1], SG[0:QG, 0, 0:6 * KR], AX.X, ALU.add))
                line.sync()
                e.sem_inc(s_frow, 1)
                line(e.tensor_copy(IOC, IOP.rearrange("p (n o) -> p n o", o=1).broadcast_to([P, P, HC])))
                e.wait_ge(s_fsum, 1)
                line(e.tensor_scalar(FL[0:1, 0:1], P3[0:1, 0:1], 0.0, None, ALU.is_gt))
                line.sync()
                e.sem_inc(s_flag, 1)

            tables = ((KT, til_f, 2), (PT, src_f, 3), (KGT, key_f, 4))
            if pe:
                e.wait_ge(s_const, 1)
                e.wait_ge(s_rows, 1)
                for n, (_, src, bank) in enumerate(tables):
                    s3 = src.rearrange("p (k h e) -> p k h e", k=KR, h=GC)
                    for h in range(GC):
                        if h:
                            e.wait_ge(s_rowc, 2 * n + 1)
                        for k in range(KR):
                            mm = e.transpose(PS[:, bank, k * QG:(k + 1) * QG], s3[0:QG, k, h, :], IDF[0:QG, 0:QG])
                        mm.then_inc(s_rowt, 1)
                e.wait_ge(s_frow, 1)
                e.matmul(P3[0:1, 0:1], SF[0:QG, 1, 0:1], ONEC[0:QG, :], start=True, stop=True)\
                 .then_inc(s_fsum, 1)
            if act:
                for n, (tab, _, bank) in enumerate(tables):
                    for h in range(GC):
                        e.wait_ge(s_rowt, 2 * n + h + 1)
                        e.copy(tab.rearrange("p (g h) -> p g h", h=GC)[:, :, h], PS[:, bank, 0:G])\
                         .then_inc(s_rowc, 1)

            e.wait_ge(s_flag, 1)
            bad = e.value_load(FL[0:1, 0:1], min_val=0, max_val=1)
            with e.If(bad == 0):
                quick_build(role, e)
            with e.Else():
                if dve:
                    e.memset(FL[0:1, 1:2], 1).then_inc(s_flag2, 1)
            e.wait_ge(s_flag2, 1)
            bad2 = e.value_load(FL[0:1, 1:2], min_val=0, max_val=1)
            with e.If(bad2 == 0):
                layers(role, e, False)
            with e.Else():
                general_build(role, e)
                layers(role, e, True)

        def quick_build(role, e):
            PER = 2 * HC
            if role == "dve":
                line = Line(e, s_bline)
                regs = [e.alloc_register(f"vb{k}") for k in range(8)]

                def source_one_hots(n0, h):
                    e.tensor_tensor(OHP[h], IOC, PTH[:, bass.ds(n0, HC)].rearrange("p (o c) -> p o c", o=1)
                                    .broadcast_to([P, P, HC]), ALU.is_equal).then_inc(s_oh, 1)

                def add_first_column(vals, n0, h, g):
                    n = n0 + g
                    if g == 0:
                        e.wait_ge(s_ohx, (n0 + HG) * GC + RING)
                        e.wait_ge(s_mv, n0 + HG - 1 + 2)
                    e.wait_ge(s_add, n + 2 * HG)
                    to = ADJ[0:PN, :, bass.ds(vals[g], 1)].rearrange("p t o -> p (t o)")
                    e.tensor_tensor(to, to, CPS[h][0:PN, g * NT:(g + 1) * NT], ALU.add).then_inc(s_add, 1)

                def load_bases(i, h):
                    e.load(regs, FT[0:1, bass.ds((i * 2 + h) * 8, 8)])
                    return [e.snap(r, min_val=0, max_val=N) for r in regs]

                def half(i, h, first=False):
                    n0 = i * PER + h * HC
                    for m in range(HC):
                        k = (h * HC + m) % RING
                        e.wait_ge(s_ohx, n0 + m + 1)
                        if m == 0:
                            source_one_hots(n0, h)
                        e.tensor_scalar(OHK[k], IOK, KT[:, bass.ds(n0 + m, 1)], None, ALU.is_equal)\
                         .then_inc(s_oh, 1)
                        if m == 1 and not first:
                            before = load_bases(i, h)
                        if m >= HC - HG and not first:
                            add_first_column(before, i * 2 * HG + (h - 1) * HG, 1 - h, m - (HC - HG))

                e.wait_ge(s_rowc, 6)
                line(e.tensor_copy(PTH[:, 0:NCH], PT))
                line(e.memset(PTH[:, NCH:NCH + HC], 0.0))
                line.sync()
                e.sem_inc(s_ohx, RING)
                e.sem_inc(s_add, 2 * HG)
                half(0, 0, True)
                half(0, 1)
                with e.Fori(1, STEPS) as i:
                    half(i, 0)
                    half(i, 1)
                last = load_bases(STEPS, 0)
                for g in range(HG):
                    add_first_column(last, G - HG, 1, g)
                e.wait_ge(s_add, G + 2 * HG)
                e.wait_ge(s_mv, G + 2)
                line(e.tensor_reduce(TMP[0:PN, 0:1], ADJ[0:PN, :, 0:min(256, N)], AX.XY, ALU.max))
                line.sync()
                line(e.tensor_scalar(TMP[0:PN, 1:2], TMP[0:PN, 0:1], 256.0, None, ALU.is_ge))
                line.sync()
                e.sem_inc(s_frow2, 1)
                e.wait_ge(s_fsum2, 1)
                line(e.tensor_scalar(FL[0:1, 1:2], P3[0:1, 0:1], 0.0, None, ALU.is_gt))
                line.sync()
                e.sem_inc(s_flag2, 1)
            if role == "pe":
                with e.Fori(0, STEPS) as i:
                    for h in range(2):
                        e.wait_ge(s_add, (i * 2 + h + 1) * HG)
                        for m in range(h * HG, (h + 1) * HG):
                            e.wait_ge(s_mv, i * 2 * HG + m + 1)
                            g = m - h * HG
                            for c in range(GC):
                                k = (m * GC + c) % RING
                                e.wait_ge(s_oh, i * (PER + 2) + h + 1 + m * GC + c + 1)
                                first, last = c == 0, c == GC - 1
                                lhs = OHP[h][:, :, g * GC + c]
                                e.matmul(CPS[h][:, g * NT:(g + 1) * NT], lhs, OHK[k][:, 0:NT],
                                         start=first, stop=last)
                                for b in range(2):
                                    lo = NT + b * HALF * NT
                                    mm = e.matmul(WPS[m % 2][:, b, 0:HALF * NT], lhs, OHK[k][:, lo:lo + HALF * NT],
                                                  start=first, stop=last)
                                mm.then_inc(s_ohx, 1)
                e.wait_ge(s_frow2, 1)
                e.matmul(P3[0:1, 0:1], TMP[0:PN, 1:2], ONEC[0:PN, :], start=True, stop=True)\
                 .then_inc(s_fsum2, 1)
            if role == "act":
                regs = [[e.alloc_register(f"ab{h}_{k}") for k in range(8)] for h in range(2)]

                def load_bases(i, h):
                    e.load(regs[h % 2], FT[0:1, bass.ds((i * 2 + h + 1) * 8, 8)])

                e.wait_ge(s_base, 64)
                e.wait_ge(s_const, 1)
                e.sem_inc(s_mv, 2)
                load_bases(0, 0)
                with e.Fori(0, STEPS) as i:
                    for m in range(2 * HG):
                        h, g = divmod(m, HG)
                        n = i * 2 * HG + m
                        if g == 0:
                            vals = [e.snap(r, min_val=0, max_val=N) for r in regs[h]]
                        e.wait_ge(s_ohx, (n + 1) * GC + RING)
                        e.wait_ge(s_mv, n + 2)
                        to = ADJ[0:PN, :, bass.ds(vals[g] + 1, 2 * HALF)]
                        e.copy(to.rearrange("p t (b d) -> p b d t", b=2),
                               WPS[m % 2][0:PN, :, 0:HALF * NT].rearrange("p b (d t) -> p b d t", t=NT))\
                         .then_inc(s_mv, 1)
                        if g == 2:
                            load_bases(i, h + 1)

        def general_build(role, e):
            KV = GW * NT
            ACC = PS[:, 0, 0:KV]
            if role == "dve":
                e.wait_ge(s_rowc, 6)
                line = Line(e, s_gline)
                line(e.memset(WBASE, -float(KV)))
                line(e.memset(ADJ[:, :, :], 0.0))
                e.sem_inc(s_gox, 2)
                e.sem_inc(s_goh, 2)

                def one_hots(w, c, k):
                    e.wait_ge(s_gox, w * NCH + c + 1)
                    e.tensor_scalar(OHK[k][:, 0:KV], IOK[:, 0:KV], WBASE, KGT[:, bass.ds(c, 1)],
                                    ALU.add, ALU.is_equal).then_inc(s_goh, 1)
                    e.tensor_scalar(OHG[k], IOP, PT[:, bass.ds(c, 1)], None, ALU.is_equal).then_inc(s_goh, 1)

                for w in line.loop(GWN, 3):
                    line.sync()
                    e.wait_ge(s_goh, w * 2 * NCH + 2)
                    line(e.tensor_scalar(WBASE, WBASE, float(KV), None, ALU.add))
                    line.sync()
                    e.sem_inc(s_null, 1)
                    with e.Fori(0, NCH // 2) as c:
                        for k in range(2):
                            one_hots(w, c * 2 + k, k)
                    e.wait_ge(s_gox, w * NCH + NCH + 2)
                    e.wait_ge(s_glo, w * 16 + 16)
                    acc = ACC[0:PN].rearrange("p (d t) -> p t d", t=NT)
                    hi = ADJ[0:PN, :, bass.ds(w * GW, GW)]
                    line(e.tensor_copy(hi, acc))
                    line.sync()
                    line(e.tensor_tensor(LOB[0:PN], acc, hi, ALU.subtract))
                line.sync()
            if role == "pe":
                def product(w, c, k, first, last):
                    e.wait_ge(s_goh, (w * NCH + c + 1) * 2 + 2)
                    e.matmul(ACC, OHG[k], OHK[k][:, 0:KV], start=first, stop=last,
                             skip_group_check=True).then_inc(s_gox, 1)

                with e.Fori(0, GWN) as w:
                    e.wait_ge(s_gline, w * 3 + 2)
                    product(w, 0, 0, True, False)
                    with e.Fori(0, NCH // 2 - 1) as c:
                        for k in range(2):
                            product(w, c * 2 + 1 + k, 1 - k, False, False)
                    product(w, NCH - 1, 1, False, True)
            if role == "sp":
                e.sem_inc(s_glo, 16)
                with e.Fori(0, GWN) as w:
                    e.wait_ge(s_gline, w * 3 + 5)
                    e.dma_start(lo_d[0:PN, :, bass.ds(w * GW, GW)], LOB[0:PN]).then_inc(s_glo, 16)
                e.wait_ge(s_glo, 16 * (GWN + 1))

        def remainders(e):
            def bring(tiles0, count, turned):
                with e.Fori(0, count) as l:
                    with e.Fori(0, NT) as j:
                        with e.Fori(0, NT) as t:
                            e.wait_ge(s_lom, (tiles0 + l * NT + j) * NT + t + 1)
                            src = lo_d[0:PN, bass.ds(j, 1), bass.ds(t * PN, P)] if turned else \
                                lo_d[0:PN, bass.ds(t, 1), bass.ds(j * PN, P)]
                            e.dma_start(LOT[0:PN, :], src.rearrange("p o d -> p (o d)")).then_inc(s_lol, 16)

            e.wait_ge(s_glo, 16 * (GWN + 1))
            bring(0, 3 + LAYERS, False)
            e.wait_ge(s_lom, (3 + LAYERS) * NT * NT + 1)
            with e.Fori(0, NT) as t:
                with e.Fori(0, NT) as b:
                    m = t * NT + b
                    blk = lo_d[0:PN, bass.ds(t, 1), bass.ds(b * PN, PN)].rearrange("p o d -> p (o d)")
                    e.dma_start(LOX[0:PN, 0:PN], blk).then_inc(s_lod, 16)
                    e.wait_ge(s_loc, m + 1)
                    e.sem_inc(s_null, 1)
                    e.dma_start(blk, LOT[0:PN, 0:PN]).then_inc(s_lod, 16)
                    e.wait_ge(s_lod, (m + 1) * 32)
            bring((3 + LAYERS) * NT, 4, True)

        def layers(role, e, general):
            pe, act, dve, pool, sp = (role == r for r in ("pe", "act", "dve", "pool", "sp"))
            if pool:
                if general:
                    remainders(e)
                return
            line = Line(e, s_dve1 if dve else s_act1)
            done = lambda s, n: e.wait_ge(s, n + 1)
            settle = lambda: e.sem_inc(s_null, 1)
            lo_at = [0]

            if dve:
                e.wait_ge(s_const, 1)
                diag = ADJ[0:PN].rearrange("p t d -> p (t d)")[:, 0:(NT - 1) * (AW + PN)]\
                    .rearrange("p (t d) -> p t d", t=NT - 1)[:, :, 0:PN]
                ones = IDB[0:PN, 0:PN].rearrange("p (o d) -> p o d", o=1).broadcast_to([PN, NT - 1, PN])
                e.tensor_tensor(diag, diag, ones, ALU.add).then_inc(s_adj, 1)
                last = ADJ[0:PN, NT - 1, (NT - 1) * PN:NT * PN]
                e.tensor_tensor(last, last, IDB[0:PN, 0:PN], ALU.add).then_inc(s_adj, 1)
            if sp:
                e.dma_start(XR[0:PN], a["x"].rearrange("(t p) f -> p t f", p=PN)).then_inc(s_x, 16)

            def stats_of(j):
                return e.bn_stats(LNS[0:PN, bass.ds(j, 1), :].rearrange("p o c -> p (o c)"), tile_of(XR, j))

            def block(b):
                t = slice(b * BT, (b + 1) * BT) if isinstance(b, int) else bass.ds(b * BT, BT)
                return Zn[0:PN, t, :], HP[0:PN, t, 0, 0:P], HP[0:PN, t, 1, 0:P]

            def high_part(E_, b, z=None):
                zb, hi, lo = block(b)
                e.activation(hi, zb if z is None else z, ACT.Copy, scale=1 / LOW).then_inc(E_["hi"], 1)

            def low_part(E_, b, n, z=None):
                done(E_["hi"], n)
                zb, hi, lo = block(b)
                e.scalar_tensor_tensor(out=lo, in0=hi, scalar=-LOW, in1=zb if z is None else z,
                                       op0=ALU.mult, op1=ALU.add).then_inc(E_["hp"], 1)

            def layer_norm(k, ph, weight=None):
                stats, sd, z = s_ln[k]
                E_ = ev[ph]
                if dve:
                    me, ve, mo, vo = (LNS[0:PN, :, c] for c in (1, 2, 4, 5))
                    mean, var = MV[0:PN, :, 0], MV[0:PN, :, 1]
                    line(e.tensor_tensor(mean, me, mo, ALU.add))
                    line(e.tensor_tensor(TMP[0:PN], me, mo, ALU.subtract))
                    line(e.tensor_tensor(var, ve, vo, ALU.add))
                    line.sync()
                    line(e.tensor_tensor(TMP[0:PN], TMP[0:PN], TMP[0:PN], ALU.mult))
                    line(e.tensor_scalar(var, var, 1.0 / P, None, ALU.mult))
                    line.sync()
                    line(e.scalar_tensor_tensor(out=var, in0=TMP[0:PN], scalar=0.25, in1=var, op0=ALU.mult,
                                                op1=ALU.add))
                    line.sync()
                    e.sem_inc(stats, 1)
                    e.wait_ge(sd, 1)
                    line(e.reciprocal(RS[0:PN], SDV[0:PN]))
                    line.sync()
                    if weight is None:
                        line(e.tensor_scalar(RS[0:PN], RS[0:PN], LOW, None, ALU.mult))
                    else:
                        line(e.tensor_tensor(RS[0:PN], RS[0:PN], weight, ALU.mult))
                    line.sync()
                    line(e.scalar_tensor_tensor(out=NBI[0:PN], in0=MV[0:PN, :, 0], scalar=-0.5, in1=RS[0:PN],
                                                op0=ALU.mult, op1=ALU.mult))
                    line.sync()
                    for b in range(NB + 1):
                        if b < NB:
                            for m in range(BT):
                                j = b * BT + m
                                line(e.tensor_scalar(Zn[0:PN, j, :], XR[0:PN, j, :], RS[0:PN, j:j + 1],
                                                     NBI[0:PN, j:j + 1], ALU.mult, ALU.add))
                            line.sync()
                            zb = block(b)[0]
                            e.tensor_scalar(zb, zb, 0.0, None, ALU.max).then_inc(z, 1)
                        if b:
                            low_part(E_, b - 1, b)
                    e.wait_ge(z, NB)
                if act:
                    e.wait_ge(stats, 1)
                    e.activation(SDV[0:PN], MV[0:PN, :, 1], ACT.Sqrt, bias=EPSC[0:PN]).then_inc(sd, 1)
                    for b in range(NB):
                        e.wait_ge(z, b + 1)
                        high_part(E_, b)

            def split(ph, wait_z):
                if act:
                    wait_z()
                    for b in range(NB):
                        high_part(ev[ph], b)
                if dve:
                    wait_z()
                    for b in range(NB):
                        low_part(ev[ph], b, b + 1)

            def extra_column(v):
                hi, lo = HP[0:PN, :, 0, X0], HP[0:PN, :, 1, X0]
                line(e.tensor_copy(hi, v))
                line.sync()
                line(e.tensor_tensor(TMP[0:PN], v, hi, ALU.subtract))
                line.sync()
                line(e.tensor_scalar(lo, TMP[0:PN], LOW, None, ALU.mult))
                line.sync()

            def tiles(ph, base, post, per=None):
                if per:
                    loop = line.loop(HT, 2 * per)
                    for i in loop:
                        for k in range(2):
                            post(i * 2 + k, k, base + i * 2 + k + 1)
                else:
                    with e.Fori(0, HT) as i:
                        for k in range(2):
                            post(i * 2 + k, k, base + i * 2 + k + 1)
                post(NT - 1, 0, base + NT)

            def paired(base, early, late, per_early=0, per_late=0):
                def turns(i):
                    for k in range(2):
                        j = i * 2 + k
                        early(j + 1, 1 - k, base + j + 2)
                        late(j, k, base + j + 1)

                early(0, 0, base + 1)
                if per_early or per_late:
                    for i in line.loop(HT, 2 * (per_early + per_late)):
                        turns(i)
                else:
                    with e.Fori(0, HT) as i:
                        turns(i)
                late(NT - 1, 0, base + NT)

            def aggregate(ph, base, width, turned, hp_base, stages, first_wait):
                E_ = ev[ph]
                spots = {NT * 9 // 20: 0, NT * 14 // 20: 1, NT - 1: 2}
                lo0 = lo_at[0]

                def one(j, k, n, late, first=False):
                    done(E_["red"], n - 2 if not first else base)
                    for t in range(NT):
                        if first and t % BT == 0:
                            done(E_["hp"], hp_base + t // BT + 1)
                        if late is not None and t in spots:
                            stages(*late, spots[t])
                        if turned:
                            lhs = ADJ[0:PN, bass.ds(j, 1), t * PN:t * PN + P].rearrange("p o d -> p (o d)")
                        else:
                            lhs = ADJ[0:PN, t, bass.ds(j * PN, P)]
                        mm = e.matmul(AG[k][:, 0:2 * width], lhs, HP[0:PN, t, :, 0:width], start=(t == 0),
                                      stop=(t == NT - 1), skip_group_check=general)
                    if general:
                        with e.Fori(0, NT) as t:
                            m = (lo0 + base + j) * NT + t
                            e.wait_ge(s_lol, (m + 1) * 16)
                            mm = e.matmul(AG[k][:, 0:2 * width], LOT[0:PN, :],
                                          HP[0:PN, bass.ds(t, 1), :, 0:width].rearrange("p o q f -> p (o q) f"),
                                          start=False, stop=True, skip_group_check=True)
                            mm.then_inc(s_lom, 1)
                        e.wait_ge(s_lom, (lo0 + base + j + 1) * NT + 1)
                        e.sem_inc(E_["agg"], 1)
                    else:
                        mm.then_inc(E_["agg"], 1)

                first_wait()
                one(0, 0, base + 1, None, True)
                with e.Fori(0, HT) as i:
                    for k in range(2):
                        one(i * 2 + k + 1, 1 - k, base + i * 2 + k + 2, (i * 2 + k, k, base + i * 2 + k + 1))
                for q in range(3):
                    stages(NT - 1, 0, base + NT, q)

            def tile_of(X, j):
                return X[0:PN, bass.ds(j, 1), :].rearrange("p o f -> p (o f)")

            def parts_sum(E_, k, n, to, width=P):
                done(E_["agg"], n)
                to = to[:, 0:width]
                line(e.tensor_scalar(to, AG[k][0:PN, width:2 * width], 1 / LOW, None, ALU.mult))
                line.sync()
                return e.tensor_tensor(to, to, AG[k][0:PN, 0:width], ALU.add)

            def di(j):
                return DI[0:PN, bass.ds(j, 1)]

            def z_of(j):
                return Zf[0:PN, bass.ds(j * P, P)]

            s0w, s1w = ST[0:PN, 0, :], ST[0:PN, 1, :]
            s0, s1 = s0w[:, 0:P], s1w[:, 0:P]

            E0 = ev["L0"]
            if dve:
                e.wait_ge(s_w, 16 * N_CONST)
                line(e.tensor_scalar(EPSL, EPS0, 1 / LOW, None, ALU.mult))
                line(e.memset(CF, 1.0))
                line(e.memset(HP[0:PN, :, 0, X0], 1.0))
                line(e.memset(HP[0:PN, :, 1, X0], 0.0))
                line.sync()
                e.sem_inc(s_ones, 1)
                e.wait_ge(s_x, 16)
                for b in line.loop(NB, BT):
                    for m in range(BT):
                        line(stats_of(b * BT + m))
                line.sync()
            layer_norm(0, "L0")
            if dve:

                def post(j, k, n):
                    line(parts_sum(E0, k, n, s1w, X0 + 1))
                    line.sync()
                    line(e.tensor_copy(DEG[0:PN, bass.ds(j, 1)], s1w[:, X0:X0 + 1]))
                    line.sync()
                    done(E0["tr"], n - 1)
                    e.scalar_tensor_tensor(out=s0, in0=z_of(j), scalar=EPSL[0:PN], in1=s1, op0=ALU.mult,
                                           op1=ALU.add).then_inc(E0["red"], 1)

                def late(j, k, n):
                    done(E0["d2"], n)
                    done(E0["red"], n if isinstance(j, int) else n + 1)
                    line(e.tensor_tensor(s1, P2[0:PN, 0:P], BB[0:PN, :], ALU.add))
                    line.sync()
                    line(e.tensor_scalar(z_of(j), s1, 0.0, None, ALU.max))
                    line.sync()
                    e.tensor_reduce(MX[0:PN, bass.ds(j, 1)], z_of(j), AX.X, ALU.max, negate=True)\
                     .then_inc(E0["z"], 1)
                    line(e.tensor_tensor(tile_of(XR, j), tile_of(XR, j), z_of(j), ALU.add))
                    line.sync()
                    line(stats_of(j))
                paired(0, post, late, 3, 4)
                line.sync()
            if act:
                e.wait_ge(s_w, 16 * N_CONST)

                def post(j, k, n):
                    done(E0["tr"], n)
                    e.copy(SF[:, 0, 0:PN], TP[:, 0:PN]).then_inc(E0["cf"], 1)
                    done(E0["d1"], n)
                    done(E0["d2"], n - 1)
                    for m in range(2):
                        e.activation(SG[:, m, 0:PN], P1[:, m * P:m * P + PN], ACT.Relu, bias=B_L0[:, m:m + 1])\
                         .then_inc(E0["rg"], 1)

                def late(j, k, n):
                    done(E0["z"], n)
                    e.wait_ge(E0["ex"], n)
                    settle()
                    e.activation(SF[0:PN, 1, :], z_of(j), ACT.Exp, bias=MX[0:PN, bass.ds(j, 1)],
                                 accum_out=SE[0:PN, bass.ds(j, 1)]).then_inc(E0["ex"], 1)
                paired(0, post, late)
            if pe:
                def stages(j, k, n, q):
                    if q == 0:
                        done(E0["red"], n)
                        e.transpose(TP[:, 0:PN], s0, IDF[0:PN, 0:PN]).then_inc(E0["tr"], 1)
                    if q == 1:
                        done(E0["cf"], n)
                        for m in range(2):
                            mm = e.matmul(P1[:, m * P:m * P + PN], WB[:, m * P:(m + 1) * P], SF[:, 0, 0:PN],
                                          start=True, stop=True)
                        mm.then_inc(E0["d1"], 1)
                    if q == 2:
                        done(E0["rg"], n * 2)
                        done(E0["z"], n - 1)
                        for m in range(2):
                            mm = e.matmul(P2[0:PN, 0:P], SG[:, m, 0:PN], WB[:, (2 + m) * P:(3 + m) * P],
                                          start=(m == 0), stop=(m == 1))
                        mm.then_inc(E0["d2"], 1)

                def first():
                    e.wait_ge(s_adj, 2)
                    e.wait_ge(s_ones, 1)
                    e.wait_ge(s_w, 16 * N_CONST)
                aggregate("L0", 0, X0 + 1, False, 0, stages, first)
            lo_at[0] += NT

            if act:
                done(E0["z"], NT)
                e.activation(SDV[0:PN], DEG[0:PN], ACT.Sqrt).then_inc(s_soft, 1)
                e.wait_ge(E0["ex"], NT + 1)
            if dve:
                e.wait_ge(s_soft, 1)
                line(e.reciprocal(DI[0:PN], SDV[0:PN]))
                line(e.tensor_scalar(DEG[0:PN], SDV[0:PN], 1 / LOW, None, ALU.mult))
                line.sync()
                line(e.tensor_scalar(DIL[0:PN], DI[0:PN], LOW, None, ALU.mult))
                line.sync()
            if sp:
                done(E0["d2"], NT)
                e.dma_start(WB[:, 0:P], a["L1_gnn_W1"]).then_inc(s_w, 16)
                e.dma_start(WB[:, P:2 * P], a["L1_gnn_W2"]).then_inc(s_w, 16)
                e.wait_ge(s_soft, 1)
                done(E0["z"], NT)
                e.dma_start(BB[:, :], bcast(a["L1_gnn_b2"])).then_inc(s_w, 16)
            n_w1 = N_CONST + 3

            if dve:
                e.wait_ge(E0["ex"], NT + 1)
            layer_norm(1, "L1a", DIL[0:PN])
            E1 = ev["L1a"]

            def scale_from_bound(row, inv):
                line(e.tensor_scalar(inv, row, 1 / TOP, 1e-30, ALU.mult, ALU.max))
                line.sync()
                line(e.reciprocal(row, inv))
                line.sync()

            def absolute(to, v):
                line(e.scalar_tensor_tensor(out=to, in0=v, scalar=-1.0, in1=v, op0=ALU.mult, op1=ALU.max))

            if dve:
                e.wait_ge(s_w, 16 * n_w1)
                far = (E + 1.0) ** 0.5 * P ** 0.5
                absw = SG[:, 1, :]
                absolute(absw, WB[:, 0:P])
                line.sync()
                e.sem_inc(s_sc[0], 1)
                absolute(BND[:, 1:2], B_L1[:, :])
                line.sync()
                e.wait_ge(s_sc[1], 1)
                line(e.scalar_tensor_tensor(out=BND[:, 0:1], in0=P3[:, 0:1], scalar=far, in1=BND[:, 1:2],
                                            op0=ALU.mult, op1=ALU.add))
                absolute(absw, WB[:, P:2 * P])
                line.sync()
                line(e.tensor_copy(SF[:, 1, :], BND[:, 0:1].broadcast_to([P, P])))
                line.sync()
                e.sem_inc(s_sc[2], 1)
                e.wait_ge(s_sc[3], 1)
                line(e.tensor_copy(SF[:, 1, :], P3[:, 0:P]))
                line.sync()
                scale_from_bound(SF[:, 1, :], INV[:, :])
                line(e.tensor_tensor(WB[:, P:2 * P], WB[:, P:2 * P], SF[:, 1, :], ALU.mult))
                line.sync()
                line(e.tensor_scalar(WB[:, P:2 * P], WB[:, P:2 * P], LOW, None, ALU.mult))
                line.sync()
                e.sem_inc(s_sc[4], 1)
                e.wait_ge(s_soft, 2)
                line(e.tensor_tensor(TMP[0:PN], MX[0:PN], SE[0:PN], ALU.subtract))
                line.sync()
                line(e.tensor_tensor(XR[0:PN], XR[0:PN], TMP[0:PN].rearrange("p (t o) -> p t o", o=1)
                                     .broadcast_to([PN, NT, P]), ALU.add))
                line.sync()
            if pe:
                e.wait_ge(s_sc[0], 1)
                e.matmul(P3[:, 0:1], SG[:, 1, :], ONEC, start=True, stop=True).then_inc(s_sc[1], 1)
                e.wait_ge(s_sc[2], 1)
                e.matmul(P3[:, 0:P], SF[:, 1, :], SG[:, 1, :], start=True, stop=True).then_inc(s_sc[3], 1)
            if act:
                e.activation(SE[0:PN], SE[0:PN], ACT.Ln).then_inc(s_soft, 1)
            if dve:
                def post(j, k, n):
                    line(parts_sum(E1, k, n, s1))
                    line.sync()
                    done(E1["tr"], n - 1)
                    e.tensor_scalar(s0, s1, di(j), None, ALU.mult).then_inc(E1["red"], 1)

                def late(j, k, n):
                    done(E1["d2"], n)
                    e.tensor_scalar(z_of(j), P2[0:PN, 0:P], di(j), None, ALU.mult).then_inc(E1["z"], 1)
                paired(0, post, late, 2, 0)
            if act:
                def post(j, k, n):
                    done(E1["tr"], n)
                    e.copy(SF[:, 0, 0:PN], TP[:, 0:PN]).then_inc(E1["cf"], 1)
                    done(E1["d1"], n)
                    done(E1["d2"], n - 1)
                    e.activation(SG[:, 0, 0:PN], P1[:, 0:PN], ACT.Relu, bias=B_L1[:, :]).then_inc(E1["rg"], 1)
                tiles("L1a", 0, post)
            if pe:
                def stages(j, k, n, q):
                    if q == 0:
                        done(E1["red"], n)
                        e.transpose(TP[:, 0:PN], s0, IDF[0:PN, 0:PN]).then_inc(E1["tr"], 1)
                    if q == 1:
                        done(E1["cf"], n)
                        e.matmul(P1[:, 0:PN], WB[:, 0:P], SF[:, 0, 0:PN], start=True, stop=True)\
                         .then_inc(E1["d1"], 1)
                    if q == 2:
                        done(E1["rg"], n)
                        done(E1["z"], n - 1)
                        e.matmul(P2[0:PN, 0:P], SG[:, 0, 0:PN], WB[:, P:2 * P], start=True, stop=True)\
                         .then_inc(E1["d2"], 1)
                aggregate("L1a", 0, P, False, 0, stages, lambda: e.wait_ge(s_sc[4], 1))
            lo_at[0] += NT

            E1b = ev["L1b"]
            split("L1b", lambda: done(E1["z"], NT))
            if dve:
                def post(j, k, n):
                    parts_sum(E1b, k, n, s1).then_inc(E1b["red"], 1)
                    done(E1b["red"], n)
                    xj = tile_of(XR, j)
                    line(e.scalar_tensor_tensor(out=s0, in0=s1, scalar=di(j), in1=INV[0:PN], op0=ALU.mult,
                                                op1=ALU.mult))
                    line(e.tensor_tensor(xj, xj, BB[0:PN, :], ALU.add))
                    line.sync()
                    line(e.tensor_tensor(xj, xj, s0, ALU.add))
                    line.sync()
                    line(stats_of(j))
                tiles("L1b", 0, post, 5)
                line.sync()
            if pe:
                aggregate("L1b", 0, P, False, 0, lambda *_: None, lambda: None)
            lo_at[0] += NT

            E2 = ev["L2"]
            layer_norm(2, "L2")
            if sp:
                done(E1["d2"], NT)
                with e.Fori(0, LAYERS) as l:
                    done(s_bn["w"], l)
                    e.dma_start(WB[:, 0:P], a["L2_gnn_W1"][bass.ds(l, 1)].rearrange("o p n -> (o p) n"))\
                     .then_inc(s_wt, 16)
                    e.dma_start(WB[:, P:2 * P], a["L2_gnn_W2"][bass.ds(l, 1)].rearrange("o p n -> (o p) n"))\
                     .then_inc(s_wt, 16)

            def bias2(q, l):
                return B_L2[:, q, bass.ds(l, 1)]

            def zc_of(j):
                return Zf[:, bass.ds(j * PN, PN)]

            def turned_block(b):
                return RB[b % 2][0:PN, 0:BT * P].rearrange("p (t f) -> p t f", f=P)

            if dve:
                absolute(SDV[:, 0:LAYERS], B_L2[:, Q_GA, :])
                absolute(RS[:, 0:LAYERS], B_L2[:, Q_BE, :])
                line.sync()
                line(e.scalar_tensor_tensor(out=SDV[:, 0:LAYERS], in0=SDV[:, 0:LAYERS], scalar=N ** 0.5,
                                            in1=RS[:, 0:LAYERS], op0=ALU.mult, op1=ALU.add))
                line.sync()
                line(e.tensor_scalar(SDV[:, 0:LAYERS], SDV[:, 0:LAYERS], 1 / TOP, 1e-30, ALU.mult, ALU.max))
                line.sync()
                line(e.reciprocal(RS[:, 0:LAYERS], SDV[:, 0:LAYERS]))
                line.sync()
                line(e.tensor_scalar(RS[:, 0:LAYERS], RS[:, 0:LAYERS], LOW, None, ALU.mult))
                line.sync()

            def layer2(l, last):
                base = l * NT
                if dve:
                    done(E2["hp"], (l + 1) * NB)
                    settle()

                    def post(j, k, n):
                        done(E2["tr"], n - 1)
                        parts_sum(E2, k, n, s0).then_inc(E2["red"], 1)

                    def late(j, k, n):
                        done(E2["d2"], n)
                        e.tensor_scalar(zc_of(j), P2[:, 0:PN], bias2(Q_B2, l), None, ALU.add)\
                         .then_inc(E2["z"], 1)
                        done(E2["z"], n)
                        line(e.bn_stats(STATS[:, 0, bass.ds(j, 1), :].rearrange("p o c -> p (o c)"), zc_of(j)))
                        line.sync()
                    paired(base, post, late, 1, 1)
                    settle()
                    line(e.bn_aggr(BNM, STATS[:, 0, :, :].rearrange("p t c -> p (t c)")))
                    line.sync()
                    e.sem_inc(s_bn["var"], 1)
                    e.wait_ge(s_bn["sd"], l + 1)
                    line(e.reciprocal(BNR, BNS))
                    line.sync()
                    line(e.tensor_tensor(BNA[:, 0:1], BNR, bias2(Q_GA, l), ALU.mult))
                    line.sync()
                    line(e.tensor_tensor(BNT, BNM[:, 0:1], BNA[:, 0:1], ALU.mult))
                    line.sync()
                    line(e.tensor_tensor(BNB[:, 0:1], bias2(Q_BE, l), BNT, ALU.subtract))
                    line.sync()
                    if not last:
                        up = RS[:, bass.ds(l, 1)]
                        line(e.tensor_tensor(BNA[:, 0:1], BNA[:, 0:1], up, ALU.mult))
                        line(e.tensor_tensor(BNB[:, 0:1], BNB[:, 0:1], up, ALU.mult))
                        line(e.tensor_copy(CF, SDV[:, bass.ds(l, 1)]))
                        line.sync()
                    e.sem_inc(s_bn["ab"], 1)
                    for b in range(NB):
                        n = (l + 1) * NB + b + 1
                        if last:
                            e.wait_ge(s_bn["tr"], n - NB)
                            xb = XR[0:PN, b * BT:(b + 1) * BT, :]
                            line(e.tensor_tensor(xb, xb, turned_block(b), ALU.add))
                            line.sync()
                            e.sem_inc(E2["hp"], 1)
                            for m in range(BT):
                                line(stats_of(b * BT + m))
                        else:
                            low_part(E2, b, n, turned_block(b))
                    if last:
                        line.sync()
                if act:
                    def post(j, k, n):
                        done(E2["tr"], n)
                        e.activation(SF[:, 0, 0:PN], TP[:, 0:PN], ACT.Copy, scale=CF).then_inc(E2["cf"], 1)
                        done(E2["d1"], n)
                        done(E2["d2"], n - 1)
                        settle()
                        e.activation(SG[:, 0, 0:PN], P1[:, 0:PN], ACT.Relu, bias=bias2(Q_B1, l))\
                         .then_inc(E2["rg"], 1)
                    tiles("L2", base, post)
                    e.wait_ge(s_bn["var"], l + 1)
                    e.activation(BNS, BNM[:, 1:2], ACT.Sqrt, bias=EPSC).then_inc(s_bn["sd"], 1)
                    e.wait_ge(s_bn["ab"], l + 1)

                    def relu(b):
                        zb = Zf[:, b * BT * PN:(b + 1) * BT * PN]
                        e.activation(zb, zb, ACT.Relu, bias=BNB[:, 0:1], scale=BNA[:, 0:1]).then_inc(s_bn["rel"], 1)

                    relu(0)
                    for b in range(NB):
                        if b + 1 < NB:
                            relu(b + 1)
                        if not last:
                            e.wait_ge(s_bn["tr"], l * NB + b + 1)
                            high_part(E2, b, turned_block(b))
                if pe:
                    def stages(j, k, n, q):
                        if q == 0:
                            done(E2["red"], n)
                            e.transpose(TP[:, 0:PN], s0, IDF[0:PN, 0:PN]).then_inc(E2["tr"], 1)
                        if q == 1:
                            done(E2["cf"], n)
                            e.matmul(P1[:, 0:PN], WB[:, 0:P], SF[:, 0, 0:PN], start=True, stop=True)\
                             .then_inc(E2["d1"], 1)
                        if q == 2:
                            done(E2["rg"], n)
                            done(E2["z"], n - 1)
                            e.matmul(P2[:, 0:PN], WB[:, P:2 * P], SG[:, 0, 0:PN], start=True, stop=True)\
                             .then_inc(E2["d2"], 1)
                    aggregate("L2", base, P, False, l * NB, stages,
                              lambda: e.wait_ge(s_wt, (l + 1) * 32))
                    e.wait_ge(E2["d2"], (l + 1) * NT + 1)
                    e.sem_inc(s_bn["w"], 1)
                    for b in range(NB):
                        e.wait_ge(s_bn["rel"], l * NB + b + 1)
                        if b >= 2:
                            done(E2["hp"], (l + 1) * NB + b - 1)
                        for m in range(BT):
                            c = (b * BT + m) * PN
                            mm = e.transpose(RB[b % 2][0:PN, m * P:(m + 1) * P], Zf[:, c:c + PN], IDF[:, :])
                        mm.then_inc(s_bn["tr"], 1)

            if dve:
                for l in line.loop(LAYERS - 1, 2 * NT + 8):
                    layer2(l, False)
            elif act or pe:
                with e.Fori(0, LAYERS - 1) as l:
                    layer2(l, False)
            layer2(LAYERS - 1, True)
            lo_at[0] += NT * LAYERS

            TB = [(q * NT // 4, (q + 1) * NT // 4) for q in range(4)]
            banks = [PS[:, q, :].bitcast(BF16) for q in range(4)]
            PB = P
            if general and pe:
                with e.Fori(0, NT * NT) as m:
                    e.wait_ge(s_lod, m * 32 + 16)
                    e.transpose(banks[0][0:PN, 0:PN], LOX[0:PN, 0:PN], IDB[0:PN, 0:PN]).then_inc(s_lox, 1)
            if general and dve:
                with e.Fori(0, NT * NT) as m:
                    e.wait_ge(s_lox, m + 1)
                    e.tensor_copy(LOT[0:PN, 0:PN], banks[0][0:PN, 0:PN]).then_inc(s_loc, 1)
            if general and pe:
                e.wait_ge(s_loc, NT * NT)
            if pe:
                with e.Fori(0, NT) as t:
                    for q, (b0, b1) in enumerate(TB):
                        done(s_at["dve" if q % 2 else "act"], t * 2)
                        for b in range(b0, b1):
                            mm = e.transpose(banks[q][0:PN, (b - b0) * PB:(b - b0) * PB + PN],
                                             ADJ[0:PN, bass.ds(t, 1), b * PN:(b + 1) * PN]
                                             .rearrange("p o d -> p (o d)"), IDB[0:PN, 0:PN])
                        mm.then_inc(s_at["tr"], 1)
            if act or dve:
                layer_norm(3, "L3a", DIL[0:PN])
                with e.Fori(0, NT) as t:
                    for q, (b0, b1) in enumerate(TB):
                        if (q % 2 == 1) != dve:
                            continue
                        e.wait_ge(s_at["tr"], t * 4 + q + 1)
                        to = ADJ[0:PN, bass.ds(t, 1), b0 * PN:b1 * PN].rearrange("p o (b d) -> p (o b) d", d=PN)
                        fr = banks[q][0:PN, 0:(b1 - b0) * PB].rearrange("p (b d) -> p b d", d=PB)[:, :, 0:PN]
                        (e.tensor_copy if dve else e.copy)(to, fr).then_inc(s_at["dve" if dve else "act"], 1)

            Y = lambda q: y_d[q]
            E3, E3b = ev["L3a"], ev["L3b"]
            if sp:
                done(E2["d2"], NT * LAYERS)
                e.dma_start(WB[:, 0:3 * P].rearrange("p (q n) -> p q n", q=3),
                            a["L3_gnn_l1_w"].rearrange("q p n -> p q n")).then_inc(s_wt, 16)
                e.wait_ge(s_ln[3][0], 1)
                e.dma_start(BB[0:1, :], a["L3_gnn_l1_b"][1:2]).then_inc(s_wt, 16)

                def post(j, k, n):
                    e.wait_ge(E3["z"], n * 2 + 1)
                    e.dma_start(y_d[1][:, bass.ds(j * PN, PN)], SG[:, 0, 0:PN]).then_inc(s_y, 16)
                    e.dma_start(y_d[0][:, bass.ds(j * PN, PN)], SG[:, 1, 0:PN]).then_inc(s_y, 16)
                tiles("L3a", 0, post)
                e.wait_ge(E3["d1"], NT + 1)
                e.dma_start(BB[0:1, :], a["L3_gnn_l1_b"][2:3]).then_inc(s_wt, 16)

                def post(j, k, n):
                    e.wait_ge(E3b["z"], n + 1)
                    e.dma_start(y_d[2][:, bass.ds(j * PN, PN)], SG[:, 0, 0:PN]).then_inc(s_y, 16)
                tiles("L3b", 0, post)
            wt0 = 32 * LAYERS

            def mix_dve(E_, first):
                yb = 0 if first else 32 * NT

                def early(j, k, n):
                    done(E_["tr"], n - 1)
                    if first:
                        line(e.tensor_scalar(s1, z_of(j), DEG[0:PN, bass.ds(j, 1)], None, ALU.mult))
                    line(parts_sum(E_, k, n, s0w, X0 + 1))
                    line.sync()
                    line(e.tensor_scalar(s0w[:, 0:X0 + 1], s0w[:, 0:X0 + 1], di(j), None if first else SPREAD,
                                         ALU.mult, *(() if first else (ALU.mult,))))
                    line.sync()
                    line(e.tensor_copy(RC[0:PN], s0w[:, X0:X0 + 1]))
                    if first:
                        line(e.tensor_scalar(z_of(j), s0, di(j), LOW / SPREAD, ALU.mult, ALU.mult))
                        line(e.tensor_scalar(TMP[0:PN, bass.ds(j, 1)], s0w[:, X0:X0 + 1], di(j), 1 / SPREAD,
                                             ALU.mult, ALU.mult))
                    line.sync()
                    e.sem_inc(E_["red"], 1)

                def late(j, k, n):
                    done(E_["d1"], n)
                    done(s_y, yb + (n - 1) * (32 if first else 16))
                    outs = ((0, P1[:, 0:PN], None, 1), (1, P1[:, P:P + PN], B_L3[:, R_B1, 0:1], 0)) if first else \
                           ((0, P1[:, 0:PN], None, 2),)
                    for r, src, bias, q in outs:
                        if bias is None:
                            line(e.tensor_copy(SG[:, r, 0:PN], src))
                        else:
                            line(e.tensor_scalar(SG[:, r, 0:PN], src, bias, None, ALU.add))
                    line.sync()
                    for r, src, bias, q in outs:
                        e.bn_stats(STATS[:, q, bass.ds(j, 1), :].rearrange("p o c -> p (o c)"), SG[:, r, 0:PN])\
                         .then_inc(E_["z"], 1)
                return early, late, 7 if first else 4, 2 if first else 1

            def mix_act(E_, first):
                def post(j, k, n):
                    done(E_["tr"], n)
                    done(E_["d1"], n - 1)
                    e.copy(SF[:, 0, 0:PN], TP[:, 0:PN]).then_inc(E_["cf"], 1)
                    if first:
                        e.copy(SF[:, 1, 0:PN], TP[:, P:P + PN]).then_inc(E_["cf"], 1)
                    e.copy(ROW[0:1, 0:PN], TP[0:1, 2 * P:2 * P + PN]).then_inc(E_["cf"], 1)
                return post

            def mix_pe(E_, first, wq):
                per = 3 if first else 2

                def stages(j, k, n, q):
                    if q == 0:
                        done(E_["red"], n)
                        e.transpose(TP[:, 0:PN], s0, IDF[0:PN, 0:PN])
                        if first:
                            e.transpose(TP[:, P:P + PN], s1, IDF[0:PN, 0:PN])
                        e.matmul(TP[0:1, 2 * P:2 * P + PN], RC[0:PN], IDF[0:PN, 0:PN], start=True, stop=True)\
                         .then_inc(E_["tr"], 1)
                    if q == 2:
                        done(E_["cf"], n * per)
                        done(E_["z"], (n - 1) * (per - 1))
                        e.matmul(P1[:, 0:PN], WB[:, wq * P:(wq + 1) * P], SF[:, 0, 0:PN], start=True, stop=False)
                        mm = e.matmul(P1[:, 0:PN], BB[0:1, :], ROW[0:1, 0:PN], start=False, stop=True)
                        if first:
                            mm = e.matmul(P1[:, P:P + PN], WB[:, 0:P], SF[:, 1, 0:PN], start=True, stop=True)
                        mm.then_inc(E_["d1"], 1)
                return stages

            if dve:
                extra_column(DI[0:PN])
                e.sem_inc(s_rt, 1)
                paired(0, *mix_dve(E3, True))
            if act:
                tiles("L3a", 0, mix_act(E3, True))
            if pe:
                def first():
                    e.wait_ge(s_at["act"], 2 * NT + 1)
                    e.wait_ge(s_at["dve"], 2 * NT + 1)
                    e.wait_ge(s_rt, 1)
                    e.wait_ge(s_wt, wt0 + 32)
                aggregate("L3a", 0, X0 + 1, True, 0, mix_pe(E3, True, 1), first)
            lo_at[0] += NT
            if dve:
                done(E3["z"], 2 * NT)
            split("L3b", lambda: done(E3["z"], 2 * NT))
            if dve:
                line(e.tensor_copy(MX[0:PN], TMP[0:PN]))
                line.sync()
                extra_column(MX[0:PN])
                e.sem_inc(s_rt, 1)
                paired(0, *mix_dve(E3b, False))
            if act:
                tiles("L3b", 0, mix_act(E3b, False))
            if pe:
                def first():
                    e.wait_ge(s_rt, 2)
                    e.wait_ge(s_wt, wt0 + 48)
                aggregate("L3b", 0, X0 + 1, True, 0, mix_pe(E3b, False, 2), first)
            lo_at[0] += NT

            VW = HPf[:, 0:9 * P]
            FP = HPf[:, 9 * P:12 * P]
            CB = HPf[:, 12 * P:15 * P]
            YT = [HPf[:, (15 + 3 * k) * P:(18 + 3 * k) * P].rearrange("p (q n) -> p q n", q=3) for k in range(2)]
            Q1T = [HPf[:, (21 + k) * P:(22 + k) * P] for k in range(2)]
            FB = HPf[:, 23 * P:24 * P]
            BR, VA, CA = Zf[:, 0:3 * P], Zf[:, 3 * P:9 * P], Zf[:, 9 * P:11 * P]
            L2R = Zf[:, 0:9 * P].rearrange("p (j g n) -> p j g n", j=3, g=3)
            L2T = Zf[:, 9 * P:18 * P].rearrange("p (j g n) -> p j g n", j=3, g=3)
            BBR = Zf[:, 18 * P:21 * P]
            if sp:
                done(E3b["agg"], NT)
                e.dma_start(FP.rearrange("p (j n) -> p j n", j=3),
                            a["L3_gnn_fp_w"].rearrange("(j p) n -> p j n", p=P)).then_inc(s_vw, 16)
                e.dma_start(FB, bcast(a["L3_gnn_fp_b"])).then_inc(s_vw, 16)
                for j in range(3):
                    e.dma_start(L2R[:, j], a["L3_gnn_l2_w"][j].rearrange("(g p) n -> p g n", p=P))\
                     .then_inc(s_vw, 16)
            if pe:
                e.wait_ge(s_vw, 80)
                done(E3b["z"], NT)
                for j in range(3):
                    for g in range(3):
                        mm = e.transpose(PS[:, j, g * P:(g + 1) * P], L2R[:, j, g, :], IDF[:, :])
                    mm.then_inc(s_vt, 1)
                for j in range(3):
                    e.wait_ge(s_vc, j + 1)
                    for g in range(3):
                        e.matmul(PS[:, 3 + j, g * P:(g + 1) * P], L2T[:, j, g, :], FP[:, j * P:(j + 1) * P],
                                 start=True, stop=True)
                    e.matmul(PS[:, 3 + j, 3 * P:4 * P], BBR[:, j * P:(j + 1) * P], FP[:, j * P:(j + 1) * P],
                             start=True, stop=True).then_inc(s_vm, 1)
            if act:
                for j in range(3):
                    e.wait_ge(s_vt, j + 1)
                    line(e.copy(L2T[:, j].rearrange("p g n -> p (g n)"), PS[:, j, 0:3 * P]))
                    line(e.activation(BBR[:, j * P:(j + 1) * P], IDF[:, :], ACT.Identity,
                                      bias=B_L3[:, R_B2, j:j + 1], scale=0.0))
                    line.sync()
                    e.sem_inc(s_vc, 1)
                for j in range(3):
                    e.wait_ge(s_vm, j + 1)
                    e.copy(VW.rearrange("p (g j n) -> p g j n", g=3, j=3)[:, :, j, :],
                           PS[:, 3 + j, 0:3 * P].rearrange("p (g n) -> p g n", g=3)).then_inc(s_vv, 1)
                    e.copy(CB[:, j * P:(j + 1) * P], PS[:, 3 + j, 3 * P:4 * P]).then_inc(s_vv, 1)
            if dve:
                for q in range(3):
                    done(E3b["z"], NT)
                    done(E3["z"], 2 * NT)
                    line(e.bn_aggr(BNM, STATS[:, q, :, :].rearrange("p t c -> p (t c)")))
                    line.sync()
                    e.sem_inc(s_bn["var"], 1)
                    e.wait_ge(s_bn["sd"], LAYERS + q + 1)
                    line(e.reciprocal(BNR, BNS))
                    line.sync()
                    line(e.tensor_tensor(BNA[:, q:q + 1], BNR, B_L3[:, R_GA, q:q + 1], ALU.mult))
                    line.sync()
                    line(e.tensor_tensor(BNT, BNM[:, 0:1], BNA[:, q:q + 1], ALU.mult))
                    line.sync()
                    line(e.tensor_tensor(BNB[:, q:q + 1], B_L3[:, R_BE, q:q + 1], BNT, ALU.subtract))
                    line.sync()
                e.sem_inc(s_bn["ab"], 1)
                absolute(BND, B_L3[:, R_GA, :])
                absolute(BND2, B_L3[:, R_BE, :])
                line.sync()
                line(e.scalar_tensor_tensor(out=BND, in0=BND, scalar=N ** 0.5, in1=BND2, op0=ALU.mult, op1=ALU.add))
                line.sync()
                for g in range(3):
                    line(e.tensor_copy(BR[:, g * P:(g + 1) * P], BND[:, g:g + 1].broadcast_to([P, P])))
                e.wait_ge(s_vv, 6)
                far = float(E + N)
                va, vw, ca, cb = (v.rearrange("p (g j n) -> p g j n", g=g, j=j) for v, g, j in
                                  ((VA, 3, 2), (VW, 3, 3), (CA, 1, 2), (CB, 1, 3)))
                absolute(va, vw[:, :, 1:3, :])
                absolute(ca, cb[:, :, 1:3, :])
                line(e.tensor_tensor(CB[:, 0:P], CB[:, 0:P], FB, ALU.add))
                line.sync()
                line(e.tensor_scalar(va[:, :, 1, :], va[:, :, 1, :], far, None, ALU.mult))
                line(e.scalar_tensor_tensor(out=CA[:, 0:P], in0=CA[:, P:2 * P], scalar=far, in1=CA[:, 0:P],
                                            op0=ALU.mult, op1=ALU.add))
                line.sync()
                e.sem_inc(s_sc[5], 1)
                line.sync()
                e.wait_ge(s_sc[3], 2)
                line(e.tensor_tensor(CA[:, 0:P], CA[:, 0:P], P3[:, 0:P], ALU.add))
                line.sync()
                scale_from_bound(CA[:, 0:P], INV[:, :])
                cb = CB[:, P:3 * P].rearrange("p (j n) -> p j n", j=2)
                scale = CA[:, 0:P].rearrange("p (o n) -> p o n", o=1).broadcast_to([P, 2, P])
                line(e.tensor_tensor(cb, cb, scale, ALU.mult))
                for g in range(3):
                    vw = VW[:, (g * 3 + 1) * P:(g * 3 + 3) * P].rearrange("p (j n) -> p j n", j=2)
                    line(e.tensor_tensor(vw, vw, scale, ALU.mult))
                line.sync()
                e.sem_inc(s_sc[4], 1)
            if act:
                for q in range(3):
                    e.wait_ge(s_bn["var"], LAYERS + q + 1)
                    e.activation(BNS, BNM[:, 1:2], ACT.Sqrt, bias=EPSC).then_inc(s_bn["sd"], 1)
                e.wait_ge(s_bn["ab"], LAYERS + 1)
            if sp:
                e.wait_ge(s_y, 1 + 48 * NT)
                e.wait_ge(s_vv, 6)
                for j in range(2):
                    e.dma_start(YT[j][:, :, 0:PN], y_d[:, :, j * PN:(j + 1) * PN].rearrange("q p n -> p q n"))\
                     .then_inc(s_yl[j], 16)

                def store(j, k, n, more=True):
                    if more:
                        done(s_vq, n)
                        e.dma_start(YT[k][:, :, 0:PN],
                                    y_d[:, :, bass.ds((j + 2) * PN, PN)].rearrange("q p n -> p q n"))\
                         .then_inc(s_yl[k], 16)
                    done(s_vd, n)
                    e.dma_start(q1_d[bass.ds(j, 1)].rearrange("o p f -> (o p) f"), Q1T[k][0:PN]).then_inc(s_q1, 16)
                with e.Fori(0, HT - 1) as i:
                    for k in range(2):
                        store(i * 2 + k, k, i * 2 + k + 1)
                store(NT - 3, 0, NT - 2)
                store(NT - 2, 1, NT - 1, False)
                store(NT - 1, 0, NT, False)
            if act:
                def post(j, k, n):
                    e.wait_ge(s_yl[k], (j - k) * 8 + 16)
                    for q in range(3):
                        yt = YT[k][:, q, 0:PN]
                        ins = e.activation(yt, yt, ACT.Relu, bias=BNB[:, q:q + 1], scale=BNA[:, q:q + 1])
                        ins.then_inc(s_vr, 1)
                tiles("V", 0, post)
            if pe:
                e.wait_ge(s_sc[5], 1)
                for g in range(3):
                    for j in range(2):
                        mm = e.matmul(P3[:, 0:P], BR[:, g * P:(g + 1) * P], VA[:, (g * 2 + j) * P:(g * 2 + j + 1) * P],
                                      start=(g + j == 0), stop=(g + j == 3))
                mm.then_inc(s_sc[3], 1)
                e.wait_ge(s_sc[4], 2)

                def post(j, k, n):
                    e.wait_ge(s_vr, n * 3 + 1)
                    done(s_vd, n - 1)
                    for q in range(3):
                        mm = e.matmul((P1, P2)[k][0:PN, 0:3 * P], YT[k][:, q, 0:PN], VW[:, q * 3 * P:(q + 1) * 3 * P],
                                      start=(q == 0), stop=(q == 2))
                    mm.then_inc(s_vq, 1)
                tiles("V", 0, post)
            if dve:
                def post(j, k, n):
                    done(s_vq, n)
                    pv = (P1, P2)[k][0:PN]
                    xj = tile_of(XR, j)
                    done(s_q1, (n - 1) * 16)
                    line(e.tensor_tensor(xj, pv[:, 0:P], xj, ALU.add))
                    line(e.tensor_tensor(Q1T[k][0:PN], pv[:, P:2 * P], CB[0:PN, P:2 * P], ALU.add))
                    line(e.tensor_tensor(s0, pv[:, 2 * P:3 * P], CB[0:PN, 2 * P:3 * P], ALU.add))
                    line.sync()
                    line(e.tensor_tensor(xj, xj, CB[0:PN, 0:P], ALU.add))
                    line(e.tensor_scalar(z_of(j), s0, di(j), LOW, ALU.mult, ALU.mult))
                    line.sync()
                    e.sem_inc(s_vd, 1)
                tiles("V", 0, post, 5)

            Ec, Ed = ev["L3c"], ev["L3d"]
            split("L3c", lambda: (done(s_vd, NT), done(s_q1, 16 * NT)))
            if sp:
                e.wait_ge(s_q1, 1 + 16 * NT)

                def post(j, k, n):
                    done(Ec["z"], n - 1)
                    e.dma_start(SG[0:PN, 0, :], q1_d[bass.ds(j, 1)].rearrange("o p f -> (o p) f"))\
                     .then_inc(s_q1l, 16)
                tiles("L3c", 0, post)

                def post(j, k, n):
                    done(Ed["z"], n)
                    e.dma_start(out[bass.ds(j * PN, PN)], s1).then_inc(s_out, 16)
                tiles("L3d", 0, post)
                e.wait_ge(s_out, 1 + 16 * NT)
            if dve:
                def post(j, k, n):
                    line(parts_sum(Ec, k, n, s1))
                    line.sync()
                    e.sem_inc(Ec["red"], 1)
                    e.wait_ge(s_q1l, n * 16 + 1)
                    line(e.scalar_tensor_tensor(out=s0, in0=s1, scalar=di(j), in1=SG[0:PN, 0, :], op0=ALU.mult,
                                                op1=ALU.add))
                    line.sync()
                    line(e.tensor_scalar(z_of(j), s0, di(j), LOW, ALU.mult, ALU.mult))
                    line.sync()
                    e.sem_inc(Ec["z"], 1)
                tiles("L3c", 0, post, 4)
            if pe:
                aggregate("L3c", 0, P, True, 0, lambda *_: None, lambda: None)
            lo_at[0] += NT
            split("L3d", lambda: done(Ec["z"], NT))
            if dve:
                def post(j, k, n):
                    line(parts_sum(Ed, k, n, s0))
                    line.sync()
                    e.sem_inc(Ed["red"], 1)
                    e.wait_ge(s_out, (n - 1) * 16 + 1)
                    line(e.scalar_tensor_tensor(out=s1, in0=s0, scalar=di(j), in1=INV[0:PN], op0=ALU.mult,
                                                op1=ALU.mult))
                    line.sync()
                    line(e.tensor_tensor(s1, s1, tile_of(XR, j), ALU.add))
                    line.sync()
                    e.sem_inc(Ed["z"], 1)
                tiles("L3d", 0, post, 4)
            if pe:
                aggregate("L3d", 0, P, True, 0, lambda *_: None, lambda: None)
            lo_at[0] += NT

        N_CONST = 14
        block = ctx.enter_context(nc.Block())

        @block.sync
        def _(e):
            program("sp", e)

        @block.gpsimd
        def _(e):
            program("pool", e)

        @block.scalar
        def _(e):
            program("act", e)

        @block.tensor
        def _(e):
            program("pe", e)

        @block.vector
        def _(e):
            program("dve", e)


INPUTS = ("x", "src", "dst", "L0_gnn_W1", "L0_gnn_b1", "L0_gnn_W2", "L0_gnn_b2", "L0_gnn_eps", "L1_gnn_W1",
          "L1_gnn_b1", "L1_gnn_W2", "L1_gnn_b2", "L2_gnn_W1", "L2_gnn_b1", "L2_gnn_W2", "L2_gnn_b2",
          "L2_gnn_gamma", "L2_gnn_beta", "L3_gnn_l1_w", "L3_gnn_l1_b", "L3_gnn_bn_gamma", "L3_gnn_bn_beta",
          "L3_gnn_l2_w", "L3_gnn_l2_b", "L3_gnn_fp_w", "L3_gnn_fp_b")


def kernel(**inputs):
    import numpy as np
    import concourse.bacc as bacc
    from concourse.bass_utils import run_bass_kernel_spmd

    nc = bacc.Bacc("TRN2", target_bir_lowering=False, num_devices=1)
    arrays, aps = {}, {}
    for name in INPUTS:
        v = np.ascontiguousarray(inputs[name])
        if name == "L0_gnn_eps":
            v = v.reshape(1)
        arrays["in_" + name] = v
        aps[name] = nc.dram_tensor("in_" + name, v.shape, mybir.dt.from_np(v.dtype), kind="ExternalInput").ap()
    out = nc.dram_tensor("out_x", arrays["in_x"].shape, F32, kind="ExternalOutput").ap()
    build(nc, aps, out)
    r = run_bass_kernel_spmd(nc, [arrays], core_ids=[0])
    return r.results[0]["out_x"]
```

```python
from contextlib import ExitStack

import concourse.bass as bass
from concourse import mybir

F32 = mybir.dt.float32
BF16 = mybir.dt.bfloat16
F16 = mybir.dt.float16
I32 = mybir.dt.int32
ALU = mybir.AluOpType
ACT = mybir.ActivationFunctionType
AX = mybir.AxisListType

P = 128
CH = 128
GC = 2
GE = GC * CH
WIN = 23
HG = 7
RING = 7
GW = 20
EPS = 1e-5
PAD_SRC = -10000000


class Line:

    def __init__(self, eng, sem):
        self.eng, self.sem, self.n, self.off = eng, sem, 0, 0

    def __call__(self, ins):
        ins.then_inc(self.sem, 1)
        self.n += 1

    def sync(self):
        self.eng.wait_ge(self.sem, self.off + self.n)

    def loop(self, times, per):
        start, off = self.n, self.off
        with self.eng.Fori(0, times) as i:
            self.off = off + i * per
            yield i
            assert self.n - start == per, (self.n - start, per)
        self.off, self.n = off, start + times * per


def divisor(n, most):
    return max(d for d in range(1, most + 1) if n % d == 0)


def build(nc, a, out):
    N, D = a["x"].shape
    E = a["src"].shape[0]
    assert D == P
    PN = divisor(N, P)
    NT = N // PN
    assert NT % 4 == 1 and NT % 5 == 0
    NB = NT // 5
    BT = 5
    HT = (NT - 1) // 2
    G = -(-E // GE)
    G = -(-G // (2 * HG)) * 2 * HG
    assert G > E // GE
    QG = divisor(G, P)
    KR = G // QG
    NCH = G * GC
    STEPS = G // (2 * HG)
    KW = WIN * NT
    KWP = KW + KW % 2
    HALF = (WIN - 1) // 2
    AW = N + WIN
    AW += AW % 2
    GWN = -(-N // GW)
    assert GWN * GW <= AW and NT * GW <= 512
    FULL = E // GE
    HC = HG * GC
    assert (2 * HC) % RING == 0 and HC >= RING + HG and HC % 2 == 0 and NCH % 2 == 0
    LAYERS = a["L2_gnn_W1"].shape[0]
    FW = P + 2
    X0 = P
    LOW = 2048.0
    TOP = 16384.0
    SPREAD = 32.0
    assert (E + N) * P ** 0.5 / SPREAD < 60000

    ctx = ExitStack()
    with ctx:
        def sb(name, shape, dt):
            return ctx.enter_context(nc.sbuf_tensor(name, shape, dt))

        def sem(name):
            return ctx.enter_context(nc.semaphore(name))

        def dram(name, shape, dt):
            return nc.dram_tensor(name, shape, dt).ap()

        RW = KR * GE
        OHW = -(-KWP // 64) * 64
        IOW = max(KWP, P)
        SRW = max(RW, HC * P // 2)
        FTW = (STEPS + 1) * 16
        ADJ = sb("ADJ", [P, NT, AW], BF16)
        HPb = sb("HPb", [P, max(NT * 2 * FW, RING * OHW + 2 * HC * P + NT * GW, 8 * RW, 60 * P)], BF16)[:, :]
        XRf = sb("XRf", [P, max(NT * P, RW + SRW + KWP // 2 + 4 + P // 2 + FTW)], F32)[:, :]
        Zf = sb("Zf", [P, max(NT * P, 3 * NCH + (NCH + HC) // 2, 25 * P)], F32)[:, :]
        HP = HPb[:, 0:NT * 2 * FW].bitcast(F16).rearrange("p (t q f) -> p t q f", t=NT, q=2)
        XR = XRf[:, 0:NT * P].rearrange("p (t f) -> p t f", t=NT)
        Zn = Zf[:, 0:NT * P].rearrange("p (t f) -> p t f", t=NT)
        WB = sb("WB", [P, max(4 * P + 6 * NT, 3 * P + 18 * NT)], F32)
        STATS = WB[:, 3 * P:3 * P + 18 * NT].rearrange("p (q t c) -> p q t c", q=3, c=6)
        LNS = WB[:, 4 * P:4 * P + 6 * NT].rearrange("p (t c) -> p t c", c=6)
        BB = sb("BB", [P, P], F32)
        IDF = sb("IDF", [P, P], F32)
        IDB = sb("IDB", [P, P], BF16)
        WL1 = sb("WL1", [P, 3, P], F32)
        INV = sb("INV", [P, P], F32)
        ST = sb("ST", [P, 2, FW], F32)
        SF = sb("SF", [P, 2, P], F32)
        SG = sb("SG", [P, 2, P], F32)
        SMW = 12 * NT + 24
        SM = sb("SM", [P, SMW], F32)
        FL = sb("FL", [P, 4], I32)
        B_L0 = sb("B_L0", [P, 2], F32)
        B_L1 = sb("B_L1", [P, 1], F32)
        B_L2 = sb("B_L2", [P, 4, LAYERS], F32)
        B_L3 = sb("B_L3", [P, 4, 3], F32)
        Q_B1, Q_B2, Q_GA, Q_BE = range(4)
        R_B1, R_GA, R_BE, R_B2 = range(4)
        LOT = sb("LOT", [P, P], BF16)
        LOX = sb("LOX", [P, P], BF16)
        ROW = sb("ROW", [1, P], F32)
        PS = ctx.enter_context(nc.psum_tensor("PS", [P, 8, 512], F32))

        at = [0]

        def small(n):
            at[0] += n
            assert at[0] <= SMW
            return SM[:, at[0] - n:at[0]]

        DI = small(NT)
        DEG = small(NT)
        DIL = small(NT)
        DIS = small(NT)
        MV = small(2 * NT).rearrange("p (t c) -> p t c", c=2)
        SDV = small(NT)
        RS = small(NT)
        NBI = small(NT)
        MX = small(NT)
        SE = small(NT)
        TMP = small(NT)
        EPSC = small(1)
        EPS0 = small(1)
        EPSL = small(1)
        CF = small(1)
        BND = small(3)
        BNM = small(2)
        BNS = small(1)
        BNR = small(1)
        BNT = small(1)
        BNA = small(3)
        BNB = small(3)
        BND2 = small(3)
        ONEC = small(1)
        WBASE = small(1)

        HPf = HPb.bitcast(F32)
        dst_i = XRf[:, 0:RW].bitcast(I32)
        src_i = XRf[:, RW:2 * RW].bitcast(I32)
        c0 = RW + SRW
        IOK = XRf[:, c0:c0 + KWP // 2].bitcast(F16)
        c0 += -(-(KWP // 2) // 4) * 4
        IOP = XRf[:, c0:c0 + P // 2].bitcast(F16)
        c0 += P // 2
        FT = XRf[:, c0:c0 + FTW].bitcast(I32)
        dst_f, src_f, til_f, key_f = (HPf[:, k * RW:(k + 1) * RW] for k in range(4))
        iota_i = HPf[:, 0:IOW].bitcast(I32)
        OHK = [HPb[:, k * OHW:k * OHW + KWP] for k in range(RING)]
        c0 = RING * OHW
        OHP = [HPb[:, c0 + k * HC * P:c0 + (k + 1) * HC * P].rearrange("p (n c) -> p n c", c=HC) for k in range(2)]
        OHG = [HPb[:, c0 + k * P:c0 + (k + 1) * P] for k in range(2)]
        c0 += 2 * HC * P
        LOB = HPb[:, c0:c0 + NT * GW].rearrange("p (t d) -> p t d", t=NT)
        KT, PT, KGT = (Zf[:, k * NCH:(k + 1) * NCH] for k in range(3))
        PTH = Zf[:, 3 * NCH:3 * NCH + (NCH + HC) // 2].bitcast(F16)
        XIN = HPf[:, 0:NT * P].rearrange("p (t f) -> p t f", t=NT)
        IOC = XRf[:, RW:RW + HC * P // 2].bitcast(F16).rearrange("p (n c) -> p n c", c=HC)

        base_d = dram("base_d", [G + 1], I32)
        lo_d = dram("lo_d", [P, NT, AW], BF16)
        y_d = dram("y_d", [3, P, N], F32)
        q1_d = dram("q1_d", [NT, PN, P], F32)

        AG = [PS[:, 0, :], PS[:, 1, :]]
        TP, P1, P2, P3 = (PS[:, b, :] for b in (2, 3, 4, 5))
        RB = [PS[:, 4:6, :].rearrange("p b c -> p (b c)"), PS[:, 6:8, :].rearrange("p b c -> p (b c)")]
        WPS = [PS[:, 0:2, :], PS[:, 2:4, :]]
        CPS = [PS[:, 4, :], PS[:, 5, :]]

        s_in, s_w1, s_w, s_x, s_base, s_const, s_pad, s_rows = (sem("s_" + n) for n in
                                                          ("in", "w1", "w", "x", "base", "const", "pad", "rows"))
        s_dve0, s_dve1, s_act1, s_pool0 = (sem(n) for n in ("s_dve0", "s_dve1", "s_act1", "s_pool0"))
        s_rowt, s_rowc = sem("s_rowt"), sem("s_rowc")
        s_frow, s_fsum, s_frow2, s_fsum2 = (sem("s_f%d" % k) for k in range(4))
        s_flag, s_flag2 = sem("s_flag"), sem("s_flag2")
        s_oh = sem("s_oh")
        s_ohx = sem("s_ohx")
        s_mv = sem("s_mv")
        s_add = sem("s_add")
        s_bline = sem("s_bline")
        s_goh, s_gox, s_gline, s_glo = (sem("s_g" + n) for n in ("oh", "ox", "line", "lo"))
        s_lol, s_lox, s_lom, s_lod, s_loc = (sem("s_lo" + n) for n in "lxmdc")
        s_adj = sem("s_adj")
        PHASES = {"L0": "tr cf d1 rg d2 z ex", "L1a": "tr cf d1 rg d2 z", "L1b": "", "L2": "tr cf d1 rg d2 z",
                  "L3a": "tr cf d1 z", "L3b": "tr cf d1 z", "L3c": "z", "L3d": "z"}
        ev = {p: {n: sem(f"{p}_{n}") for n in ("agg red hi hp " + more).split()}
              for p, more in PHASES.items()}
        s_ln = [[sem(f"ln{k}_{m}") for m in range(5)] for k in range(4)]
        s_soft, s_sc = sem("s_soft"), [sem(f"s_sc{m}") for m in range(6)]
        s_bn = {n: sem("bn_" + n) for n in ("var", "sd", "ab", "rel", "tr", "w")}
        s_wt, s_ones = sem("s_wt"), sem("s_ones")
        s_at = {n: sem("at_" + n) for n in ("tr", "act", "dve")}
        s_y, s_yl0, s_vw, s_vt, s_vc, s_vm, s_vv, s_vr, s_vq, s_vd = (sem("s_v%d" % k) for k in range(10))
        s_yl = [s_yl0] + [sem(f"s_yl{k}") for k in range(1, 4)]
        s_null, s_xg, s_iota = sem("s_null"), sem("s_xg"), sem("s_iota")
        s_q1b = sem("s_q1b")
        s_q1, s_q1l, s_out = sem("s_q1"), sem("s_q1l"), sem("s_out")
        s_rt = sem("s_rt")
        credited = [s for p in PHASES for s in ev[p].values()] + [s_y, s_q1, s_q1l, 
                                                                  s_vr, s_vq, s_vd, s_vd, s_out, s_lom,
                                                                  s_q1b, s_bn["w"]]

        def col(v):
            return v.rearrange("(p o) -> p o", o=1)

        def bcast(v, n=P):
            return v.rearrange("(o n) -> o n", o=1).broadcast_to([n, v.shape[0]])

        def scale_from_bound(e, line, row, inv):
            line(e.tensor_scalar(inv, row, 1 / TOP, 1e-30, ALU.mult, ALU.max))
            line.sync()
            line(e.reciprocal(row, inv))
            line.sync()

        def absolute(e, line, to, v):
            line(e.scalar_tensor_tensor(out=to, in0=v, scalar=-1.0, in1=v, op0=ALU.mult, op1=ALU.max))

        def program(role, e):
            pe, act, dve, pool, sp = (role == r for r in ("pe", "act", "dve", "pool", "sp"))

            n_in = 2 * (sum(1 for k in range(KR) if FULL - k * QG > 0) + (1 if E % GE else 0))
            if sp:
                e.wait_ge(s_pad, 2)
                for dram_t, tile in ((a["dst"], dst_i), (a["src"], src_i)):
                    t3 = tile.rearrange("p (k e) -> p k e", k=KR)
                    for k in range(KR):
                        n = min(QG, FULL - k * QG)
                        if n > 0:
                            e.dma_start(t3[0:n, k, :], dram_t[k * QG * GE:(k * QG + n) * GE]
                                        .rearrange("(q e) -> q e", e=GE)).then_inc(s_in, 16)
                    r = E - FULL * GE
                    if r:
                        q, k = FULL % QG, FULL // QG
                        e.dma_start(t3[q:q + 1, k, 0:r], dram_t[FULL * GE:E].rearrange("(o e) -> o e", o=1))\
                         .then_inc(s_in, 16)
            if act:
                e.dma_start(WL1[:, 0], a["L1_gnn_W1"]).then_inc(s_w1, 16)
                e.dma_start(WL1[:, 1], a["L1_gnn_W2"]).then_inc(s_w1, 16)
                e.dma_start(B_L1[:, :], col(a["L1_gnn_b1"])).then_inc(s_w1, 16)
                e.wait_ge(s_in, 16 * n_in)
                e.dma_start(WL1[:, 2], bcast(a["L1_gnn_b2"])).then_inc(s_w, 16)
                e.dma_start(WB[:, 0:2 * P], a["L0_gnn_W1"]).then_inc(s_w, 16)
                e.dma_start(WB[:, 2 * P:4 * P].rearrange("p (k n) -> p k n", k=2),
                            a["L0_gnn_W2"].rearrange("(k p) n -> p k n", p=P)).then_inc(s_w, 16)
                e.dma_start(BB[:, :], bcast(a["L0_gnn_b2"])).then_inc(s_w, 16)
                e.dma_start(EPS0, bcast(a["L0_gnn_eps"])).then_inc(s_w, 16)
                e.dma_start(B_L0[:, :], a["L0_gnn_b1"].rearrange("(k p) -> p k", p=P),
                            allow_slow_non_contiguous=True).then_inc(s_w, 16)
                for q, n in enumerate(("b1", "b2", "gamma", "beta")):
                    e.dma_start(B_L2[:, q, :], a["L2_gnn_" + n].rearrange("l p -> p l"),
                                allow_slow_non_contiguous=True).then_inc(s_w, 16)
                for q, n in enumerate(("l1_b", "bn_gamma", "bn_beta", "l2_b")):
                    v = a["L3_gnn_" + n]
                    v = v.rearrange("q p -> p q") if len(v.shape) == 2 else v.rearrange("(q p) -> p q", p=P)
                    e.dma_start(B_L3[:, q, :], v, allow_slow_non_contiguous=True).then_inc(s_w, 16)
            if pool:
                for s in credited:
                    e.sem_inc(s, 1)
                line = Line(e, s_pool0)
                line(e.iota(iota_i, [[1, IOW]], base=0, channel_multiplier=0))
                line.sync()
                e.sem_inc(s_iota, 1)
                line(e.memset(IDF[:, :], 0.0))
                line(e.memset(ADJ[:, :, 0:1], 0.0))
                line(e.memset(ADJ[:, :, AW - WIN - 8:AW], 0.0))
                line.sync()
                line(e.affine_select(out=IDF[:, :], in_=IDF[:, :], compare_op=ALU.not_equal, fill=1.0,
                                     base=0, pattern=[[-1, P]], channel_multiplier=1))
                line.sync()
                line(e.tensor_copy(IDB[:, :], IDF[:, :]))
                line.sync()
                e.sem_inc(s_const, 1)
            if dve:
                line = Line(e, s_dve0)
                e.memset(dst_i, N).then_inc(s_pad, 1)
                e.memset(src_i, PAD_SRC).then_inc(s_pad, 1)
                e.memset(FL[:, 3:4], N).then_inc(s_pad, 1)
                line(e.memset(ONEC, 1.0))
                line(e.memset(EPSC, EPS))
                e.wait_ge(s_w1, 48)
                far = (E + 1.0) ** 0.5 * P ** 0.5
                absw = SG[:, 1, :]
                absolute(e, line, absw, WL1[:, 0])
                line.sync()
                e.sem_inc(s_sc[0], 1)
                absolute(e, line, BND[:, 1:2], B_L1[:, :])
                line.sync()
                e.wait_ge(s_sc[1], 1)
                line(e.scalar_tensor_tensor(out=BND[:, 0:1], in0=P3[:, 0:1], scalar=far, in1=BND[:, 1:2],
                                            op0=ALU.mult, op1=ALU.add))
                absolute(e, line, absw, WL1[:, 1])
                line.sync()
                line(e.tensor_copy(SF[:, 1, :], BND[:, 0:1].broadcast_to([P, P])))
                line.sync()
                e.sem_inc(s_sc[2], 1)
                e.wait_ge(s_sc[3], 1)
                line(e.tensor_copy(SF[:, 1, :], P3[:, 0:P]))
                line.sync()
                scale_from_bound(e, line, SF[:, 1, :], INV[:, :])
                line(e.tensor_tensor(WL1[:, 1], WL1[:, 1], SF[:, 1, :], ALU.mult))
                line.sync()
                line(e.tensor_scalar(WL1[:, 1], WL1[:, 1], LOW, None, ALU.mult))
                line.sync()
                e.sem_inc(s_sc[4], 1)
                e.wait_ge(s_iota, 1)
                line(e.tensor_copy(IOK, iota_i[:, 0:KWP]))
                line(e.tensor_copy(IOP, iota_i[:, 0:P]))
                line.sync()
                e.wait_ge(s_in, 16 * n_in)
                line(e.tensor_copy(src_f, src_i))
                line(e.tensor_copy(dst_f, dst_i))
                line.sync()
                line(e.tensor_scalar(key_f.bitcast(I32), src_f, -(PN - 1) / 2.0, 1.0 / PN, ALU.add, ALU.mult))
                line.sync()
                line(e.tensor_copy(til_f, key_f.bitcast(I32)))
                line.sync()
                line(e.scalar_tensor_tensor(out=src_f, in0=til_f, scalar=-float(PN), in1=src_f,
                                            op0=ALU.mult, op1=ALU.add))
                line.sync()
                for cmp, edge, way in ((ALU.is_lt, 0.0, -1.0), (ALU.is_ge, float(PN), 1.0)):
                    line(e.tensor_scalar(key_f, src_f, edge, way, cmp, ALU.mult))
                    line.sync()
                    line(e.tensor_tensor(til_f, til_f, key_f, ALU.add))
                    line(e.scalar_tensor_tensor(out=src_f, in0=key_f, scalar=-float(PN), in1=src_f,
                                                op0=ALU.mult, op1=ALU.add))
                    line.sync()
                line(e.scalar_tensor_tensor(out=key_f, in0=dst_f, scalar=float(NT), in1=til_f,
                                            op0=ALU.mult, op1=ALU.add))
                d3 = dst_f.rearrange("p (k e) -> p k e", k=KR)
                t3 = til_f.rearrange("p (k e) -> p k e", k=KR)
                m3 = key_f.rearrange("p (k e) -> p k e", k=KR)
                line(e.tensor_scalar(ST[:, 0, 0:KR], d3[:, :, 0], -float(NT), None, ALU.mult))
                line.sync()
                for k in range(KR):
                    line(e.tensor_scalar(t3[:, k, :], m3[:, k, :], ST[:, 0, k:k + 1], None, ALU.add))
                line.sync()
                e.sem_inc(s_rows, 1)
            if sp:
                e.wait_ge(s_in, 16 * n_in)
                e.wait_ge(s_pad, 3)
                e.dma_start(base_d[0:G].rearrange("(k q) -> q k", k=KR),
                            dst_i[0:QG, :].rearrange("p (k e) -> p k e", k=KR)[:, :, 0],
                            allow_slow_non_contiguous=True).then_inc(s_base, 16)
                e.dma_start(base_d[G:G + 1].rearrange("(o n) -> o n", o=1), FL[0:1, 3:4]).then_inc(s_base, 16)
                e.wait_ge(s_base, 32)
                e.dma_start(ST[0:QG, 1, 0:KR].bitcast(I32), base_d[1:G + 1].rearrange("(k q) -> q k", k=KR),
                            allow_slow_non_contiguous=True).then_inc(s_base, 16)
                e.dma_start(FT[0:1, 8:8 + 16 * STEPS].rearrange("o (s g) -> o s g", g=8)[:, :, 0:HG],
                            base_d[0:G].rearrange("(o s g) -> o s g", o=1, g=HG)).then_inc(s_base, 16)
            if dve:
                dense = float(min(256, N // 2))
                d = d3[0:QG]
                flags = SG[0:QG, 0, 0:6 * KR].rearrange("p (k c) -> p k c", c=6)
                nxt = SF[0:QG, 0, 0:KR]
                e.wait_ge(s_base, 64)
                line(e.tensor_copy(nxt, ST[0:QG, 1, 0:KR].bitcast(I32)))
                line(e.memset(FT[0:1, :].rearrange("o (s g) -> o s g", g=8)[:, :, HG:8], 0))
                line(e.memset(FT[0:1, 0:HG], 0))
                line(e.memset(FT[0:1, 8 + 16 * STEPS:8 + 16 * STEPS + HG], 0))
                line(e.memset(SG[0:QG, 0, :], 0.0))
                line(e.memset(SG[0:QG, 1, :], 0.0))
                cmp3 = src_i[0:QG, :].bitcast(F32).rearrange("p (k e) -> p k e", k=KR)
                line(e.tensor_tensor(cmp3[:, :, 0:GE - 1], d[:, :, 0:GE - 1], d[:, :, 1:GE], ALU.is_gt))
                line.sync()
                first, mid = d[:, :, 0], d[:, :, CH]
                for k in range(KR):
                    line(e.tensor_reduce(flags[:, k, 0:1], cmp3[:, k, 0:GE - 1], AX.X, ALU.add))
                line(e.tensor_tensor(flags[:, :, 1], d[:, :, GE - 1], nxt, ALU.is_gt))
                w = [SG[0:QG, 1, c * KR:(c + 1) * KR] for c in range(3)]
                line(e.tensor_tensor(w[0], nxt, first, ALU.subtract))
                line(e.tensor_tensor(w[1], first, mid, ALU.is_equal))
                line(e.tensor_tensor(w[2], mid, nxt, ALU.is_equal))
                line.sync()
                line(e.tensor_scalar(flags[:, :, 2], w[0], float(WIN - 1), None, ALU.is_gt))
                for c, v in ((1, first), (2, mid)):
                    line(e.scalar_tensor_tensor(out=w[c], in0=v, scalar=dense, in1=w[c],
                                                op0=ALU.is_ge, op1=ALU.mult))
                    line.sync()
                    line(e.scalar_tensor_tensor(out=flags[:, :, 2 + c], in0=v, scalar=float(N), in1=w[c],
                                                op0=ALU.is_lt, op1=ALU.mult))
                line(e.tensor_scalar(flags[0:1, 0, 5:6], first[0:1, 0:1], 0.0, None, ALU.is_gt))
                line.sync()
                line(e.tensor_reduce(SF[0:QG, 1, 0:1], SG[0:QG, 0, 0:6 * KR], AX.X, ALU.add))
                line.sync()
                e.sem_inc(s_frow, 1)
                line(e.tensor_copy(IOC, IOP.rearrange("p (n o) -> p n o", o=1).broadcast_to([P, P, HC])))
                e.wait_ge(s_fsum, 1)
                line(e.tensor_scalar(FL[0:1, 0:1], P3[0:1, 0:1], 0.0, None, ALU.is_gt))
                line.sync()
                e.sem_inc(s_flag, 1)

            if pe:
                e.wait_ge(s_sc[0], 1)
                e.matmul(P3[:, 0:1], SG[:, 1, :], ONEC, start=True, stop=True).then_inc(s_sc[1], 1)
                e.wait_ge(s_sc[2], 1)
                e.matmul(P3[:, 0:P], SF[:, 1, :], SG[:, 1, :], start=True, stop=True).then_inc(s_sc[3], 1)
            tables = ((KT, til_f, 2), (PT, src_f, 3), (KGT, key_f, 4))
            if pe:
                e.wait_ge(s_const, 1)
                e.wait_ge(s_rows, 1)
                for n, (_, src, bank) in enumerate(tables):
                    s3 = src.rearrange("p (k h e) -> p k h e", k=KR, h=GC)
                    for h in range(GC):
                        if h:
                            e.wait_ge(s_rowc, 2 * n + 1)
                        for k in range(KR):
                            mm = e.transpose(PS[:, bank, k * QG:(k + 1) * QG], s3[0:QG, k, h, :], IDF[0:QG, 0:QG])
                        mm.then_inc(s_rowt, 1)
                e.wait_ge(s_frow, 1)
                e.matmul(P3[0:1, 0:1], SF[0:QG, 1, 0:1], ONEC[0:QG, :], start=True, stop=True)\
                 .then_inc(s_fsum, 1)
            if act:
                for n, (tab, _, bank) in enumerate(tables):
                    for h in range(GC):
                        e.wait_ge(s_rowt, 2 * n + h + 1)
                        e.copy(tab.rearrange("p (g h) -> p g h", h=GC)[:, :, h], PS[:, bank, 0:G])\
                         .then_inc(s_rowc, 1)

            e.wait_ge(s_flag, 1)
            bad = e.value_load(FL[0:1, 0:1], min_val=0, max_val=1)
            with e.If(bad == 0):
                quick_build(role, e)
            with e.Else():
                if dve:
                    e.memset(FL[0:1, 1:2], 1).then_inc(s_flag2, 1)
            e.wait_ge(s_flag2, 1)
            bad2 = e.value_load(FL[0:1, 1:2], min_val=0, max_val=1)
            with e.If(bad2 == 0):
                layers(role, e, False)
            with e.Else():
                general_build(role, e)
                layers(role, e, True)

        def load_x(e, s_x):
            e.dma_start(XIN[0:PN], a["x"].rearrange("(t p) f -> p t f", p=PN)).then_inc(s_x, 16)

        def quick_build(role, e):
            PER = 2 * HC
            if role == "dve":
                line = Line(e, s_bline)
                regs = [e.alloc_register(f"vb{k}") for k in range(8)]

                def source_one_hots(n0, h):
                    e.tensor_tensor(OHP[h], IOC, PTH[:, bass.ds(n0, HC)].rearrange("p (o c) -> p o c", o=1)
                                    .broadcast_to([P, P, HC]), ALU.is_equal).then_inc(s_oh, 1)

                def add_first_column(vals, n0, h, g):
                    n = n0 + g
                    if g == 0:
                        e.wait_ge(s_ohx, (n0 + HG) * GC + RING)
                        e.wait_ge(s_mv, n0 + HG - 1 + 2)
                    e.wait_ge(s_add, n + 2 * HG)
                    to = ADJ[0:PN, :, bass.ds(vals[g], 1)].rearrange("p t o -> p (t o)")
                    e.tensor_tensor(to, to, CPS[h][0:PN, g * NT:(g + 1) * NT], ALU.add).then_inc(s_add, 1)

                def load_bases(i, h):
                    e.load(regs, FT[0:1, bass.ds((i * 2 + h) * 8, 8)])
                    return [e.snap(r, min_val=0, max_val=N) for r in regs]

                def half(i, h, first=False):
                    n0 = i * PER + h * HC
                    for m in range(HC):
                        k = (h * HC + m) % RING
                        if m % 2 == 0:
                            e.wait_ge(s_ohx, n0 + m + 2)
                        if m == 0:
                            source_one_hots(n0, h)
                        e.tensor_scalar(OHK[k], IOK, KT[:, bass.ds(n0 + m, 1)], None, ALU.is_equal)\
                         .then_inc(s_oh, 1)
                        if m == 1 and not first:
                            before = load_bases(i, h)
                        if m >= HC - HG and not first:
                            add_first_column(before, i * 2 * HG + (h - 1) * HG, 1 - h, m - (HC - HG))

                e.wait_ge(s_rowc, 6)
                line(e.tensor_copy(PTH[:, 0:NCH], PT))
                line(e.memset(PTH[:, NCH:NCH + HC], 0.0))
                line.sync()
                e.sem_inc(s_ohx, RING)
                e.sem_inc(s_add, 2 * HG)
                half(0, 0, True)
                half(0, 1)
                with e.Fori(0, (STEPS - 1) // 2) as i:
                    for k in range(4):
                        half(i * 2 + 1 + k // 2, k % 2)
                if (STEPS - 1) % 2:
                    half(STEPS - 1, 0)
                    half(STEPS - 1, 1)
                last = load_bases(STEPS, 0)
                for g in range(HG):
                    add_first_column(last, G - HG, 1, g)
                e.wait_ge(s_add, G + 2 * HG)
                e.wait_ge(s_mv, G + 2)
                line(e.tensor_reduce(TMP[0:PN, 0:1], ADJ[0:PN, :, 0:min(256, N)], AX.XY, ALU.max))
                line.sync()
                line(e.tensor_scalar(TMP[0:PN, 1:2], TMP[0:PN, 0:1], 256.0, None, ALU.is_ge))
                line.sync()
                e.sem_inc(s_frow2, 1)
                e.wait_ge(s_fsum2, 1)
                line(e.tensor_scalar(FL[0:1, 1:2], P3[0:1, 0:1], 0.0, None, ALU.is_gt))
                line.sync()
                e.wait_ge(s_x, 16)
                e.sem_inc(s_flag2, 1)
            if role == "sp":
                e.wait_ge(s_ohx, NCH + RING)
                load_x(e, s_x)
            if role == "pe":
                with e.Fori(0, STEPS) as i:
                    for h in range(2):
                        e.wait_ge(s_add, (i * 2 + h + 1) * HG)
                        for m in range(h * HG, (h + 1) * HG):
                            e.wait_ge(s_mv, i * 2 * HG + m + 1)
                            g = m - h * HG
                            for c in range(GC):
                                k = (m * GC + c) % RING
                                e.wait_ge(s_oh, i * (PER + 2) + h + 1 + m * GC + c + 1)
                                first, last = c == 0, c == GC - 1
                                lhs = OHP[h][:, :, g * GC + c]
                                e.matmul(CPS[h][:, g * NT:(g + 1) * NT], lhs, OHK[k][:, 0:NT],
                                         start=first, stop=last)
                                for b in range(2):
                                    lo = NT + b * HALF * NT
                                    mm = e.matmul(WPS[m % 2][:, b, 0:HALF * NT], lhs, OHK[k][:, lo:lo + HALF * NT],
                                                  start=first, stop=last)
                                mm.then_inc(s_ohx, 1)
                e.wait_ge(s_frow2, 1)
                e.matmul(P3[0:1, 0:1], TMP[0:PN, 1:2], ONEC[0:PN, :], start=True, stop=True)\
                 .then_inc(s_fsum2, 1)
            if role == "act":
                regs = [[e.alloc_register(f"ab{h}_{k}") for k in range(8)] for h in range(2)]

                def load_bases(i, h):
                    e.load(regs[h % 2], FT[0:1, bass.ds((i * 2 + h + 1) * 8, 8)])

                e.wait_ge(s_base, 64)
                e.wait_ge(s_const, 1)
                e.sem_inc(s_mv, 2)
                load_bases(0, 0)
                with e.Fori(0, STEPS) as i:
                    for m in range(2 * HG):
                        h, g = divmod(m, HG)
                        n = i * 2 * HG + m
                        if g == 0:
                            vals = [e.snap(r, min_val=0, max_val=N) for r in regs[h]]
                        e.wait_ge(s_ohx, (n + 1) * GC + RING)
                        e.wait_ge(s_mv, n + 2)
                        to = ADJ[0:PN, :, bass.ds(vals[g] + 1, 2 * HALF)]
                        e.copy(to.rearrange("p t (b d) -> p b d t", b=2),
                               WPS[m % 2][0:PN, :, 0:HALF * NT].rearrange("p b (d t) -> p b d t", t=NT))\
                         .then_inc(s_mv, 1)
                        if g == 2:
                            load_bases(i, h + 1)

        def general_build(role, e):
            KV = GW * NT
            ACC = PS[:, 0, 0:KV]
            if role == "dve":
                e.wait_ge(s_rowc, 6)
                line = Line(e, s_gline)
                line(e.memset(WBASE, -float(KV)))
                line(e.memset(ADJ[:, :, :], 0.0))
                e.sem_inc(s_gox, 2)
                e.sem_inc(s_goh, 2)

                def one_hots(w, c, k):
                    e.wait_ge(s_gox, w * NCH + c + 1)
                    e.tensor_scalar(OHK[k][:, 0:KV], IOK[:, 0:KV], WBASE, KGT[:, bass.ds(c, 1)],
                                    ALU.add, ALU.is_equal).then_inc(s_goh, 1)
                    e.tensor_scalar(OHG[k], IOP, PT[:, bass.ds(c, 1)], None, ALU.is_equal).then_inc(s_goh, 1)

                for w in line.loop(GWN, 3):
                    line.sync()
                    e.wait_ge(s_goh, w * 2 * NCH + 2)
                    line(e.tensor_scalar(WBASE, WBASE, float(KV), None, ALU.add))
                    line.sync()
                    e.sem_inc(s_null, 1)
                    with e.Fori(0, NCH // 2) as c:
                        for k in range(2):
                            one_hots(w, c * 2 + k, k)
                    e.wait_ge(s_gox, w * NCH + NCH + 2)
                    e.wait_ge(s_glo, w * 16 + 16)
                    acc = ACC[0:PN].rearrange("p (d t) -> p t d", t=NT)
                    hi = ADJ[0:PN, :, bass.ds(w * GW, GW)]
                    line(e.tensor_copy(hi, acc))
                    line.sync()
                    line(e.tensor_tensor(LOB[0:PN], acc, hi, ALU.subtract))
                line.sync()
            if role == "pe":
                def product(w, c, k, first, last):
                    e.wait_ge(s_goh, (w * NCH + c + 1) * 2 + 2)
                    e.matmul(ACC, OHG[k], OHK[k][:, 0:KV], start=first, stop=last,
                             skip_group_check=True).then_inc(s_gox, 1)

                with e.Fori(0, GWN) as w:
                    e.wait_ge(s_gline, w * 3 + 2)
                    product(w, 0, 0, True, False)
                    with e.Fori(0, NCH // 2 - 1) as c:
                        for k in range(2):
                            product(w, c * 2 + 1 + k, 1 - k, False, False)
                    product(w, NCH - 1, 1, False, True)
            if role == "sp":
                e.sem_inc(s_glo, 16)
                with e.Fori(0, GWN) as w:
                    e.wait_ge(s_gline, w * 3 + 5)
                    e.dma_start(lo_d[0:PN, :, bass.ds(w * GW, GW)], LOB[0:PN]).then_inc(s_glo, 16)
                e.wait_ge(s_glo, 16 * (GWN + 1))
                load_x(e, s_xg)

        def remainders(e):
            def bring(tiles0, count, turned):
                with e.Fori(0, count) as l:
                    with e.Fori(0, NT) as j:
                        with e.Fori(0, NT) as t:
                            e.wait_ge(s_lom, (tiles0 + l * NT + j) * NT + t + 1)
                            src = lo_d[0:PN, bass.ds(j, 1), bass.ds(t * PN, P)] if turned else \
                                lo_d[0:PN, bass.ds(t, 1), bass.ds(j * PN, P)]
                            e.dma_start(LOT[0:PN, :], src.rearrange("p o d -> p (o d)")).then_inc(s_lol, 16)

            e.wait_ge(s_glo, 16 * (GWN + 1))
            bring(0, 3 + LAYERS, False)
            e.wait_ge(s_lom, (3 + LAYERS) * NT * NT + 1)
            with e.Fori(0, NT) as t:
                with e.Fori(0, NT) as b:
                    m = t * NT + b
                    blk = lo_d[0:PN, bass.ds(t, 1), bass.ds(b * PN, PN)].rearrange("p o d -> p (o d)")
                    e.dma_start(LOX[0:PN, 0:PN], blk).then_inc(s_lod, 16)
                    e.wait_ge(s_loc, m + 1)
                    e.sem_inc(s_null, 1)
                    e.dma_start(blk, LOT[0:PN, 0:PN]).then_inc(s_lod, 16)
                    e.wait_ge(s_lod, (m + 1) * 32)
            bring((3 + LAYERS) * NT, 4, True)

        def layers(role, e, general):
            pe, act, dve, pool, sp = (role == r for r in ("pe", "act", "dve", "pool", "sp"))
            if pool:
                if general:
                    remainders(e)
                return
            line = Line(e, s_dve1 if dve else s_act1)
            done = lambda s, n: e.wait_ge(s, n + 1)
            settle = lambda: e.sem_inc(s_null, 1)
            lo_at = [0]

            if dve:
                e.wait_ge(s_const, 1)
                diag = ADJ[0:PN].rearrange("p t d -> p (t d)")[:, 0:(NT - 1) * (AW + PN)]\
                    .rearrange("p (t d) -> p t d", t=NT - 1)[:, :, 0:PN]
                ones = IDB[0:PN, 0:PN].rearrange("p (o d) -> p o d", o=1).broadcast_to([PN, NT - 1, PN])
                e.tensor_tensor(diag, diag, ones, ALU.add).then_inc(s_adj, 1)
                last = ADJ[0:PN, NT - 1, (NT - 1) * PN:NT * PN]
                e.tensor_tensor(last, last, IDB[0:PN, 0:PN], ALU.add).then_inc(s_adj, 1)
            def stats_of(j):
                return e.bn_stats(LNS[0:PN, bass.ds(j, 1), :].rearrange("p o c -> p (o c)"), tile_of(XR, j))

            def block(b):
                t = slice(b * BT, (b + 1) * BT) if isinstance(b, int) else bass.ds(b * BT, BT)
                return Zn[0:PN, t, :], HP[0:PN, t, 0, 0:P], HP[0:PN, t, 1, 0:P]

            def high_part(E_, b, z=None):
                zb, hi, lo = block(b)
                e.activation(hi, zb if z is None else z, ACT.Copy, scale=1 / LOW).then_inc(E_["hi"], 1)

            def low_part(E_, b, n, z=None):
                done(E_["hi"], n)
                zb, hi, lo = block(b)
                e.scalar_tensor_tensor(out=lo, in0=hi, scalar=-LOW, in1=zb if z is None else z,
                                       op0=ALU.mult, op1=ALU.add).then_inc(E_["hp"], 1)

            MINE = 3

            def normalize(k, weight=None, ph=None):
                stats, sd, z, rs, za = s_ln[k]
                me, ve, mo, vo = (LNS[0:PN, :, c] for c in (1, 2, 4, 5))
                mean, var = MV[0:PN, :, 0], MV[0:PN, :, 1]
                line(e.tensor_tensor(mean, me, mo, ALU.add))
                line(e.tensor_tensor(TMP[0:PN], me, mo, ALU.subtract))
                line(e.tensor_tensor(var, ve, vo, ALU.add))
                line.sync()
                line(e.tensor_tensor(TMP[0:PN], TMP[0:PN], TMP[0:PN], ALU.mult))
                line(e.tensor_scalar(var, var, 1.0 / P, None, ALU.mult))
                line.sync()
                line(e.scalar_tensor_tensor(out=var, in0=TMP[0:PN], scalar=0.25, in1=var, op0=ALU.mult,
                                            op1=ALU.add))
                line.sync()
                e.sem_inc(stats, 1)
                e.wait_ge(sd, 1)
                line(e.reciprocal(RS[0:PN], SDV[0:PN]))
                line.sync()
                if weight is None:
                    line(e.tensor_scalar(RS[0:PN], RS[0:PN], LOW, None, ALU.mult))
                else:
                    line(e.tensor_tensor(RS[0:PN], RS[0:PN], weight, ALU.mult))
                line.sync()
                line(e.scalar_tensor_tensor(out=NBI[0:PN], in0=MV[0:PN, :, 0], scalar=-0.5, in1=RS[0:PN],
                                            op0=ALU.mult, op1=ALU.mult))
                line.sync()
                e.sem_inc(rs, 1)
                for b in range(NB + 1):
                    if b < NB:
                        for m in range(MINE):
                            j = b * BT + m
                            line(e.tensor_scalar(Zn[0:PN, j, :], XR[0:PN, j, :], RS[0:PN, j:j + 1],
                                                 NBI[0:PN, j:j + 1], ALU.mult, ALU.add))
                        line.sync()
                        zb = Zn[0:PN, b * BT:b * BT + MINE, :]
                        e.tensor_scalar(zb, zb, 0.0, None, ALU.max).then_inc(z, 1)
                    if b and ph:
                        low_part(ev[ph], b - 1, b)
                e.wait_ge(z, NB)

            def deviation(k):
                stats, sd, z, rs, za = s_ln[k]
                e.wait_ge(stats, 1)
                e.activation(SDV[0:PN], MV[0:PN, :, 1], ACT.Sqrt, bias=EPSC[0:PN]).then_inc(sd, 1)

            def normalize_rest(k, ph):
                stats, sd, z, rs, za = s_ln[k]
                e.wait_ge(rs, 1)
                for b in range(NB):
                    for m in range(MINE, BT):
                        j = b * BT + m
                        e.activation(Zn[0:PN, j, :], XR[0:PN, j, :], ACT.Relu, bias=NBI[0:PN, j:j + 1],
                                     scale=RS[0:PN, j:j + 1]).then_inc(za, 1)
                    e.wait_ge(za, (b + 1) * (BT - MINE))
                    e.wait_ge(z, b + 1)
                    high_part(ev[ph], b)

            def layer_norm(k, ph, weight=None):
                if dve:
                    normalize(k, weight, ph)
                if act:
                    deviation(k)
                    normalize_rest(k, ph)

            def split(ph, wait_z):
                if act:
                    wait_z()
                    for b in range(NB):
                        high_part(ev[ph], b)
                if dve:
                    wait_z()
                    for b in range(NB):
                        low_part(ev[ph], b, b + 1)

            def extra_column(v):
                hi, lo = HP[0:PN, :, 0, X0], HP[0:PN, :, 1, X0]
                line(e.tensor_copy(hi, v))
                line.sync()
                line(e.tensor_tensor(TMP[0:PN], v, hi, ALU.subtract))
                line.sync()
                line(e.tensor_scalar(lo, TMP[0:PN], LOW, None, ALU.mult))
                line.sync()

            def tiles(ph, base, post, per=None):
                if per:
                    loop = line.loop(HT, 2 * per)
                    for i in loop:
                        for k in range(2):
                            post(i * 2 + k, k, base + i * 2 + k + 1)
                else:
                    with e.Fori(0, HT) as i:
                        for k in range(2):
                            post(i * 2 + k, k, base + i * 2 + k + 1)
                post(NT - 1, 0, base + NT)

            def paired(base, early, late, per_early=0, per_late=0):
                def turns(i):
                    for k in range(2):
                        j = i * 2 + k
                        early(j + 1, 1 - k, base + j + 2)
                        late(j, k, base + j + 1)

                early(0, 0, base + 1)
                if per_early or per_late:
                    for i in line.loop(HT, 2 * (per_early + per_late)):
                        turns(i)
                else:
                    with e.Fori(0, HT) as i:
                        turns(i)
                late(NT - 1, 0, base + NT)

            def aggregate(ph, base, width, turned, hp_base, stages, first_wait, q0=9, q1=14, closing=None):
                E_ = ev[ph]
                spots = {NT * q0 // 20: 0, NT * q1 // 20: 1, NT - 1: 2}
                lo0 = lo_at[0]

                def one(j, k, n, late, first=False):
                    done(E_["red"], n - 2 if not first else base)
                    for t in range(NT):
                        if first and t % BT == 0:
                            done(E_["hp"], hp_base + t // BT + 1)
                        if late is not None and t in spots:
                            stages(*late, spots[t])
                        if turned:
                            lhs = ADJ[0:PN, bass.ds(j, 1), t * PN:t * PN + P].rearrange("p o d -> p (o d)")
                        else:
                            lhs = ADJ[0:PN, t, bass.ds(j * PN, P)]
                        mm = e.matmul(AG[k][:, 0:2 * width], lhs, HP[0:PN, t, :, 0:width], start=(t == 0),
                                      stop=(t == NT - 1), skip_group_check=general)
                    if general:
                        with e.Fori(0, NT) as t:
                            m = (lo0 + base + j) * NT + t
                            e.wait_ge(s_lol, (m + 1) * 16)
                            mm = e.matmul(AG[k][:, 0:2 * width], LOT[0:PN, :],
                                          HP[0:PN, bass.ds(t, 1), :, 0:width].rearrange("p o q f -> p (o q) f"),
                                          start=False, stop=True, skip_group_check=True)
                            mm.then_inc(s_lom, 1)
                        e.wait_ge(s_lom, (lo0 + base + j + 1) * NT + 1)
                        e.sem_inc(E_["agg"], 1)
                    else:
                        mm.then_inc(E_["agg"], 1)

                first_wait()
                one(0, 0, base + 1, None, True)
                with e.Fori(0, (NT - 1) // 4) as i:
                    for k in range(4):
                        j = i * 4 + k
                        one(j + 1, (k + 1) % 2, base + j + 2, (j, k % 2, base + j + 1))
                if closing:
                    closing()
                for q in range(3):
                    stages(NT - 1, 0, base + NT, q)

            def tile_of(X, j):
                return X[0:PN, bass.ds(j, 1), :].rearrange("p o f -> p (o f)")

            def parts_sum(E_, k, n, to, width=P, scale=None, factor=1.0, plus=None):
                done(E_["agg"], n)
                step, width = width, min(width, to.shape[1])
                to = to[:, 0:width]
                hi, lo = AG[k][0:PN, 0:width], AG[k][0:PN, step:step + width]
                if scale is not None:
                    low_scale, high_scale = scale
                    line(e.tensor_scalar(to, lo, low_scale, factor / LOW, ALU.mult, ALU.mult))
                    line.sync()
                    return e.scalar_tensor_tensor(out=to, in0=hi, scalar=high_scale, in1=to, op0=ALU.mult,
                                                  op1=ALU.add)
                if plus is not None:
                    line(e.scalar_tensor_tensor(out=to, in0=lo, scalar=1 / LOW, in1=plus, op0=ALU.mult,
                                                op1=ALU.add))
                else:
                    line(e.tensor_scalar(to, lo, 1 / LOW, None, ALU.mult))
                line.sync()
                return e.tensor_tensor(to, to, hi, ALU.add)

            def di(j):
                return DI[0:PN, bass.ds(j, 1)]

            def z_of(j):
                return Zf[0:PN, bass.ds(j * P, P)]

            s0w, s1w = ST[0:PN, 0, :], ST[0:PN, 1, :]
            s0, s1 = s0w[:, 0:P], s1w[:, 0:P]

            E0 = ev["L0"]
            if dve:
                e.wait_ge(s_w, 16 * N_CONST)
                line(e.tensor_scalar(EPSL, EPS0, 1 / LOW, None, ALU.mult))
                line(e.memset(CF, 1.0))
                e.wait_ge(s_xg if general else s_x, 16)
                line(e.tensor_copy(XR[0:PN], XIN[0:PN]))
                line.sync()
                line(e.memset(HP[0:PN, :, 0, X0], 1.0))
                line(e.memset(HP[0:PN, :, 1, X0], 0.0))
                line.sync()
                e.sem_inc(s_ones, 1)
                for b in line.loop(NB, BT):
                    for m in range(BT):
                        line(stats_of(b * BT + m))
                line.sync()
            layer_norm(0, "L0")
            if dve:

                def post(j, k, n):
                    line(e.tensor_scalar(s1, z_of(j), EPSL[0:PN], None, ALU.mult))
                    line.sync()
                    done(E0["tr"], n - 1)
                    done(E0["agg"], n)
                    line(e.tensor_copy(DEG[0:PN, bass.ds(j, 1)], AG[k][0:PN, X0:X0 + 1]))
                    parts_sum(E0, k, n, s0, X0 + 1, plus=s1).then_inc(E0["red"], 1)

                def late(j, k, n):
                    done(E0["d2"], n)
                    done(E0["red"], n if isinstance(j, int) else n + 1)
                    line(e.tensor_tensor(s1, P2[0:PN, 0:P], BB[0:PN, :], ALU.add))
                    line.sync()
                    line(e.tensor_scalar(z_of(j), s1, 0.0, None, ALU.max))
                    line.sync()
                    e.tensor_reduce(MX[0:PN, bass.ds(j, 1)], z_of(j), AX.X, ALU.max, negate=True)\
                     .then_inc(E0["z"], 1)
                    line(e.tensor_tensor(tile_of(XR, j), tile_of(XR, j), z_of(j), ALU.add))
                    line.sync()
                    line(stats_of(j))
                paired(0, post, late, 3, 4)
                line.sync()
            if act:
                e.wait_ge(s_w, 16 * N_CONST)

                def post(j, k, n):
                    done(E0["tr"], n)
                    e.copy(SF[:, 0, 0:PN], TP[:, 0:PN]).then_inc(E0["cf"], 1)
                    done(E0["d1"], n)
                    done(E0["d2"], n - 1)
                    for m in range(2):
                        e.activation(SG[:, m, 0:PN], P1[:, m * P:m * P + PN], ACT.Relu, bias=B_L0[:, m:m + 1])\
                         .then_inc(E0["rg"], 1)

                def late(j, k, n):
                    done(E0["z"], n)
                    e.wait_ge(E0["ex"], n)
                    settle()
                    e.activation(SF[0:PN, 1, :], z_of(j), ACT.Exp, bias=MX[0:PN, bass.ds(j, 1)],
                                 accum_out=SE[0:PN, bass.ds(j, 1)]).then_inc(E0["ex"], 1)
                paired(0, post, late)
            if pe:
                def stages(j, k, n, q):
                    if q == 0:
                        done(E0["red"], n)
                        e.transpose(TP[:, 0:PN], s0, IDF[0:PN, 0:PN]).then_inc(E0["tr"], 1)
                    if q == 1:
                        done(E0["cf"], n)
                        for m in range(2):
                            mm = e.matmul(P1[:, m * P:m * P + PN], WB[:, m * P:(m + 1) * P], SF[:, 0, 0:PN],
                                          start=True, stop=True)
                        mm.then_inc(E0["d1"], 1)
                    if q == 2:
                        done(E0["rg"], n * 2)
                        done(E0["z"], n - 1)
                        for m in range(2):
                            mm = e.matmul(P2[0:PN, 0:P], SG[:, m, 0:PN], WB[:, (2 + m) * P:(3 + m) * P],
                                          start=(m == 0), stop=(m == 1))
                        mm.then_inc(E0["d2"], 1)

                def first():
                    e.wait_ge(s_adj, 2)
                    e.wait_ge(s_ones, 1)
                    e.wait_ge(s_w, 16 * N_CONST)
                aggregate("L0", 0, X0 + 1, False, 0, stages, first, 10, 14)
            lo_at[0] += NT

            if act:
                done(E0["z"], NT)
                e.activation(SDV[0:PN], DEG[0:PN], ACT.Sqrt).then_inc(s_soft, 1)
                e.wait_ge(E0["ex"], NT + 1)
            if dve:
                e.wait_ge(s_soft, 1)
                line(e.reciprocal(DI[0:PN], SDV[0:PN]))
                line(e.tensor_scalar(DEG[0:PN], SDV[0:PN], 1 / LOW, None, ALU.mult))
                line.sync()
                line(e.tensor_scalar(DIL[0:PN], DI[0:PN], LOW, None, ALU.mult))
                line(e.tensor_scalar(DIS[0:PN], DI[0:PN], SPREAD, None, ALU.mult))
                line.sync()
            if dve:
                e.wait_ge(E0["ex"], NT + 1)
            layer_norm(1, "L1a", DIL[0:PN])
            E1 = ev["L1a"]

            if dve:
                e.wait_ge(s_soft, 2)
                line(e.tensor_tensor(TMP[0:PN], MX[0:PN], SE[0:PN], ALU.subtract))
                line.sync()
                line(e.tensor_tensor(XR[0:PN], XR[0:PN], TMP[0:PN].rearrange("p (t o) -> p t o", o=1)
                                     .broadcast_to([PN, NT, P]), ALU.add))
                line.sync()
            if act:
                e.activation(SE[0:PN], SE[0:PN], ACT.Ln).then_inc(s_soft, 1)
            if dve:
                def post(j, k, n):
                    done(E1["tr"], n - 1)
                    parts_sum(E1, k, n, s0, P, (di(j), di(j))).then_inc(E1["red"], 1)

                def late(j, k, n):
                    done(E1["d2"], n)
                    e.tensor_scalar(z_of(j), P2[0:PN, 0:P], di(j), None, ALU.mult).then_inc(E1["z"], 1)
                paired(0, post, late, 1, 0)
            if act:
                def post(j, k, n):
                    done(E1["tr"], n)
                    e.copy(SF[:, 0, 0:PN], TP[:, 0:PN]).then_inc(E1["cf"], 1)
                    done(E1["d1"], n)
                    done(E1["d2"], n - 1)
                    e.activation(SG[:, 0, 0:PN], P1[:, 0:PN], ACT.Relu, bias=B_L1[:, :]).then_inc(E1["rg"], 1)
                tiles("L1a", 0, post)
            if pe:
                def stages(j, k, n, q):
                    if q == 0:
                        done(E1["red"], n)
                        e.transpose(TP[:, 0:PN], s0, IDF[0:PN, 0:PN]).then_inc(E1["tr"], 1)
                    if q == 1:
                        done(E1["cf"], n)
                        e.matmul(P1[:, 0:PN], WL1[:, 0], SF[:, 0, 0:PN], start=True, stop=True)\
                         .then_inc(E1["d1"], 1)
                    if q == 2:
                        done(E1["rg"], n)
                        done(E1["z"], n - 1)
                        e.matmul(P2[0:PN, 0:P], SG[:, 0, 0:PN], WL1[:, 1], start=True, stop=True)\
                         .then_inc(E1["d2"], 1)
                aggregate("L1a", 0, P, False, 0, stages, lambda: e.wait_ge(s_sc[4], 1))
            lo_at[0] += NT

            E1b = ev["L1b"]
            split("L1b", lambda: done(E1["z"], NT))
            if dve:
                def post(j, k, n):
                    parts_sum(E1b, k, n, s1, P, (di(j), di(j))).then_inc(E1b["red"], 1)
                    done(E1b["red"], n)
                    xj = tile_of(XR, j)
                    line(e.tensor_tensor(s0, s1, INV[0:PN], ALU.mult))
                    line(e.tensor_tensor(xj, xj, WL1[0:PN, 2], ALU.add))
                    line.sync()
                    line(e.tensor_tensor(xj, xj, s0, ALU.add))
                    line.sync()
                    line(stats_of(j))
                tiles("L1b", 0, post, 5)
                line.sync()
            if pe:
                aggregate("L1b", 0, P, False, 0, lambda *_: None, lambda: None)
            lo_at[0] += NT

            E2 = ev["L2"]
            layer_norm(2, "L2")
            if sp:
                done(E0["d2"], NT)
                with e.Fori(0, LAYERS) as l:
                    done(s_bn["w"], l)
                    e.dma_start(WB[:, 0:P], a["L2_gnn_W1"][bass.ds(l, 1)].rearrange("o p n -> (o p) n"))\
                     .then_inc(s_wt, 16)
                    e.dma_start(WB[:, P:2 * P], a["L2_gnn_W2"][bass.ds(l, 1)].rearrange("o p n -> (o p) n"))\
                     .then_inc(s_wt, 16)

            def bias2(q, l):
                return B_L2[:, q, bass.ds(l, 1)]

            def zc_of(j):
                return Zf[:, bass.ds(j * PN, PN)]

            def turned_block(b):
                return RB[b % 2][0:PN, 0:BT * P].rearrange("p (t f) -> p t f", f=P)

            if dve:
                absolute(e, line, SDV[:, 0:LAYERS], B_L2[:, Q_GA, :])
                absolute(e, line, RS[:, 0:LAYERS], B_L2[:, Q_BE, :])
                line.sync()
                line(e.scalar_tensor_tensor(out=SDV[:, 0:LAYERS], in0=SDV[:, 0:LAYERS], scalar=N ** 0.5,
                                            in1=RS[:, 0:LAYERS], op0=ALU.mult, op1=ALU.add))
                line.sync()
                line(e.tensor_scalar(SDV[:, 0:LAYERS], SDV[:, 0:LAYERS], 1 / TOP, 1e-30, ALU.mult, ALU.max))
                line.sync()
                line(e.reciprocal(RS[:, 0:LAYERS], SDV[:, 0:LAYERS]))
                line.sync()
                line(e.tensor_scalar(RS[:, 0:LAYERS], RS[:, 0:LAYERS], LOW, None, ALU.mult))
                line.sync()

            def layer2(l, last):
                base = l * NT
                if dve:
                    done(E2["hp"], (l + 1) * NB)
                    settle()

                    def post(j, k, n):
                        done(E2["tr"], n - 1)
                        parts_sum(E2, k, n, s0).then_inc(E2["red"], 1)

                    def late(j, k, n):
                        done(E2["d2"], n)
                        e.tensor_scalar(zc_of(j), P2[:, 0:PN], bias2(Q_B2, l), None, ALU.add)\
                         .then_inc(E2["z"], 1)
                        done(E2["z"], n)
                        line(e.bn_stats(STATS[:, 0, bass.ds(j, 1), :].rearrange("p o c -> p (o c)"), zc_of(j)))
                        line.sync()
                    paired(base, post, late, 1, 1)
                    settle()
                    line(e.bn_aggr(BNM, STATS[:, 0, :, :].rearrange("p t c -> p (t c)")))
                    line.sync()
                    e.sem_inc(s_bn["var"], 1)
                    e.wait_ge(s_bn["sd"], l + 1)
                    line(e.reciprocal(BNR, BNS))
                    line.sync()
                    line(e.tensor_tensor(BNA[:, 0:1], BNR, bias2(Q_GA, l), ALU.mult))
                    line.sync()
                    line(e.tensor_tensor(BNT, BNM[:, 0:1], BNA[:, 0:1], ALU.mult))
                    line.sync()
                    line(e.tensor_tensor(BNB[:, 0:1], bias2(Q_BE, l), BNT, ALU.subtract))
                    line.sync()
                    if not last:
                        up = RS[:, bass.ds(l, 1)]
                        line(e.tensor_tensor(BNA[:, 0:1], BNA[:, 0:1], up, ALU.mult))
                        line(e.tensor_tensor(BNB[:, 0:1], BNB[:, 0:1], up, ALU.mult))
                        line(e.tensor_copy(CF, SDV[:, bass.ds(l, 1)]))
                        line.sync()
                    e.sem_inc(s_bn["ab"], 1)
                    for b in range(NB):
                        n = (l + 1) * NB + b + 1
                        if last:
                            e.wait_ge(s_bn["tr"], n - NB)
                            xb = XR[0:PN, b * BT:(b + 1) * BT, :]
                            line(e.tensor_tensor(xb, xb, turned_block(b), ALU.add))
                            line.sync()
                            e.sem_inc(E2["hp"], 1)
                            for m in range(BT):
                                line(stats_of(b * BT + m))
                        else:
                            low_part(E2, b, n, turned_block(b))
                    if last:
                        line.sync()
                if act:
                    def post(j, k, n):
                        done(E2["tr"], n)
                        e.activation(SF[:, 0, 0:PN], TP[:, 0:PN], ACT.Copy, scale=CF).then_inc(E2["cf"], 1)
                        done(E2["d1"], n)
                        done(E2["d2"], n - 1)
                        settle()
                        e.activation(SG[:, 0, 0:PN], P1[:, 0:PN], ACT.Relu, bias=bias2(Q_B1, l))\
                         .then_inc(E2["rg"], 1)
                    tiles("L2", base, post)
                    e.wait_ge(s_bn["var"], l + 1)
                    e.activation(BNS, BNM[:, 1:2], ACT.Sqrt, bias=EPSC).then_inc(s_bn["sd"], 1)
                    e.wait_ge(s_bn["ab"], l + 1)

                    def relu(b):
                        zb = Zf[:, b * BT * PN:(b + 1) * BT * PN]
                        e.activation(zb, zb, ACT.Relu, bias=BNB[:, 0:1], scale=BNA[:, 0:1]).then_inc(s_bn["rel"], 1)

                    relu(0)
                    for b in range(NB):
                        if b + 1 < NB:
                            relu(b + 1)
                        if not last:
                            e.wait_ge(s_bn["tr"], l * NB + b + 1)
                            high_part(E2, b, turned_block(b))
                if pe:
                    def stages(j, k, n, q):
                        if q == 0:
                            done(E2["red"], n)
                            e.transpose(TP[:, 0:PN], s0, IDF[0:PN, 0:PN]).then_inc(E2["tr"], 1)
                        if q == 1:
                            done(E2["cf"], n)
                            e.matmul(P1[:, 0:PN], WB[:, 0:P], SF[:, 0, 0:PN], start=True, stop=True)\
                             .then_inc(E2["d1"], 1)
                        if q == 2:
                            done(E2["rg"], n)
                            done(E2["z"], n - 1)
                            e.matmul(P2[:, 0:PN], WB[:, P:2 * P], SG[:, 0, 0:PN], start=True, stop=True)\
                             .then_inc(E2["d2"], 1)
                    aggregate("L2", base, P, False, l * NB, stages,
                              lambda: e.wait_ge(s_wt, (l + 1) * 32))
                    e.wait_ge(E2["d2"], (l + 1) * NT + 1)
                    e.sem_inc(s_bn["w"], 1)
                    for b in range(NB):
                        e.wait_ge(s_bn["rel"], l * NB + b + 1)
                        if b >= 2:
                            done(E2["hp"], (l + 1) * NB + b - 1)
                        for m in range(BT):
                            c = (b * BT + m) * PN
                            mm = e.transpose(RB[b % 2][0:PN, m * P:(m + 1) * P], Zf[:, c:c + PN], IDF[:, :])
                        mm.then_inc(s_bn["tr"], 1)

            if dve:
                for l in line.loop(LAYERS - 1, 2 * NT + 8):
                    layer2(l, False)
            elif act or pe:
                with e.Fori(0, LAYERS - 1) as l:
                    layer2(l, False)
            layer2(LAYERS - 1, True)
            lo_at[0] += NT * LAYERS

            TB = [(q * NT // 4, (q + 1) * NT // 4) for q in range(4)]
            banks = [PS[:, q, :].bitcast(BF16) for q in range(8)]
            PB = P
            if general and pe:
                with e.Fori(0, NT * NT) as m:
                    e.wait_ge(s_lod, m * 32 + 16)
                    e.transpose(banks[0][0:PN, 0:PN], LOX[0:PN, 0:PN], IDB[0:PN, 0:PN]).then_inc(s_lox, 1)
            if general and dve:
                with e.Fori(0, NT * NT) as m:
                    e.wait_ge(s_lox, m + 1)
                    e.tensor_copy(LOT[0:PN, 0:PN], banks[0][0:PN, 0:PN]).then_inc(s_loc, 1)
            if general and pe:
                e.wait_ge(s_loc, NT * NT)
            ALONE = min(4, (NT - 1) // 2 * 2)

            def turn_row(t, k, wait):
                for q, (b0, b1) in enumerate(TB):
                    if wait == "first":
                        e.wait_ge(s_at["act"], (t - 2) * 4 + q + 1)
                    if wait == "shared":
                        if q % 2:
                            e.wait_ge(s_at["dve"], (t - 2 - ALONE) * 2 + q // 2 + 1)
                        else:
                            e.wait_ge(s_at["act"], ALONE * 4 + (t - 2 - ALONE) * 2 + q // 2 + 1)
                    for b in range(b0, b1):
                        mm = e.transpose(banks[k * 4 + q][0:PN, (b - b0) * PB:(b - b0) * PB + PN],
                                         ADJ[0:PN, bass.ds(t, 1), b * PN:(b + 1) * PN]
                                         .rearrange("p o d -> p (o d)"), IDB[0:PN, 0:PN])
                    mm.then_inc(s_at["tr"], 1)

            def copy_row(t, k, mine):
                for q in mine:
                    b0, b1 = TB[q]
                    e.wait_ge(s_at["tr"], t * 4 + q + 1)
                    to = ADJ[0:PN, bass.ds(t, 1), b0 * PN:b1 * PN].rearrange("p o (b d) -> p (o b) d", d=PN)
                    fr = banks[k * 4 + q][0:PN, 0:(b1 - b0) * PB].rearrange("p (b d) -> p b d", d=PB)[:, :, 0:PN]
                    (e.tensor_copy if dve else e.copy)(to, fr).then_inc(s_at["dve" if dve else "act"], 1)

            def rows(t0, t1, do):
                if t1 > t0:
                    with e.Fori(t0 // 2, t1 // 2) as i:
                        for k in range(2):
                            do(i * 2 + k, k)

            if pe:
                turn_row(0, 0, None)
                done(E2["hp"], (LAYERS + 1) * NB)
                turn_row(1, 1, None)
                mid = min(ALONE + 2, NT - 1)
                rows(2, mid, lambda t, k: turn_row(t, k, "first"))
                rows(mid, NT - 1, lambda t, k: turn_row(t, k, "shared"))
                turn_row(NT - 1, 0, "shared" if NT - 1 >= ALONE + 2 else "first")
            if dve:
                normalize(3, DIL[0:PN])
                rows(ALONE, NT - 1, lambda t, k: copy_row(t, k, (1, 3)))
                copy_row(NT - 1, 0, (1, 3))
                for b in range(NB):
                    low_part(ev["L3a"], b, b + 1)
            if act:
                deviation(3)
                rows(0, ALONE, lambda t, k: copy_row(t, k, range(4)))
                rows(ALONE, NT - 1, lambda t, k: copy_row(t, k, (0, 2)))
                copy_row(NT - 1, 0, (0, 2))
                normalize_rest(3, "L3a")

            VW = HPf[:, 0:9 * P]
            CB = HPf[:, 12 * P:15 * P]
            YT = [HPf[:, (15 + 3 * k) * P:(18 + 3 * k) * P].rearrange("p (q n) -> p q n", q=3) for k in range(4)]
            Q1T = [HPf[:, (27 + k) * P:(28 + k) * P] for k in range(2)]
            L2R = Zf[:, 0:9 * P].rearrange("p (j g n) -> p j g n", j=3, g=3)
            L2T = Zf[:, 9 * P:18 * P].rearrange("p (j g n) -> p j g n", j=3, g=3)
            BBR, FP, FB = Zf[:, 18 * P:21 * P], Zf[:, 21 * P:24 * P], Zf[:, 24 * P:25 * P]
            VZ, CZ = Zf[:, 0:9 * P], BBR
            VA, BR, CA = Zf[:, 9 * P:15 * P], Zf[:, 15 * P:18 * P], Zf[:, 21 * P:23 * P]

            Y = lambda q: y_d[q]
            E3, E3b = ev["L3a"], ev["L3b"]
            if sp:
                done(E2["d2"], NT * LAYERS)
                e.dma_start(WB[:, 0:3 * P].rearrange("p (q n) -> p q n", q=3),
                            a["L3_gnn_l1_w"].rearrange("q p n -> p q n")).then_inc(s_wt, 16)
                e.wait_ge(s_ln[3][0], 1)
                e.dma_start(BB[0:1, :], a["L3_gnn_l1_b"][1:2]).then_inc(s_wt, 16)

                def post(j, k, n):
                    e.wait_ge(E3["z"], n * 2 + 1)
                    e.dma_start(y_d[1][:, bass.ds(j * PN, PN)], SG[:, 0, 0:PN]).then_inc(s_y, 16)
                    e.dma_start(y_d[0][:, bass.ds(j * PN, PN)], SG[:, 1, 0:PN]).then_inc(s_y, 16)
                tiles("L3a", 0, post)
                e.wait_ge(E3["d1"], NT + 1)
                e.dma_start(BB[0:1, :], a["L3_gnn_l1_b"][2:3]).then_inc(s_wt, 16)

                done(E3b["hp"], NB)
                e.dma_start(FP.rearrange("p (j n) -> p j n", j=3),
                            a["L3_gnn_fp_w"].rearrange("(j p) n -> p j n", p=P)).then_inc(s_vw, 16)
                e.dma_start(FB, bcast(a["L3_gnn_fp_b"])).then_inc(s_vw, 16)
                for j in range(3):
                    e.dma_start(L2R[:, j], a["L3_gnn_l2_w"][j].rearrange("(g p) n -> p g n", p=P))\
                     .then_inc(s_vw, 16)

                def post(j, k, n):
                    e.wait_ge(E3b["z"], n + 1)
                    e.dma_start(y_d[2][:, bass.ds(j * PN, PN)], SG[:, 0, 0:PN]).then_inc(s_y, 16)
                tiles("L3b", 0, post)
            wt0 = 32 * LAYERS

            def mix_dve(E_, first):
                yb = 0 if first else 32 * NT

                def early(j, k, n):
                    done(E_["tr"], n - 1)
                    if first:
                        line(e.tensor_scalar(s1, z_of(j), DEG[0:PN, bass.ds(j, 1)], None, ALU.mult))
                    scales = (di(j), di(j)) if first else (di(j), DIS[0:PN, bass.ds(j, 1)])
                    line(parts_sum(E_, k, n, s0w, X0 + 1, scales, 1.0 if first else SPREAD))
                    line.sync()
                    e.sem_inc(E_["red"], 1)
                    if first:
                        line(e.tensor_scalar(z_of(j), s0, di(j), LOW / SPREAD, ALU.mult, ALU.mult))
                        line(e.tensor_scalar(TMP[0:PN, bass.ds(j, 1)], s0w[:, X0:X0 + 1], di(j), 1 / SPREAD,
                                             ALU.mult, ALU.mult))
                        line.sync()

                def late(j, k, n):
                    done(E_["d1"], n)
                    done(s_y, yb + (n - 1) * (32 if first else 16))
                    outs = ((0, P1[:, 0:PN], None, 1), (1, P1[:, P:P + PN], B_L3[:, R_B1, 0:1], 0)) if first else \
                           ((0, P1[:, 0:PN], None, 2),)
                    for r, src, bias, q in outs:
                        if bias is None:
                            line(e.tensor_copy(SG[:, r, 0:PN], src))
                        else:
                            line(e.tensor_scalar(SG[:, r, 0:PN], src, bias, None, ALU.add))
                    line.sync()
                    for r, src, bias, q in outs:
                        e.bn_stats(STATS[:, q, bass.ds(j, 1), :].rearrange("p o c -> p (o c)"), SG[:, r, 0:PN])\
                         .then_inc(E_["z"], 1)
                return early, late, 5 if first else 2, 2 if first else 1

            def mix_act(E_, first):
                def post(j, k, n):
                    done(E_["tr"], n)
                    done(E_["d1"], n - 1)
                    e.copy(SF[:, 0, 0:PN], TP[:, 0:PN]).then_inc(E_["cf"], 1)
                    if first:
                        e.copy(SF[:, 1, 0:PN], TP[:, P:P + PN]).then_inc(E_["cf"], 1)
                    e.copy(ROW[0:1, 0:PN], TP[0:1, 2 * P:2 * P + PN]).then_inc(E_["cf"], 1)
                return post

            def mix_pe(E_, first, wq):
                per = 3 if first else 2

                def stages(j, k, n, q):
                    if q == 0:
                        done(E_["red"], n)
                        e.transpose(TP[:, 0:PN], s0, IDF[0:PN, 0:PN])
                        if first:
                            e.transpose(TP[:, P:P + PN], s1, IDF[0:PN, 0:PN])
                        e.matmul(TP[0:1, 2 * P:2 * P + PN], s0w[:, X0:X0 + 1], IDF[0:PN, 0:PN], start=True, stop=True)\
                         .then_inc(E_["tr"], 1)
                    if q == 2:
                        done(E_["cf"], n * per)
                        done(E_["z"], (n - 1) * (per - 1))
                        e.matmul(P1[:, 0:PN], WB[:, wq * P:(wq + 1) * P], SF[:, 0, 0:PN], start=True, stop=False)
                        mm = e.matmul(P1[:, 0:PN], BB[0:1, :], ROW[0:1, 0:PN], start=False, stop=True)
                        if first:
                            mm = e.matmul(P1[:, P:P + PN], WB[:, 0:P], SF[:, 1, 0:PN], start=True, stop=True)
                        mm.then_inc(E_["d1"], 1)
                return stages

            if dve:
                extra_column(DI[0:PN])
                e.sem_inc(s_rt, 1)
                paired(0, *mix_dve(E3, True))
            if act:
                tiles("L3a", 0, mix_act(E3, True))
            if pe:
                def first():
                    e.wait_ge(s_at["act"], 2 * NT + 2 * ALONE)
                    e.wait_ge(s_at["dve"], 2 * (NT - ALONE))
                    e.wait_ge(s_rt, 1)
                    e.wait_ge(s_wt, wt0 + 32)
                aggregate("L3a", 0, X0 + 1, True, 0, mix_pe(E3, True, 1), first, 12, 16)
            lo_at[0] += NT
            if dve:
                done(E3["z"], 2 * NT)
            split("L3b", lambda: done(E3["z"], 2 * NT))
            if dve:
                line(e.tensor_copy(MX[0:PN], TMP[0:PN]))
                line.sync()
                extra_column(MX[0:PN])
                e.sem_inc(s_rt, 1)
                paired(0, *mix_dve(E3b, False))
            if act:
                tiles("L3b", 0, mix_act(E3b, False))
            if pe:
                def first():
                    e.wait_ge(s_rt, 2)
                    e.wait_ge(s_wt, wt0 + 48)

                def turn_weights():
                    e.wait_ge(s_vw, 80)
                    for j in range(3):
                        for g in range(3):
                            mm = e.transpose(PS[:, 4 + j, g * P:(g + 1) * P], L2R[:, j, g, :], IDF[:, :])
                        mm.then_inc(s_vt, 1)
                aggregate("L3b", 0, X0 + 1, True, 0, mix_pe(E3b, False, 2), first, 12, 16, turn_weights)
                for j in range(3):
                    e.wait_ge(s_vc, j + 1)
                    bank = (7, 4, 5)[j]
                    for g in range(3):
                        e.matmul(PS[:, bank, g * P:(g + 1) * P], L2T[:, j, g, :], FP[:, j * P:(j + 1) * P],
                                 start=True, stop=True)
                    e.matmul(PS[:, bank, 3 * P:4 * P], BBR[:, j * P:(j + 1) * P], FP[:, j * P:(j + 1) * P],
                             start=True, stop=True).then_inc(s_vm, 1)
            lo_at[0] += NT

            if act:
                for j in range(3):
                    e.wait_ge(s_vt, j + 1)
                    line(e.copy(L2T[:, j].rearrange("p g n -> p (g n)"), PS[:, 4 + j, 0:3 * P]))
                    line(e.activation(BBR[:, j * P:(j + 1) * P], IDF[:, :], ACT.Identity,
                                      bias=B_L3[:, R_B2, j:j + 1], scale=0.0))
                    line.sync()
                    e.sem_inc(s_vc, 1)
                for j in range(3):
                    e.wait_ge(s_vm, j + 1)
                    bank = (7, 4, 5)[j]
                    e.copy(VZ.rearrange("p (g j n) -> p g j n", g=3, j=3)[:, :, j, :],
                           PS[:, bank, 0:3 * P].rearrange("p (g n) -> p g n", g=3)).then_inc(s_vv, 1)
                    e.copy(CZ[:, j * P:(j + 1) * P], PS[:, bank, 3 * P:4 * P]).then_inc(s_vv, 1)
            if dve:
                for q in range(3):
                    done(E3b["z"], NT)
                    done(E3["z"], 2 * NT)
                    line(e.bn_aggr(BNM, STATS[:, q, :, :].rearrange("p t c -> p (t c)")))
                    line.sync()
                    e.sem_inc(s_bn["var"], 1)
                    e.wait_ge(s_bn["sd"], LAYERS + q + 1)
                    line(e.reciprocal(BNR, BNS))
                    line.sync()
                    line(e.tensor_tensor(BNA[:, q:q + 1], BNR, B_L3[:, R_GA, q:q + 1], ALU.mult))
                    line.sync()
                    line(e.tensor_tensor(BNT, BNM[:, 0:1], BNA[:, q:q + 1], ALU.mult))
                    line.sync()
                    line(e.tensor_tensor(BNB[:, q:q + 1], B_L3[:, R_BE, q:q + 1], BNT, ALU.subtract))
                    line.sync()
                e.sem_inc(s_bn["ab"], 1)
                absolute(e, line, BND, B_L3[:, R_GA, :])
                absolute(e, line, BND2, B_L3[:, R_BE, :])
                line.sync()
                line(e.scalar_tensor_tensor(out=BND, in0=BND, scalar=N ** 0.5, in1=BND2, op0=ALU.mult, op1=ALU.add))
                line.sync()
                e.wait_ge(s_vv, 6)
                for g in range(3):
                    line(e.tensor_copy(BR[:, g * P:(g + 1) * P], BND[:, g:g + 1].broadcast_to([P, P])))
                far = float(E + N)
                va, vz, vw, ca, cz, cb = (v.rearrange("p (g j n) -> p g j n", g=g, j=j) for v, g, j in
                                          ((VA, 3, 2), (VZ, 3, 3), (VW, 3, 3), (CA, 1, 2), (CZ, 1, 3), (CB, 1, 3)))
                absolute(e, line, va, vz[:, :, 1:3, :])
                absolute(e, line, ca, cz[:, :, 1:3, :])
                line.sync()
                line(e.tensor_scalar(va[:, :, 1, :], va[:, :, 1, :], far, None, ALU.mult))
                line.sync()
                e.sem_inc(s_sc[5], 1)
                line(e.scalar_tensor_tensor(out=CA[:, 0:P], in0=CA[:, P:2 * P], scalar=far, in1=CA[:, 0:P],
                                            op0=ALU.mult, op1=ALU.add))
                line(e.tensor_tensor(CB[:, 0:P], CZ[:, 0:P], FB, ALU.add))
                line(e.tensor_copy(vw[:, :, 0, :], vz[:, :, 0, :]))
                line.sync()
                e.wait_ge(s_sc[3], 2)
                line(e.tensor_tensor(CA[:, 0:P], CA[:, 0:P], P3[:, 0:P], ALU.add))
                line.sync()
                scale_from_bound(e, line, CA[:, 0:P], INV[:, :])
                scale = CA[:, 0:P].rearrange("p (o n) -> p o n", o=1).broadcast_to([P, 2, P])
                line(e.tensor_tensor(cb[:, 0, 1:3, :], cz[:, 0, 1:3, :], scale, ALU.mult))
                for g in range(3):
                    line(e.tensor_tensor(vw[:, g, 1:3, :], vz[:, g, 1:3, :], scale, ALU.mult))
                line.sync()
                e.sem_inc(s_sc[4], 1)
            if act:
                for q in range(3):
                    e.wait_ge(s_bn["var"], LAYERS + q + 1)
                    e.activation(BNS, BNM[:, 1:2], ACT.Sqrt, bias=EPSC).then_inc(s_bn["sd"], 1)
                e.wait_ge(s_bn["ab"], LAYERS + 1)
            if sp:
                e.wait_ge(s_y, 1 + 48 * NT)
                for j in range(4):
                    e.dma_start(YT[j][:, :, 0:PN], y_d[:, :, j * PN:(j + 1) * PN].rearrange("q p n -> p q n"))\
                     .then_inc(s_yl[j], 16)

                def store(j, k, n, more=True):
                    if more:
                        done(s_vq, n)
                        e.dma_start(YT[k][:, :, 0:PN],
                                    y_d[:, :, bass.ds((j + 4) * PN, PN)].rearrange("q p n -> p q n"))\
                         .then_inc(s_yl[k], 16)
                    e.wait_ge(s_vd, n + 2)
                    e.dma_start(q1_d[bass.ds(j, 1)].rearrange("o p f -> (o p) f"), Q1T[k % 2][0:PN])\
                     .then_inc((s_q1, s_q1b)[k % 2], 16)
                if NT > 5:
                    with e.Fori(0, (NT - 5) // 4) as i:
                        for k in range(4):
                            store(i * 4 + k, k, i * 4 + k + 1)
                for j in range(NT - 5, NT):
                    store(j, j % 4, j + 1, j + 4 < NT)

            def fours(post, per=0):
                if per:
                    for i in line.loop((NT - 1) // 4, 4 * per):
                        for k in range(4):
                            post(i * 4 + k, k, i * 4 + k + 1)
                else:
                    with e.Fori(0, (NT - 1) // 4) as i:
                        for k in range(4):
                            post(i * 4 + k, k, i * 4 + k + 1)
                post(NT - 1, 0, NT)
            if act:
                def post(j, k, n):
                    e.wait_ge(s_yl[k], (j - k) * 4 + 16)
                    for q in range(3):
                        yt = YT[k][:, q, 0:PN]
                        ins = e.activation(yt, yt, ACT.Relu, bias=BNB[:, q:q + 1], scale=BNA[:, q:q + 1])
                        ins.then_inc(s_vr, 1)
                fours(post)
            if pe:
                e.wait_ge(s_sc[5], 1)
                for g in range(3):
                    for j in range(2):
                        mm = e.matmul(P3[:, 0:P], BR[:, g * P:(g + 1) * P], VA[:, (g * 2 + j) * P:(g * 2 + j + 1) * P],
                                      start=(g + j == 0), stop=(g + j == 3))
                mm.then_inc(s_sc[3], 1)
                e.wait_ge(s_sc[4], 2)

                def post(j, k, n):
                    e.wait_ge(s_vr, n * 3 + 1)
                    e.wait_ge(s_vd, n)
                    for q in range(3):
                        mm = e.matmul((P1, P2)[k % 2][0:PN, 0:3 * P], YT[k][:, q, 0:PN], VW[:, q * 3 * P:(q + 1) * 3 * P],
                                      start=(q == 0), stop=(q == 2))
                    mm.then_inc(s_vq, 1)
                fours(post)
            if dve:
                def post(j, k, n):
                    done(s_vq, n)
                    pv = (P1, P2)[k % 2][0:PN]
                    xj = tile_of(XR, j)
                    done((s_q1, s_q1b)[k % 2], (j - k % 2) * 8)
                    line(e.tensor_tensor(xj, pv[:, 0:P], xj, ALU.add))
                    line(e.tensor_tensor(Q1T[k % 2][0:PN], pv[:, P:2 * P], CB[0:PN, P:2 * P], ALU.add))
                    line(e.tensor_tensor(s0, pv[:, 2 * P:3 * P], CB[0:PN, 2 * P:3 * P], ALU.add))
                    line.sync()
                    line(e.tensor_tensor(xj, xj, CB[0:PN, 0:P], ALU.add))
                    line(e.tensor_scalar(z_of(j), s0, di(j), LOW, ALU.mult, ALU.mult))
                    line.sync()
                    e.sem_inc(s_vd, 1)
                fours(post, 5)

            def all_stored():
                done(s_q1, 16 * (HT + 1))
                done(s_q1b, 16 * HT)

            Ec, Ed = ev["L3c"], ev["L3d"]
            split("L3c", lambda: (e.wait_ge(s_vd, NT + 2), all_stored()))
            if sp:
                all_stored()

                def post(j, k, n):
                    done(Ec["z"], n - 1)
                    e.dma_start(SG[0:PN, 0, :], q1_d[bass.ds(j, 1)].rearrange("o p f -> (o p) f"))\
                     .then_inc(s_q1l, 16)
                tiles("L3c", 0, post)

                def post(j, k, n):
                    done(Ed["z"], n)
                    e.dma_start(out[bass.ds(j * PN, PN)], s1).then_inc(s_out, 16)
                tiles("L3d", 0, post)
                e.wait_ge(s_out, 1 + 16 * NT)
            if dve:
                def post(j, k, n):
                    line(parts_sum(Ec, k, n, s1))
                    line.sync()
                    e.sem_inc(Ec["red"], 1)
                    e.wait_ge(s_q1l, n * 16 + 1)
                    line(e.scalar_tensor_tensor(out=s0, in0=s1, scalar=di(j), in1=SG[0:PN, 0, :], op0=ALU.mult,
                                                op1=ALU.add))
                    line.sync()
                    line(e.tensor_scalar(z_of(j), s0, di(j), LOW, ALU.mult, ALU.mult))
                    line.sync()
                    e.sem_inc(Ec["z"], 1)
                tiles("L3c", 0, post, 4)
            if pe:
                aggregate("L3c", 0, P, True, 0, lambda *_: None, lambda: None)
            lo_at[0] += NT
            split("L3d", lambda: done(Ec["z"], NT))
            if dve:
                def post(j, k, n):
                    line(parts_sum(Ed, k, n, s0))
                    line.sync()
                    e.sem_inc(Ed["red"], 1)
                    e.wait_ge(s_out, (n - 1) * 16 + 1)
                    line(e.scalar_tensor_tensor(out=s1, in0=s0, scalar=di(j), in1=INV[0:PN], op0=ALU.mult,
                                                op1=ALU.mult))
                    line.sync()
                    line(e.tensor_tensor(s1, s1, tile_of(XR, j), ALU.add))
                    line.sync()
                    e.sem_inc(Ed["z"], 1)
                tiles("L3d", 0, post, 4)
            if pe:
                aggregate("L3d", 0, P, True, 0, lambda *_: None, lambda: None)
            lo_at[0] += NT

        N_CONST = 14
        block = ctx.enter_context(nc.Block())

        @block.sync
        def _(e):
            program("sp", e)

        @block.gpsimd
        def _(e):
            program("pool", e)

        @block.scalar
        def _(e):
            program("act", e)

        @block.tensor
        def _(e):
            program("pe", e)

        @block.vector
        def _(e):
            program("dve", e)


INPUTS = ("x", "src", "dst", "L0_gnn_W1", "L0_gnn_b1", "L0_gnn_W2", "L0_gnn_b2", "L0_gnn_eps", "L1_gnn_W1",
          "L1_gnn_b1", "L1_gnn_W2", "L1_gnn_b2", "L2_gnn_W1", "L2_gnn_b1", "L2_gnn_W2", "L2_gnn_b2",
          "L2_gnn_gamma", "L2_gnn_beta", "L3_gnn_l1_w", "L3_gnn_l1_b", "L3_gnn_bn_gamma", "L3_gnn_bn_beta",
          "L3_gnn_l2_w", "L3_gnn_l2_b", "L3_gnn_fp_w", "L3_gnn_fp_b")


def kernel(**inputs):
    import numpy as np
    import concourse.bacc as bacc
    from concourse.bass_utils import run_bass_kernel_spmd

    nc = bacc.Bacc("TRN2", target_bir_lowering=False, num_devices=1)
    arrays, aps = {}, {}
    for name in INPUTS:
        v = np.ascontiguousarray(inputs[name])
        if name == "L0_gnn_eps":
            v = v.reshape(1)
        arrays["in_" + name] = v
        aps[name] = nc.dram_tensor("in_" + name, v.shape, mybir.dt.from_np(v.dtype), kind="ExternalInput").ap()
    out = nc.dram_tensor("out_x", arrays["in_x"].shape, F32, kind="ExternalOutput").ap()
    build(nc, aps, out)
    r = run_bass_kernel_spmd(nc, [arrays], core_ids=[0])
    return r.results[0]["out_x"]
```
